# Optimizing a Trainium2 kernel written in Bass

```python
import numpy as np
import jax
import jax.numpy as jnp

def _softmax(x, axis=-1):
    return jax.nn.softmax(x, axis=axis)

def _gelu(x):
    return jax.nn.gelu(x, approximate=True)

def _silu(x):
    return jax.nn.silu(x)

def _sigmoid(x):
    return jax.nn.sigmoid(x)

def _layernorm(x, axis=-1, eps=1e-05):
    m = jnp.mean(x, axis=axis, keepdims=True)
    v = jnp.var(x, axis=axis, keepdims=True)
    return (x - m) / jnp.sqrt(v + eps)

def _scatter_add(tgt, idx, src, axis=0):
    return tgt.at[idx].add(src)

def _segment_sum(src, seg, n):
    return jax.ops.segment_sum(src, seg, n)
kernel_name = 'mk_decoder_postln_d1_seqx_r8_ef5c97'

def setup_inputs(seed: int=0):
    np.random.seed(seed)
    _w = jnp.asarray

    def _rec_inputs():
        import jax
        import jax.numpy as jnp
        _rk = jax.random.key(seed)
        x = 7.22e-05 + 1 * jax.random.normal(jax.random.fold_in(_rk, 1), (32, 128, 128), jnp.float32)
        _lenS = 128 - jax.random.randint(jax.random.fold_in(_rk, 7), (32,), 0, max(1, 128 // 4) + 1, jnp.int32)
        _lenS2 = 77 - jax.random.randint(jax.random.fold_in(_rk, 8), (32,), 0, max(1, 77 // 4) + 1, jnp.int32)
        _ctx_1024P = jax.random.normal(jax.random.fold_in(_rk, 11), (32, 16, 128), jnp.float32)
        _ctx_1024c = jax.random.dirichlet(jax.random.fold_in(_rk, 511), 0.3 * jnp.ones((16,), jnp.float32), (32, 77))
        _ctx_1024t = jnp.einsum('bsk,bkd->bsd', _ctx_1024c, _ctx_1024P)
        _ctx_1024t = _ctx_1024t * jax.lax.rsqrt(jnp.mean(jnp.square(_ctx_1024t)) + 1e-12) * 0.953939
        ctx_1024 = -1.52775e-05 + 0.999936 * (_ctx_1024t + 0.3 * jax.random.normal(jax.random.fold_in(_rk, 611), (32, 77, 128), jnp.float32))
        return (x, ctx_1024)
    x, ctx_1024 = _rec_inputs()

    def _L0_attn_setup():
        import jax, jax.numpy as jnp
        import numpy as np
        from jax import lax
        D_MODEL = 128
        D_STATE = 128
        D_CONV = 4
        EXPAND = 2
        HEADDIM = 64
        D_INNER = EXPAND * D_MODEL
        NHEADS = D_INNER // HEADDIM
        CONV_DIM = D_INNER + 2 * D_STATE
        D_IN_PROJ = 2 * D_INNER + 2 * D_STATE + NHEADS
        EPS = 1e-05

        def _ssm_forward(x, in_proj_w, conv_w, conv_b, norm_w, out_proj_w, dt_bias, A_log, D_param):
            B, L, _ = x.shape
            zxbcdt = jnp.einsum('bld,ed->ble', x, in_proj_w)
            z = zxbcdt[..., :D_INNER]
            xBC = zxbcdt[..., D_INNER:D_INNER + CONV_DIM]
            dt = zxbcdt[..., D_INNER + CONV_DIM:]
            xBC_c = lax.conv_general_dilated(xBC.transpose(0, 2, 1), conv_w, window_strides=(1,), padding=[(D_CONV - 1, 0)], feature_group_count=CONV_DIM, dimension_numbers=('NCH', 'OIH', 'NCH'))
            xBC = jax.nn.silu((xBC_c + conv_b[None, :, None]).transpose(0, 2, 1))
            x_part = xBC[..., :D_INNER]
            B_part = xBC[..., D_INNER:D_INNER + D_STATE]
            C_part = xBC[..., D_INNER + D_STATE:]
            x_heads = x_part.reshape(B, L, NHEADS, HEADDIM)
            dt = jax.nn.softplus(dt + dt_bias)
            A = -jnp.exp(A_log)

            def step(state, inp):
                x_t, B_t, C_t, dt_t = inp
                decay = jnp.exp(A[None, :] * dt_t)
                state = state * decay[:, :, None, None] + (x_t * dt_t[:, :, None])[..., None] * B_t[:, None, None, :]
                y_t = jnp.einsum('bhpn,bn->bhp', state, C_t)
                return (state, y_t)
            state0 = jnp.zeros((B, NHEADS, HEADDIM, D_STATE), dtype=x.dtype)
            inputs = (jnp.moveaxis(x_heads, 1, 0), jnp.moveaxis(B_part, 1, 0), jnp.moveaxis(C_part, 1, 0), jnp.moveaxis(dt, 1, 0))
            _, y_seq = lax.scan(step, state0, inputs)
            y = jnp.moveaxis(y_seq, 0, 1).reshape(B, L, D_INNER)
            D_full = jnp.repeat(D_param, HEADDIM)
            y = y + x_part * D_full
            y = y * jax.nn.silu(z)
            y = y * jax.lax.rsqrt(jnp.mean(y * y, axis=-1, keepdims=True) + EPS) * norm_w
            return jnp.einsum('ble,de->bld', y, out_proj_w)
        key = jax.random.key(seed)
        ks = jax.random.split(key, 8)
        B, L = (2, 256)
        x = jax.random.normal(ks[0], (B, L, D_MODEL), dtype=jnp.float32)
        in_proj_w = jax.random.normal(ks[1], (D_IN_PROJ, D_MODEL), dtype=jnp.float32) * 0.02
        conv_w = jax.random.normal(ks[2], (CONV_DIM, 1, D_CONV), dtype=jnp.float32) * 0.2
        conv_b = jax.random.normal(ks[3], (CONV_DIM,), dtype=jnp.float32) * 0.02
        norm_w = jnp.ones((D_INNER,), dtype=jnp.float32)
        out_proj_w = jax.random.normal(ks[4], (D_MODEL, D_INNER), dtype=jnp.float32) * 0.02
        dt_bias = jax.random.normal(ks[5], (NHEADS,), dtype=jnp.float32) * 0.1
        A_log = jax.random.normal(ks[6], (NHEADS,), dtype=jnp.float32) * 0.1
        D_param = jnp.ones((NHEADS,), dtype=jnp.float32)
        return {'x': x, 'in_proj_w': in_proj_w, 'conv_w': conv_w, 'conv_b': conv_b, 'norm_w': norm_w, 'out_proj_w': out_proj_w, 'dt_bias': dt_bias, 'A_log': A_log, 'D_param': D_param}
    _L0_attn_all = _L0_attn_setup()
    _L0_attn_in = {k: v for k, v in _L0_attn_all.items() if k in ('in_proj_w', 'conv_w', 'conv_b', 'norm_w', 'out_proj_w', 'dt_bias', 'A_log', 'D_param')}
    del _L0_attn_all

    def _L0_xattn_setup():
        import jax, jax.numpy as jnp
        import numpy as np
        HIDDEN = 128
        key = jax.random.key(seed)
        ks = jax.random.split(key, 8)
        s = 1.0 / np.sqrt(HIDDEN)
        return {'query': jax.random.normal(ks[0], (8, 128, HIDDEN), dtype=jnp.float32), 'ref': jax.random.normal(ks[1], (8, 512, HIDDEN), dtype=jnp.float32), 'Wq': jax.random.normal(ks[2], (HIDDEN, HIDDEN), dtype=jnp.float32) * s, 'bq': jax.random.normal(ks[3], (HIDDEN,), dtype=jnp.float32) * s, 'Wk': jax.random.normal(ks[4], (HIDDEN, HIDDEN), dtype=jnp.float32) * s, 'bk': jax.random.normal(ks[5], (HIDDEN,), dtype=jnp.float32) * s, 'Wv': jax.random.normal(ks[6], (HIDDEN, HIDDEN), dtype=jnp.float32) * s, 'bv': jax.random.normal(ks[7], (HIDDEN,), dtype=jnp.float32) * s}
    _L0_xattn_all = _L0_xattn_setup()
    _L0_xattn_in = {k: v for k, v in _L0_xattn_all.items() if k in ('Wq', 'bq', 'Wk', 'bk', 'Wv', 'bv')}
    del _L0_xattn_all

    def _L0_ffn_setup():
        import jax, jax.numpy as jnp
        import numpy as np
        B, L, D = (4, 64, 128)
        E, TOP_K = (16, 4)
        F = 4 * D
        key = jax.random.key(seed)
        ks = jax.random.split(key, 6)
        scale = 0.02
        return {'x': jax.random.normal(ks[0], (B, L, D), jnp.float32), 'keys': jax.random.normal(ks[1], (E, D), jnp.float32), 'w1': jax.random.normal(ks[2], (E, F, D), jnp.float32) * scale, 'b1': jnp.zeros((E, F), jnp.float32), 'w2': jax.random.normal(ks[3], (E, D, F), jnp.float32) * scale, 'b2': jnp.zeros((E, D), jnp.float32), 'rw': jax.random.normal(ks[4], (E, D), jnp.float32) * scale, 'rb': jnp.zeros((E,), jnp.float32)}
    _L0_ffn_all = _L0_ffn_setup()
    _L0_ffn_in = {k: v for k, v in _L0_ffn_all.items() if k in ('keys', 'w1', 'b1', 'w2', 'b2', 'rw', 'rb')}
    del _L0_ffn_all
    return {'x': x, 'ctx_1024': ctx_1024, 'L0_attn_in_proj_w': _L0_attn_in['in_proj_w'], 'L0_attn_conv_w': _L0_attn_in['conv_w'], 'L0_attn_conv_b': _L0_attn_in['conv_b'], 'L0_attn_norm_w': _L0_attn_in['norm_w'], 'L0_attn_out_proj_w': _L0_attn_in['out_proj_w'], 'L0_attn_dt_bias': _L0_attn_in['dt_bias'], 'L0_attn_A_log': _L0_attn_in['A_log'], 'L0_attn_D_param': _L0_attn_in['D_param'], 'L0_xattn_Wq': _L0_xattn_in['Wq'], 'L0_xattn_bq': _L0_xattn_in['bq'], 'L0_xattn_Wk': _L0_xattn_in['Wk'], 'L0_xattn_bk': _L0_xattn_in['bk'], 'L0_xattn_Wv': _L0_xattn_in['Wv'], 'L0_xattn_bv': _L0_xattn_in['bv'], 'L0_ffn_keys': _L0_ffn_in['keys'], 'L0_ffn_w1': _L0_ffn_in['w1'], 'L0_ffn_b1': _L0_ffn_in['b1'], 'L0_ffn_w2': _L0_ffn_in['w2'], 'L0_ffn_b2': _L0_ffn_in['b2'], 'L0_ffn_rw': _L0_ffn_in['rw'], 'L0_ffn_rb': _L0_ffn_in['rb']}

def reference(x, ctx_1024, L0_attn_in_proj_w, L0_attn_conv_w, L0_attn_conv_b, L0_attn_norm_w, L0_attn_out_proj_w, L0_attn_dt_bias, L0_attn_A_log, L0_attn_D_param, L0_xattn_Wq, L0_xattn_bq, L0_xattn_Wk, L0_xattn_bk, L0_xattn_Wv, L0_xattn_bv, L0_ffn_keys, L0_ffn_w1, L0_ffn_b1, L0_ffn_w2, L0_ffn_b2, L0_ffn_rw, L0_ffn_rb):
    import jax
    import jax.numpy as jnp

    def _L0_attn_ref(x, in_proj_w, conv_w, conv_b, norm_w, out_proj_w, dt_bias, A_log, D_param):
        import jax, jax.numpy as jnp
        import numpy as np
        from jax import lax
        D_MODEL = 128
        D_STATE = 128
        D_CONV = 4
        EXPAND = 2
        HEADDIM = 64
        D_INNER = EXPAND * D_MODEL
        NHEADS = D_INNER // HEADDIM
        CONV_DIM = D_INNER + 2 * D_STATE
        D_IN_PROJ = 2 * D_INNER + 2 * D_STATE + NHEADS
        EPS = 1e-05

        def _ssm_forward(x, in_proj_w, conv_w, conv_b, norm_w, out_proj_w, dt_bias, A_log, D_param):
            B, L, _ = x.shape
            zxbcdt = jnp.einsum('bld,ed->ble', x, in_proj_w)
            z = zxbcdt[..., :D_INNER]
            xBC = zxbcdt[..., D_INNER:D_INNER + CONV_DIM]
            dt = zxbcdt[..., D_INNER + CONV_DIM:]
            xBC_c = lax.conv_general_dilated(xBC.transpose(0, 2, 1), conv_w, window_strides=(1,), padding=[(D_CONV - 1, 0)], feature_group_count=CONV_DIM, dimension_numbers=('NCH', 'OIH', 'NCH'))
            xBC = jax.nn.silu((xBC_c + conv_b[None, :, None]).transpose(0, 2, 1))
            x_part = xBC[..., :D_INNER]
            B_part = xBC[..., D_INNER:D_INNER + D_STATE]
            C_part = xBC[..., D_INNER + D_STATE:]
            x_heads = x_part.reshape(B, L, NHEADS, HEADDIM)
            dt = jax.nn.softplus(dt + dt_bias)
            A = -jnp.exp(A_log)

            def step(state, inp):
                x_t, B_t, C_t, dt_t = inp
                decay = jnp.exp(A[None, :] * dt_t)
                state = state * decay[:, :, None, None] + (x_t * dt_t[:, :, None])[..., None] * B_t[:, None, None, :]
                y_t = jnp.einsum('bhpn,bn->bhp', state, C_t)
                return (state, y_t)
            state0 = jnp.zeros((B, NHEADS, HEADDIM, D_STATE), dtype=x.dtype)
            inputs = (jnp.moveaxis(x_heads, 1, 0), jnp.moveaxis(B_part, 1, 0), jnp.moveaxis(C_part, 1, 0), jnp.moveaxis(dt, 1, 0))
            _, y_seq = lax.scan(step, state0, inputs)
            y = jnp.moveaxis(y_seq, 0, 1).reshape(B, L, D_INNER)
            D_full = jnp.repeat(D_param, HEADDIM)
            y = y + x_part * D_full
            y = y * jax.nn.silu(z)
            y = y * jax.lax.rsqrt(jnp.mean(y * y, axis=-1, keepdims=True) + EPS) * norm_w
            return jnp.einsum('ble,de->bld', y, out_proj_w)
        return _ssm_forward(x, in_proj_w, conv_w, conv_b, norm_w, out_proj_w, dt_bias, A_log, D_param)

    def _L0_xattn_ref(query, ref, Wq, bq, Wk, bk, Wv, bv):
        import jax, jax.numpy as jnp
        import numpy as np
        HIDDEN = 128
        norm_fact = 1.0 / np.sqrt(HIDDEN).astype(np.float32)
        Q = query @ Wq + bq
        K = ref @ Wk + bk
        V = ref @ Wv + bv
        scores = jnp.einsum('bqh,bkh->bqk', Q, K)
        attn = jax.nn.softmax(scores, axis=-1) * norm_fact
        return jnp.einsum('bqk,bkh->bqh', attn, V)

    def _L0_ffn_ref(x, keys, w1, b1, w2, b2, rw, rb):
        import jax, jax.numpy as jnp
        import numpy as np
        B, L, D = (4, 64, 128)
        E, TOP_K = (16, 4)
        F = 4 * D
        diff = x[:, :, None, :] - keys
        dist2 = jnp.sum(diff * diff, axis=-1)
        logits = -dist2 + jnp.einsum('bld,ed->ble', x, rw) + rb
        topv, topi = jax.lax.top_k(logits, TOP_K)
        w = jax.nn.softmax(topv, axis=-1)
        hidden = jax.nn.gelu(jnp.einsum('bld,efd->blef', x, w1) + b1, approximate=False)
        exp_out = jnp.einsum('blef,edf->bled', hidden, w2) + b2
        sel = jnp.take_along_axis(exp_out, topi[..., None], axis=2)
        fused = jnp.sum(w[..., None] * sel, axis=2)
        return fused
    x = _layernorm(x + _L0_attn_ref(x, L0_attn_in_proj_w, L0_attn_conv_w, L0_attn_conv_b, L0_attn_norm_w, L0_attn_out_proj_w, L0_attn_dt_bias, L0_attn_A_log, L0_attn_D_param), axis=-1)
    x = _layernorm(x + _L0_xattn_ref(x, ctx_1024, L0_xattn_Wq, L0_xattn_bq, L0_xattn_Wk, L0_xattn_bk, L0_xattn_Wv, L0_xattn_bv), axis=-1)
    x = _layernorm(x + _L0_ffn_ref(x, L0_ffn_keys, L0_ffn_w1, L0_ffn_b1, L0_ffn_w2, L0_ffn_b2, L0_ffn_rw, L0_ffn_rb), axis=-1)
    return x

_drawn_inputs = setup_inputs


def setup_inputs(seed=0):
    import zlib

    import numpy as np

    out = dict(_drawn_inputs(seed))
    spreads = {'L0_attn_norm_w': (1.0, 0.2),
     'L0_attn_D_param': (1.0, 0.6),
     'L0_ffn_b1': (0.0, 0.336),
     'L0_ffn_b2': (0.0, 0.1),
     'L0_ffn_rb': (0.0, 2.0)}
    factors = {'L0_attn_dt_bias': 64.0,
     'L0_attn_A_log': 64.0,
     'L0_xattn_bq': 2.903,
     'L0_xattn_bk': 64.0,
     'L0_xattn_bv': 6.724,
     'L0_ffn_rw': 8.0}
    for name, (base, spread) in spreads.items():
        noise = np.random.default_rng([zlib.crc32(name.encode()), seed]).standard_normal(out[name].shape)
        drawn = base * np.exp(spread * noise) if base else spread * noise
        out[name] = jnp.asarray(drawn.astype(out[name].dtype))
    for name, factor in factors.items():
        out[name] = (out[name] * factor).astype(out[name].dtype)
    return out
```

```python
from contextlib import ExitStack

import numpy as np

import concourse.bass as bass
from concourse import mybir

F32 = mybir.dt.float32
F32R = mybir.dt.float32r
F16 = mybir.dt.float16
BF16 = mybir.dt.bfloat16
I32 = mybir.dt.int32
U32 = mybir.dt.uint32
ALU = mybir.AluOpType
ACT = mybir.ActivationFunctionType
AX_X = mybir.AxisListType.X

P = 128
SEQS, L, D = 32, 128, 128
TOKENS = SEQS * L
LC = 77
HEADS, HD = 4, 64
INNER = HEADS * HD
CONV = INNER + 2 * P
TAPS = 4
E, TOPK, FF = 16, 4, 512
NF = FF // P
EPS = 1e-5
GT = 4
GROUPS = SEQS // GT
GTOK = GT * L
PADT = 132
OFF = TAPS - 1
STEP = 256
HALVES = STEP // P
STEPS = -(-(TOPK * TOKENS + E * (STEP - 1)) // STEP)
STEPS += STEPS % 2
REGION = TOKENS + STEP
ROW_W = 130
W_COL, DST_COL = 128, 129
W_SCALE = 64.0
SKIP_DST = 1 << 20
NORM_FACT = float(1.0 / np.sqrt(np.float32(D)))
N_CONST = 21
N_WEIGHTS = 21
N_SCALED = 9
N_PLAN = 16


def decoder_layer(nc, x, xT, ctxT, in_wT, conv_w, conv_b, norm_w, out_wT, dt_bias, a_log, d_param,
                  wq, bq, wk, bk, wv, bv, keysT, w1T, b1T, w2T, b2, rwT, rb, out):
    with ExitStack() as ctx:
        def sb(name, shape, dt=F32):
            return ctx.enter_context(nc.sbuf_tensor(name, shape, dt))

        def bank(name):
            return ctx.enter_context(nc.psum_tensor(name, [P, 512], F32))

        sems = {}

        def sem(name):
            if name not in sems:
                sems[name] = ctx.enter_context(nc.semaphore(name))
            return sems[name]

        def wait(eng, name, count):
            if not (isinstance(count, int) and count <= 0):
                eng.wait_ge(sem(name), count)

        def wait_load(eng, name, g, p):
            if p is None:
                wait(eng, name, 16 * g + 16)
            else:
                wait(eng, name, 8 * (g - p) + 16)

        rows_dram = nc.dram_tensor("rows_dram", [E * REGION + STEP, ROW_W], F32).ap()
        parts_dram = nc.dram_tensor("parts_dram", [TOPK * TOKENS, D], F32).ap()
        x2_dram = nc.dram_tensor("x2_dram", [SEQS, L, D], F32).ap()

        ident = sb("ident", [P, P])
        ident16 = sb("ident16", [P, P], F16)
        causal = sb("causal", [P, P])
        after = sb("after", [P, P], F32R)
        before16 = sb("before16", [P, P], BF16)
        ones16 = sb("ones16", [P, P], BF16)
        ones = sb("ones", [P, P])
        unscale16 = sb("unscale16", [2, P], F16)
        iota_e = sb("iota_e", [P, E])
        region_of = sb("region_of", [P, E])
        dst_of = [sb(f"dst_of{n}", [P, GT * TOPK]) for n in range(2)]
        multiples = sb("multiples", [1, E])
        step_no = sb("step_no", [1, STEPS])
        upto = sb("upto", [1, E, E])
        minus_half = sb("minus_half", [P, GT])
        eps4 = sb("eps4", [P, GT])
        pad_rows = sb("pad_rows", [P, HALVES, ROW_W])

        conv_hi = sb("conv_hi", [P, TAPS, CONV], F32R)
        conv_lo = sb("conv_lo", [P, TAPS, CONV], F32R)
        z_hi = sb("z_hi", [P, INNER], F32R)
        z_lo = sb("z_lo", [P, INNER], F32R)
        convb = sb("convb", [P, 4])
        convb_half = sb("convb_half", [P, 4])
        out_wn = sb("out_wn", [P, 2, D])
        normw = sb("normw", [P, 2])
        dcol = sb("dcol", [P, 2])
        d_diag = sb("d_diag", [P, 2, P])
        dtb = sb("dtb", [P, HEADS])
        alog = sb("alog", [P, HEADS])
        a_exp = sb("a_exp", [P, HEADS])
        wq_s = sb("wq_s", [P, D])
        wk_s = sb("wk_s", [P, D])
        wv_n = sb("wv_n", [P, D])
        bq_s = sb("bq_s", [P, 1])
        bk_s = sb("bk_s", [P, 1])
        bv_n = sb("bv_n", [P, D])
        keys_s = sb("keys_s", [P, E])
        rw_s = sb("rw_s", [P, E])
        rb_s = sb("rb_s", [P, E])
        keys_sq = sb("keys_sq", [P, E])
        route_w = sb("route_w", [P, E])
        route_b = sb("route_b", [P, E])
        w1_hi = sb("w1_hi", [P, E, NF, P], F16)
        w1_lo = sb("w1_lo", [P, E, NF, P], F16)
        w2_s = sb("w2_s", [P, E, NF, D])
        b1_s = sb("b1_s", [P, E, NF])
        b2_16 = sb("b2_16", [2, E, D], F16)

        ARENA = 11430
        arena = sb("arena", [P, ARENA])
        used = {"at": 0}

        def take(*shape):
            n = int(np.prod(shape))
            v = arena[:, used["at"]:used["at"] + n]
            used["at"] += n
            assert used["at"] <= ARENA, used["at"]
            if len(shape) == 2:
                v = v.rearrange("p (a b) -> p a b", b=shape[1])
            if len(shape) == 3:
                v = v.rearrange("p (a b c) -> p a b c", b=shape[1], c=shape[2])
            return v

        in_w = take(CONV + INNER + HEADS)
        conv_wb = take(TAPS, CONV)
        conv_f = take(TAPS, CONV)
        z_half = take(INNER)
        xT_all = take(SEQS, L)
        dtw = take(8, SEQS * HEADS)
        after_f = take(P)
        before_f = take(P)
        out_w = take(2, D)
        wv_s = take(D)
        bv_s = take(D)
        b2_lo = xT_all[0:1, E:E + E // 2, :].rearrange("p e d -> p (e d)").bitcast(F16)
        b2_stage = xT_all[0:1, 0:E, :].rearrange("p e d -> p (e d)")
        used["at"] = 0
        x_tok = [take(GT, D) for _ in range(2)]
        ctx_s = [take(GT, LC + 1) for _ in range(2)]
        th = [take(GTOK) for _ in range(2)]
        xbc = take(4, GTOK)
        z_gate = take(GT, INNER)
        xdt = take(GT, INNER)
        cb_masked = take(GT, L)
        decay = [take(HEADS, L) for _ in range(2)]
        gatedT = take(GT, 2, P)
        res1 = take(GT, D)
        x1 = [take(GT, D) for _ in range(2)]
        junk = take(INNER)
        kT_s = take(GT, LC)
        used["at"] = 0
        xg = [take(HALVES, ROW_W) for _ in range(4)]
        xgT = [take(STEP).bitcast(F16).rearrange("p (a b) -> p a b", a=2) for _ in range(2)]
        hid = [take(NF, STEP) for _ in range(2)]
        y_s = [take(HALVES, D) for _ in range(2)]
        over = take(E, E)[0:1, :, :]
        done = take(STEPS, E)[0:1, :, :]
        used["at"] = 0
        x2_back = [take(GT, D) for _ in range(2)]
        parts = [take(TOPK, GT * D) for _ in range(2)]
        total = [take(GT, D) for _ in range(2)]
        y_out = [take(GT, D) for _ in range(2)]

        dta = sb("dta", [P, 3, SEQS * HEADS])
        dta_g = [sb(f"dta_g{p}", [P, 3, GT * HEADS]) for p in range(2)]
        xT_g = [sb(f"xT_g{p}", [P, GT, L]) for p in range(2)]
        x_hi = [sb(f"x_hi{p}", [P, GT, PADT], F32R) for p in range(2)]
        x_lo = [sb(f"x_lo{p}", [P, GT, PADT], F32R) for p in range(2)]
        adt_hi = sb("adt_hi", [P, 2 * HEADS, L], F32R)
        adt_lo = sb("adt_lo", [P, 2 * HEADS, L], F32R)
        x1T_s = sb("x1T_s", [P, GTOK])
        qT_s = sb("qT_s", [P, GTOK])
        v_s = sb("v_s", [P, GT, D])
        prob = sb("prob", [P, GT, LC])
        probT = sb("probT", [P, GT, L])
        res2 = sb("res2", [P, GT, D])
        x2 = [sb(f"x2_{p}", [P, GT, D]) for p in range(2)]
        x2T_s = sb("x2T_s", [P, GTOK])
        rows = [sb(f"rows{p}", [P, GT, TOPK, ROW_W]) for p in range(2)]
        w1_stage = [sb(f"w1_stage{p}", [P, FF]) for p in range(2)]

        ss = sb("ss", [P, GT])
        stats = [sb(f"stats{n}", [P, GT, 6]) for n in range(3)]
        mv = [sb(f"mv{n}", [P, GT, 2]) for n in range(3)]
        var_e = [sb(f"var_e{n}", [P, GT]) for n in range(3)]
        rstd = [sb(f"rstd{n}", [P, GT]) for n in range(3)]
        neg_max = sb("neg_max", [P, GT])
        prob_sum = sb("prob_sum", [P, GT])
        prob_rsum = sb("prob_rsum", [P, GT])
        logit = sb("logit", [P, GT, E])
        top8 = sb("top8", [P, GT, 8])
        idx8 = sb("idx8", [P, GT, 8], U32)
        idx_f = sb("idx_f", [P, GT, TOPK])
        d4 = sb("d4", [P, GT, TOPK])
        e4 = sb("e4", [P, GT, TOPK])
        s4 = sb("s4", [P, GT])
        r4 = sb("r4", [P, GT])
        onehot = sb("onehot", [P, GT * TOPK, E])
        picked = sb("picked", [P, GT, E], BF16)
        group_n = sb("group_n", [P, E])
        carry16 = [sb(f"carry16_{n}", [P, E], BF16) for n in range(2)]
        slot = sb("slot", [P, GT, E])
        pos_f = sb("pos_f", [P, GT * TOPK])
        pos = [sb(f"pos{p}", [P, GT * TOPK], U32) for p in range(2)]

        cnt = sb("cnt", [1, E])
        n_steps = sb("n_steps", [1, E])
        last_step = sb("last_step", [1, E])
        step_ef = sb("step_ef", [1, STEPS])
        steps_before = sb("steps_before", [1, STEPS])
        row_f = sb("row_f", [1, STEPS])
        step_row = sb("step_row", [1, STEPS], I32)
        step_e = sb("step_e", [1, STEPS], I32)
        pad_f = sb("pad_f", [1, E])
        pad_at = sb("pad_at", [1, E], I32)

        banks = [bank(f"bank{n}") for n in range(8)]
        turn_ps = [banks[p][:, 0:STEP].bitcast(F16).rearrange("p (a b) -> p a b", a=2) for p in range(2)]
        front, segs, mids = banks[0:2], banks[2:4], banks[4:6]
        late = banks[6:8]

        block = ctx.enter_context(nc.Block())

        SCHEDULE = (("Aa", 0), ("Ca", 2), ("Ba", 1), ("Cb", 2), ("Ab", 0), ("Bb", 1), ("Ac", 0))

        def group_loop(eng, parts_of, schedule=SCHEDULE):
            def iteration(g, p):
                for part, lag in schedule:
                    if part not in parts_of or isinstance(g, int) and not 0 <= g - lag < GROUPS:
                        continue
                    parts_of[part](g - lag, (p - lag) % 2)

            for g in range(4):
                iteration(g, g % 2)
            with eng.Fori(2, GROUPS // 2) as i:
                iteration(2 * i, 0)
                iteration(2 * i + 1, 1)
            for g in range(GROUPS, GROUPS + 2):
                iteration(g, g % 2)

        @block.sync
        def _(sp):
            for q in range(4):
                n = SEQS // 4
                sp.dma_start(xT_all[:, n * q:n * q + n, :],
                             xT[:, n * L * q:n * L * (q + 1)].rearrange("d (s l) -> d s l", l=L)
                             ).then_inc(sem("xT_loaded"), 16)

            def load_x(g, p):
                wait(sp, "x_lo", g - 1)
                sp.dma_start(xT_g[p][:, :, :], xT3[:, bass.ds(GT * g, GT), :]).then_inc(sem(f"xT_loaded{p}"), 16)
                wait(sp, "res1", GT * (g - 1))
                sp.dma_start(x_tok[p], x[bass.ds(GT * g, GT), :, :].rearrange("s l d -> l s d")
                             ).then_inc(sem(f"x_loaded{p}"), 16)

            def load_ctx(g, p):
                wait(sp, "v_proj", g - 1)
                wait(sp, "k_proj", g - 1)
                sp.dma_start(ctx_s[p][:, :, 0:LC],
                             ctxT[:, bass.ds(GT * g, GT), :]).then_inc(sem(f"ctx_loaded{p}"), 16)

            def load_w1(c, p):
                for n in range(2):
                    wait(sp, "w1_low", 2 * c + n - 1)
                    sp.dma_start(w1_stage[n][:, :], w1T[:, bass.ds(2 * c + n, 1), :].rearrange("d e f -> d (e f)")
                                 ).then_inc(sem(f"w1_loaded{n}"), 16)

            sp.wait_ge(sem("dt_proj"), 1)
            sp.dma_start(b2_stage, b2).then_inc(sem("b2_loaded"), 16)
            xT3 = xT.rearrange("d (s l) -> d s l", l=L)
            sp.wait_ge(sem("conv_low"), 1)
            sp.wait_ge(sem("z_low"), 1)
            sp.wait_ge(sem("dt_split"), 3)
            sp.wait_ge(sem("b2_low"), 1)
            sp.dma_start(b2_16[1:2, :, :].rearrange("p e d -> p (e d)"), b2_lo).then_inc(sem("b2_split"), 16)
            sp.wait_ge(sem("b2_split"), 16)
            sp.wait_ge(sem("masks"), 2)
            sp.wait_ge(sem("scaled"), N_SCALED)
            group_loop(sp, {"Aa": load_x, "Ba": load_w1, "Ab": load_ctx})

            sp.wait_ge(sem("constants"), N_CONST)
            sp.dma_start(rows_dram[E * REGION:E * REGION + STEP, :].rearrange("(i p) w -> p i w", p=P),
                         pad_rows[:, :, :]).then_inc(sem("padded"), 16)
            sp.wait_ge(sem("plan"), N_PLAN)
            for p in range(2):
                sp.wait_ge(sem(f"rows_sent{p}"), 16 * GT * TOPK * GROUPS // 2)
            with sp.Fori(0, E) as e:
                at = sp.value_load(pad_at[0:1, bass.ds(e, 1)], min_val=0, max_val=E * REGION - STEP)
                sp.dma_start(rows_dram[bass.ds(at, STEP), :].rearrange("(i p) w -> p i w", p=P),
                             pad_rows[:, :, :]).then_inc(sem("padded"), 16)
            sp.wait_ge(sem("padded"), 16 * (E + 1))

            def load_rows(j, b):
                at = sp.value_load(step_row[0:1, bass.ds(j, 1)], min_val=0, max_val=E * REGION)
                sp.dma_start(xg[b], rows_dram[bass.ds(at, STEP), :].rearrange("(i p) w -> p i w", p=P)
                             ).then_inc(sem(f"xg_loaded{b}"), 16)

            for b in range(4):
                load_rows(b, b)
            with sp.Fori(1, STEPS // 4) as i:
                for b in range(4):
                    sp.wait_ge(sem(f"parts_sent{b}"), 32 * i)
                    load_rows(4 * i + b, b)

            for b in range(4):
                sp.wait_ge(sem(f"parts_sent{b}"), 32 * (STEPS // 4))
            for p in range(2):
                sp.wait_ge(sem(f"x2_stored{p}"), 16 * (GROUPS // 2))
            parts_v = parts_dram.rearrange("(k n p) d -> p k n d", k=TOPK, p=P)

            def load_parts(i):
                for p in range(2):
                    wait(sp, f"normed{p}", i)
                    sp.dma_start(x2_back[p], x2_dram[bass.ds(GT * (2 * i + p), GT), :, :].rearrange("s l d -> l s d")
                                 ).then_inc(sem(f"parts_loaded{p}"), 16)
                    for k in range(TOPK):
                        sp.dma_start(parts[p][:, k, :].rearrange("p (t d) -> p t d", d=D),
                                     parts_v[:, k, bass.ds(GT * (2 * i + p), GT), :]
                                     ).then_inc(sem(f"parts_loaded{p}"), 16)

            load_parts(0)
            with sp.Fori(1, GROUPS // 2) as i:
                load_parts(i)
            for p in range(2):
                sp.wait_ge(sem(f"stored{p}"), 16 * (GROUPS // 2))

        @block.gpsimd
        def _(pool):
            pool.memset(ident[:, :], 0.0).then_inc(sem("const0"), 1)
            pool.memset(ident16[:, :], 0.0).then_inc(sem("const0"), 1)
            pool.memset(ones[:, :], 1.0).then_inc(sem("const0"), 1)
            pool.memset(pad_rows[:, :, :], 0.0).then_inc(sem("const0"), 1)
            pool.memset(upto[:, :, :], 1.0).then_inc(sem("const0"), 1)
            c = sem("constants")
            pool.memset(ones16[:, :], 1.0).then_inc(c, 1)
            pool.memset(unscale16[:, :], 1.0 / W_SCALE).then_inc(c, 1)
            pool.memset(minus_half[:, :], -0.5).then_inc(c, 1)
            pool.memset(eps4[:, :], EPS).then_inc(c, 1)
            pool.memset(carry16[1][:, :], 0.0).then_inc(c, 1)
            for p in range(2):
                pool.memset(x_hi[p][:, :, :].bitcast(F32), 0.0).then_inc(c, 1)
                pool.memset(x_lo[p][:, :, :].bitcast(F32), 0.0).then_inc(c, 1)
            pool.iota(iota_e[:, :], [[1, E]], base=0, channel_multiplier=0,
                      allow_small_or_imprecise_dtypes=True).then_inc(c, 1)
            pool.iota(region_of[:, :], [[REGION, E]], base=0, channel_multiplier=0,
                      allow_small_or_imprecise_dtypes=True).then_inc(c, 1)
            pool.iota(dst_of[0][:, :], [[L, GT], [TOKENS, TOPK]], base=0, channel_multiplier=1,
                      allow_small_or_imprecise_dtypes=True).then_inc(c, 1)
            pool.iota(multiples[:, :], [[STEP, E]], base=0, channel_multiplier=0,
                      allow_small_or_imprecise_dtypes=True).then_inc(c, 1)
            pool.iota(step_no[:, :], [[1, STEPS]], base=0, channel_multiplier=0,
                      allow_small_or_imprecise_dtypes=True).then_inc(c, 1)
            pool.wait_ge(sem("const0"), 5)
            for m in (ident, ident16):
                pool.affine_select(out=m[:, :], in_=m[:, :], compare_op=ALU.not_equal, fill=1.0, base=0,
                                   pattern=[[-1, P]], channel_multiplier=1).then_inc(c, 1)
            pool.affine_select(out=causal[:, :], in_=ones[:, :], compare_op=ALU.is_ge, fill=0.0, base=0,
                               pattern=[[1, P]], channel_multiplier=-1).then_inc(c, 1)
            pool.affine_select(out=after_f, in_=ones[:, :], compare_op=ALU.is_gt, fill=0.0, base=0,
                               pattern=[[-1, P]], channel_multiplier=1).then_inc(c, 1)
            pool.affine_select(out=before_f, in_=ones[:, :], compare_op=ALU.is_gt, fill=0.0, base=0,
                               pattern=[[1, P]], channel_multiplier=-1).then_inc(c, 1)
            pool.affine_select(out=upto[:, :, :], in_=upto[:, :, :], compare_op=ALU.is_ge, fill=0.0, base=0,
                               pattern=[[1, E], [-1, E]], channel_multiplier=0).then_inc(c, 1)
            pool.iota(pad_rows[:, :, DST_COL:DST_COL + 1].bitcast(I32), [[0, HALVES]], base=SKIP_DST,
                      channel_multiplier=0).then_inc(c, 1)

            def gate():
                pool.sem_inc(sem("pool_gate"), 1)

            def split_x(g, p):
                wait(pool, "x_hi", g + 1)
                wait(pool, "z_proj", 2 * (g - 1))
                pool.tensor_tensor(x_lo[p][:, :, OFF:OFF + L], xT_g[p][:, :, :],
                                   x_hi[p][:, :, OFF:OFF + L].bitcast(F32), ALU.subtract
                                   ).then_inc(sem("x_lo"), 1)

            def spread_adt(g, p, h):
                wait(pool, "dta_g", g + 1)
                wait(pool, "seg", GT * g + 2 * h)
                gate()
                for n, dst in ((1, adt_hi), (2, adt_lo)):
                    col = dta_g[p][:, n, 2 * HEADS * h:2 * HEADS * (h + 1)]
                    pool.affine_select(out=dst[:, :, :], in_=col.unsqueeze(2).to_broadcast([P, 2 * HEADS, L]),
                                       compare_op=ALU.is_ge, fill=0.0, base=0,
                                       pattern=[[0, 2 * HEADS], [1, L]], channel_multiplier=-1
                                       ).then_inc(sem("adt"), 1)

            def inv_sqrt(n, src, name_in, count, name_out, done_count):
                wait(pool, name_in, count)
                pool.tensor_tensor(var_e[n][:, :], src, eps4[:, :], ALU.add).then_inc(sem(name_out + "_e"), 1)
                wait(pool, name_out + "_e", done_count)
                pool.tensor_tensor(rstd[n][:, :], var_e[n][:, :], minus_half[:, :], ALU.pow).then_inc(sem(name_out), 1)

            def norm_y(g, p):
                inv_sqrt(2, ss[:, :], "sumsq", GT * (g + 1), "rms", g + 1)

            def norm_a(g, p):
                inv_sqrt(0, mv[0][:, :, 1], "mv0", g + 1, "rstd0", g + 1)

            def norm_b(b, p):
                inv_sqrt(1, mv[1][:, :, 1], "mv1", b + 1, "rstd1", b + 1)

            def send_rows(c_, p, t):
                wait(pool, "pos", c_ + 1)
                wait(pool, "row_copies", c_ + 1)
                wait(pool, "row_w", c_ + 1)
                wait(pool, "row_dst", c_ + 1)
                gate()
                for k in range(TOPK):
                    n = TOPK * t + k
                    pool.indirect_dma_start(rows_dram, bass.IndirectOffsetOnAxis(ap=pos[p][:, n:n + 1], axis=0),
                                            rows[p][:, t, k, :], None).then_inc(sem(f"rows_sent{p}"), 16)

            def first(g, p):
                split_x(g, p)
                spread_adt(g, p, 0)

            def rows_of(t):
                return lambda c_, p: send_rows(c_, p, t)

            group_loop(pool, {"first": first, "adt1": lambda g, p: spread_adt(g, p, 1), "norm_b": norm_b,
                              "norm_y": norm_y, "norm_a": norm_a} | {f"rows{t}": rows_of(t) for t in range(GT)},
                       (("first", 0), ("adt1", 0), ("rows0", 2), ("norm_b", 1), ("rows1", 2), ("norm_y", 0),
                        ("rows2", 2), ("norm_a", 0), ("rows3", 2)))

            limit = pool.to_reg(TOPK * TOKENS - 1)

            def send_parts(j4, b):
                pool.wait_ge(sem("y_scaled"), 2 * (4 * j4 + b + 1))
                gate()
                for i in range(HALVES):
                    dst = xg[b][:, i, DST_COL:DST_COL + 1].bitcast(U32)
                    pool.indirect_dma_start(parts_dram, bass.IndirectOffsetOnAxis(ap=dst, axis=0),
                                            y_s[b % 2][:, i, :], None, bounds_check=limit, oob_is_err=False
                                            ).then_inc(sem(f"parts_sent{b}"), 16)

            with pool.Fori(0, STEPS // 4) as i:
                for b in range(4):
                    send_parts(i, b)

            with pool.Fori(0, GROUPS // 2) as i:
                for p in range(2):
                    f = 2 * i + p
                    inv_sqrt(2, mv[2][:, :, 1], "mv2", f + 1, "rstd2", f + 1)

        @block.scalar
        def _(act):
            def load(dst, src, name="weights"):
                act.dma_start(dst, src).then_inc(sem(name), 16)

            load(in_w, in_wT)
            load(conv_wb.rearrange("p j c -> p (j c)"), conv_w.partition_broadcast(P))
            load(dtb[:, :], dt_bias.partition_broadcast(P))
            load(alog[:, :], a_log.partition_broadcast(P))
            load(convb[:, :], conv_b)
            load(out_w, out_wT)
            load(normw[:, :], norm_w)
            for h in range(HEADS):
                load(dcol[HD * (h % 2):HD * (h % 2) + HD, h // 2:h // 2 + 1],
                     d_param[h:h + 1].partition_broadcast(HD))
            load(wq_s[:, :], wq)
            load(wk_s[:, :], wk)
            load(wv_s, wv)
            load(bq_s[:, :], bq)
            load(bk_s[:, :], bk)
            load(bv_s, bv.partition_broadcast(P))
            load(keys_s[:, :], keysT)
            load(rw_s[:, :], rwT)
            load(rb_s[:, :], rb.partition_broadcast(P))
            load(b1_s[:, :, :], b1T)
            for q in range(4):
                load(w2_s[:, 4 * q:4 * q + 4, :, :], w2T[:, 4 * q:4 * q + 4, :, :], "w2_loaded")

            act.wait_ge(sem("dt_negabs"), 1)
            act.activation(dtw[:, 2, :], dtw[:, 1, :], ACT.Exp).then_inc(sem("dt_exp"), 1)
            act.activation(a_exp[:, :], alog[:, :], ACT.Exp).then_inc(sem("a_exp"), 1)
            act.wait_ge(sem("dt_onep"), 1)
            act.activation(dtw[:, 4, :], dtw[:, 3, :], ACT.Ln).then_inc(sem("dt_ln"), 1)
            act.wait_ge(sem("conv_full"), 1)
            act.activation(conv_hi[:, :, :], conv_f, ACT.Copy).then_inc(sem("conv_high"), 1)
            act.wait_ge(sem("z_full"), 1)
            act.activation(z_hi[:, :], z_half, ACT.Copy).then_inc(sem("z_high"), 1)

            act.wait_ge(sem("constants"), N_CONST)

            def split_x(g, p):
                wait_load(act, f"xT_loaded{p}", g, p)
                wait(act, "z_proj", 2 * (g - 1))
                wait(act, "x_lo", g - 1)
                act.activation(x_hi[p][:, :, OFF:OFF + L], xT_g[p][:, :, :], ACT.Copy).then_inc(sem("x_hi"), 1)

            def conv_out(g, p):
                wait(act, "y", GT * g)
                for c in range(4):
                    wait(act, "conv", 4 * g + c + 1)
                    act.activation(xbc[:, c, :], front[c % 2][:, :], ACT.Identity, bias=convb_half[:, c:c + 1]
                                   ).then_inc(sem("conv_val"), 1)
                    wait(act, "xbc", 4 * g + c - 1)
                    act.activation(th[c % 2], front[c % 2][:, :], ACT.Tanh, bias=convb_half[:, c:c + 1]
                                   ).then_inc(sem("conv_tanh"), 1)
                wait(act, "gatedT_ps", 2 * g)
                for h in range(2):
                    wait(act, "z_proj", 2 * g + h + 1)
                    act.activation(z_gate[:, 2 * h:2 * h + 2, :],
                                   front[h][:, :].rearrange("p (t n) -> p t n", t=2), ACT.Tanh
                                   ).then_inc(sem("z_tanh"), 1)

            def decays(g, p):
                for t in range(GT):
                    wait(act, "seg", GT * g + t + 1)
                    wait(act, "y", GT * g + t - 1)
                    act.activation(decay[t % 2], segs[t % 2][:, :].rearrange("p (h l) -> p h l", h=HEADS),
                                   ACT.Exp).then_inc(sem("decay"), 1)

            def gated_out(g, p):
                wait(act, "rms", g)
                for h in range(2):
                    wait(act, "gated", 2 * g + h + 1)
                    for t in (2 * h, 2 * h + 1):
                        wait(act, "sumsq", GT * g + t)
                        act.activation(junk, z_gate[:, t, :], ACT.Square, scale=INNER ** -0.5,
                                       accum_out=ss[:, t:t + 1]).then_inc(sem("sumsq"), 1)
                    if h == 0:
                        wait(act, "mixed", g)
                    wait(act, "gatedT_ps", 2 * g + h + 1)
                    act.activation(gatedT[:, 2 * h:2 * h + 2, :, :],
                                   mids[1 - h][:, :].rearrange("p (t c l) -> p t c l", t=2, c=2), ACT.Copy
                                   ).then_inc(sem("gatedT"), 1)

            def project_out(b, p):
                wait(act, "k_proj", b + 1)
                wait(act, "scores", b)
                act.activation(kT_s, late[1][:, 0:GT * LC].rearrange("p (t l) -> p t l", t=GT),
                               ACT.Identity, bias=bk_s[:, 0:1]).then_inc(sem("kT"), 1)
                wait(act, "x1T_ps", b + 1)
                wait(act, "q_proj", b)
                act.activation(x1T_s[:, :], late[0][:, :], ACT.Copy).then_inc(sem("x1T"), 1)
                wait(act, "q_proj", b + 1)
                act.activation(qT_s[:, :], late[1][:, :], ACT.Identity, bias=bq_s[:, 0:1]).then_inc(sem("qT"), 1)

            def softmax(b, p):
                wait(act, "neg_max", b + 1)
                wait(act, "probT_ps", b)
                wait(act, "prob_rsum", b)
                for t in range(GT):
                    act.activation(prob[:, t, :], late[0][:, t * LC:(t + 1) * LC], ACT.Exp,
                                   bias=neg_max[:, t:t + 1], accum_out=prob_sum[:, t:t + 1]
                                   ).then_inc(sem("prob"), 1)
                wait(act, "probT_ps", b + 1)
                wait(act, "attended", b)
                act.activation(probT[0:LC, :, :], late[1][0:LC, :].rearrange("p (t l) -> p t l", t=GT),
                               ACT.Copy).then_inc(sem("probT"), 1)

            def route_a(c, p):
                wait(act, "x2T_ps", c + 1)
                wait(act, "logits", c)
                act.activation(x2T_s[:, :], late[0][:, :], ACT.Copy).then_inc(sem("x2T"), 1)
                wait(act, "x2", c + 1)
                if not isinstance(c, int) or c >= 2:
                    act.wait_ge(sem(f"rows_sent{p}"), 8 * GT * TOPK * (c - p))
                act.activation(rows[p][:, :, 0, 0:D // 2].bitcast(F16), x2[p][:, :, :], ACT.Copy
                               ).then_inc(sem("row_high"), 1)
                for n in range(2):
                    wait_load(act, f"w1_loaded{n}", c, None)
                    act.activation(w1_hi[:, bass.ds(2 * c + n, 1), :, :].rearrange("p e f m -> p (e f m)"),
                                   w1_stage[n][:, :], ACT.Copy, scale=W_SCALE).then_inc(sem("w1_high"), 1)

            def route_b_(c, p):
                wait(act, "top_diff", c + 1)
                wait(act, "row_w", c)
                act.activation(e4[:, :, :], d4[:, :, :], ACT.Exp).then_inc(sem("top_exp"), 1)
                wait(act, "row_low", c + 1)
                act.activation(rows[p][:, :, 1:TOPK, 0:D],
                               rows[p][:, :, 0:1, 0:D].to_broadcast([P, GT, TOPK - 1, D]), ACT.Copy
                               ).then_inc(sem("row_copies"), 1)
                act.dma_start(x2_dram[bass.ds(GT * c, GT), :, :].rearrange("s l d -> l s d"), x2[p][:, :, :]
                              ).then_inc(sem(f"x2_stored{p}"), 16)

            def first(g, p):
                split_x(g, p)
                conv_out(g, p)

            group_loop(act, {"Aa": first, "Ca": route_a, "Ba": project_out, "Cb": route_b_,
                             "Ab": decays, "Bb": softmax, "Ac": gated_out})

            def gelus(j, p, b):
                ex = act.value_load(step_e[0:1, bass.ds(j, 1)], min_val=0, max_val=E - 1)
                wait(act, "down", j - 1)
                for f in range(NF):
                    act.wait_ge(sem("up"), 2 * j + f // 2 + 1)
                    hb = banks[2 + 2 * p + f // 2]
                    act.activation(hid[p][:, f, :], hb[:, (f % 2) * STEP:(f % 2 + 1) * STEP], ACT.Gelu,
                                   bias=b1_s[:, bass.ds(ex, 1), f:f + 1].rearrange("p e f -> p (e f)"),
                                   scale=1.0 / W_SCALE).then_inc(sem("hidden"), 1)

            act.wait_ge(sem("plan"), N_PLAN)
            for j in range(2):
                gelus(j, j, 0)
            with act.Fori(1, STEPS // 2) as i:
                for p in range(2):
                    gelus(2 * i + p, p, 0)

            with act.Fori(0, GROUPS // 2) as i:
                for p in range(2):
                    act.wait_ge(sem(f"normed{p}"), i + 1)
                    act.dma_start(out[bass.ds(GT * (2 * i + p), GT), :, :].rearrange("s l d -> l s d"), y_out[p]
                                  ).then_inc(sem(f"stored{p}"), 16)

        @block.vector
        def _(dve):
            v = nc.vector
            dve.wait_ge(sem("weights"), 16 * N_WEIGHTS)
            dve.wait_ge(sem("constants"), N_CONST)
            dve.wait_ge(sem("dt_proj"), 1)
            dtv = banks[0][:, 0:SEQS * HEADS].rearrange("p (s h) -> p s h", h=HEADS)
            dt3 = dtw.rearrange("p n (s h) -> p n s h", h=HEADS)
            v.tensor_tensor(dt3[:, 0, :, :], dtv, dtb[:, :].unsqueeze(1).to_broadcast([P, SEQS, HEADS]), ALU.add
                            ).then_inc(sem("dt_u"), 1)
            v.tensor_copy(after[:, :], after_f).then_inc(sem("masks"), 1)
            v.tensor_copy(before16[:, :], before_f).then_inc(sem("masks"), 1)
            dve.wait_ge(sem("dt_u"), 1)
            v.scalar_tensor_tensor(dtw[:, 1, :], dtw[:, 0, :], -1.0, dtw[:, 0, :], ALU.mult, ALU.min
                                   ).then_inc(sem("dt_negabs"), 1)
            v.scalar_tensor_tensor(conv_f, conv_wb, 0.5, in_w[:, INNER:INNER + CONV].unsqueeze(1).to_broadcast(
                [P, TAPS, CONV]), ALU.mult, ALU.mult).then_inc(sem("conv_full"), 1)
            dve.wait_ge(sem("dt_exp"), 1)
            v.tensor_scalar(dtw[:, 3, :], dtw[:, 2, :], 1.0, None, ALU.add).then_inc(sem("dt_onep"), 1)
            v.tensor_scalar(z_half, in_w[:, 0:INNER], 0.5, None, ALU.mult).then_inc(sem("z_full"), 1)
            dve.wait_ge(sem("dt_onep"), 1)
            v.tensor_scalar(dtw[:, 5, :], dtw[:, 3, :], -1.0, None, ALU.add).then_inc(sem("dt_wm"), 1)
            dve.wait_ge(sem("dt_wm"), 1)
            v.scalar_tensor_tensor(dtw[:, 6, :], dtw[:, 5, :], 0.0, dtw[:, 2, :], ALU.is_equal, ALU.mult
                                   ).then_inc(sem("dt_tiny"), 1)
            v.tensor_scalar(dtw[:, 7, :], dtw[:, 5, :], 1e-30, None, ALU.max).then_inc(sem("dt_wmax"), 1)
            dve.wait_ge(sem("dt_wmax"), 1)
            dve.wait_ge(sem("dt_tiny"), 1)
            v.reciprocal(dtw[:, 5, :], dtw[:, 7, :]).then_inc(sem("dt_recip"), 1)
            dve.wait_ge(sem("dt_recip"), 1)
            v.tensor_tensor(dtw[:, 7, :], dtw[:, 5, :], dtw[:, 2, :], ALU.mult).then_inc(sem("dt_ratio"), 1)
            dve.wait_ge(sem("dt_ratio"), 1)
            dve.wait_ge(sem("dt_ln"), 1)
            v.tensor_tensor(dtw[:, 5, :], dtw[:, 7, :], dtw[:, 4, :], ALU.mult).then_inc(sem("dt_log"), 1)
            dve.wait_ge(sem("dt_log"), 1)
            v.tensor_tensor(dtw[:, 7, :], dtw[:, 5, :], dtw[:, 6, :], ALU.add).then_inc(sem("dt_log"), 1)
            dve.wait_ge(sem("dt_log"), 2)
            v.scalar_tensor_tensor(dta[:, 0, :], dtw[:, 0, :], 0.0, dtw[:, 7, :], ALU.max, ALU.add
                                   ).then_inc(sem("dt_split"), 1)
            dve.wait_ge(sem("dt_split"), 1)
            dve.wait_ge(sem("a_exp"), 1)
            v.scalar_tensor_tensor(dt3[:, 1, :, :], dta[:, 0, :].rearrange("p (s h) -> p s h", h=HEADS), -1.0,
                                   a_exp[:, :].unsqueeze(1).to_broadcast([P, SEQS, HEADS]), ALU.mult, ALU.mult
                                   ).then_inc(sem("adt_full"), 1)
            dve.wait_ge(sem("adt_full"), 1)
            v.tensor_copy(dta[:, 1, :].bitcast(F32R), dtw[:, 1, :]).then_inc(sem("dt_split"), 1)
            dve.wait_ge(sem("dt_split"), 2)
            v.tensor_tensor(dta[:, 2, :].bitcast(F32R), dtw[:, 1, :], dta[:, 1, :], ALU.subtract
                            ).then_inc(sem("dt_split"), 1)
            dve.wait_ge(sem("conv_high"), 1)
            v.tensor_tensor(conv_lo[:, :, :], conv_f, conv_hi[:, :, :].bitcast(F32), ALU.subtract
                            ).then_inc(sem("conv_low"), 1)
            dve.wait_ge(sem("z_high"), 1)
            v.tensor_tensor(z_lo[:, :], z_half, z_hi[:, :].bitcast(F32), ALU.subtract).then_inc(sem("z_low"), 1)
            s = sem("scaled")
            v.tensor_scalar(convb_half[:, :], convb[:, :], 0.5, None, ALU.mult).then_inc(s, 1)
            for c in range(2):
                v.tensor_scalar(out_wn[:, c, :], out_w[:, c, :], normw[:, c:c + 1], None, ALU.mult).then_inc(s, 1)
                v.tensor_scalar(d_diag[:, c, :], ident[:, :], dcol[:, c:c + 1], None, ALU.mult).then_inc(s, 1)
            v.tensor_scalar(wv_n[:, :], wv_s, NORM_FACT, None, ALU.mult).then_inc(s, 1)
            v.tensor_scalar(bv_n[:, :], bv_s, NORM_FACT, None, ALU.mult).then_inc(s, 1)
            v.scalar_tensor_tensor(route_w[:, :], keys_s[:, :], 2.0, rw_s[:, :], ALU.mult, ALU.add).then_inc(s, 1)
            v.tensor_tensor(keys_sq[:, :], keys_s[:, :], keys_s[:, :], ALU.mult).then_inc(sem("keys_sq"), 1)
            dve.wait_ge(sem("keys_norm"), 1)
            v.tensor_tensor(route_b[:, :], rb_s[:, :], banks[1][:, 0:E], ALU.subtract).then_inc(s, 1)
            dve.wait_ge(sem("dt_split"), 3)
            dve.wait_ge(sem("b2_loaded"), 16)
            b2_hi = b2_16[0:1, :, :].rearrange("p e d -> p (e d)")
            v.tensor_scalar(b2_hi, b2_stage, W_SCALE, None, ALU.mult).then_inc(sem("b2_high"), 1)
            dve.wait_ge(sem("b2_high"), 1)
            v.scalar_tensor_tensor(b2_lo, b2_stage, W_SCALE, b2_hi, ALU.mult, ALU.subtract).then_inc(sem("b2_low"), 1)

            def conv_out(g, p):
                wait(dve, "adt", 4 * (g - 1))
                v.tensor_copy(dta_g[p][:, :, :], dta[:, :, bass.ds(GT * HEADS * g, GT * HEADS)]
                              ).then_inc(sem("dta_g"), 1)
                for c in range(4):
                    wait(dve, "conv_tanh", 4 * g + c + 1)
                    v.scalar_tensor_tensor(xbc[:, c, :], th[c % 2], 1.0, xbc[:, c, :], ALU.add, ALU.mult
                                           ).then_inc(sem("xbc"), 1)
                for h in range(2):
                    wait(dve, "z_tanh", 2 * g + h + 1)
                    zz = z_gate[:, 2 * h:2 * h + 2, :].rearrange("p t n -> p (t n)")
                    v.scalar_tensor_tensor(zz, zz, 1.0, front[h][:, :], ALU.add, ALU.mult
                                           ).then_inc(sem("z_gate"), 1)

            def scan(g, p):
                wait(dve, "dta_g", g + 1)
                wait(dve, "y", GT * g)
                for h in range(2):
                    wait(dve, "x_turned", 2 * g + h + 1)
                    dtc = dta_g[p][:, 0, 2 * HEADS * h:2 * HEADS * (h + 1)]
                    v.tensor_tensor(xdt[:, 2 * h:2 * h + 2, :].rearrange("p t (h n) -> p (t h) n", n=HD),
                                    front[h][:, :].rearrange("p (a n) -> p a n", n=HD),
                                    dtc.unsqueeze(2).to_broadcast([P, 2 * HEADS, HD]), ALU.mult
                                    ).then_inc(sem("xdt"), 1)
                wait(dve, "cb", g + 1)
                v.tensor_tensor(cb_masked, mids[0][:, :].rearrange("p (t l) -> p t l", t=GT),
                                causal[:, :].unsqueeze(1).to_broadcast([P, GT, L]), ALU.mult
                                ).then_inc(sem("cb_masked"), 1)
                wait(dve, "cb_masked", g + 1)
                for t in range(GT):
                    wait(dve, "decay", GT * g + t + 1)
                    v.tensor_tensor(decay[t % 2], decay[t % 2],
                                    cb_masked[:, t:t + 1, :].to_broadcast([P, HEADS, L]), ALU.mult
                                    ).then_inc(sem("mix"), 1)
                    if t % 2:
                        h = t // 2
                        wait(dve, "y", GT * g + t + 1)
                        wait(dve, "z_gate", 2 * g + h + 1)
                        zz = z_gate[:, 2 * h:2 * h + 2, :].rearrange("p t n -> p (t n)")
                        v.tensor_tensor(zz, mids[1 - h][:, :], zz, ALU.mult).then_inc(sem("gated"), 1)

            def layer_norm(n, g, res, res_name, out_of, out_name):
                for t in range(GT):
                    wait(dve, res_name, GT * g + t + 1)
                    v.bn_stats(stats[n][:, t, :], res[:, t, :]).then_inc(sem(f"stats{n}"), 1)
                wait(dve, f"stats{n}", GT * (g + 1))
                wait(dve, f"rstd{n}_e", g)
                dve.sem_inc(sem("dve_gate"), 1)
                for t in range(GT):
                    ins = v.bn_aggr(mv[n][:, t, :], stats[n][:, t, :])
                ins.then_inc(sem(f"mv{n}"), 1)
                wait(dve, f"mv{n}", g + 1)
                wait(dve, f"rstd{n}", g + 1)
                for t in range(GT):
                    ins = v.tensor_scalar(out_of[:, t, :], res[:, t, :], mv[n][:, t, 0:1], rstd[n][:, t:t + 1],
                                          ALU.subtract, ALU.mult)
                ins.then_inc(sem(out_name), 1)

            def mixer_out(g, p):
                wait(dve, "mixed", g + 1)
                wait(dve, "rms", g + 1)
                wait_load(dve, f"x_loaded{p}", g, p)
                for t in range(GT):
                    v.scalar_tensor_tensor(res1[:, t, :], mids[1][:, t * D:(t + 1) * D], rstd[2][:, t:t + 1],
                                           x_tok[p][:, t, :], ALU.mult, ALU.add).then_inc(sem("res1"), 1)
                wait(dve, "x1T_ps", g - 1)
                wait(dve, "res2", GT * (g - 1))
                layer_norm(0, g, res1, "res1", x1[p], "x1")

            def attend_a(b, p):
                wait(dve, "v_proj", b + 1)
                wait(dve, "attended", b)
                v.tensor_tensor(v_s[0:LC, :, :], late[0][0:LC, :].rearrange("p (t d) -> p t d", t=GT),
                                bv_n[0:LC, :].unsqueeze(1).to_broadcast([LC, GT, D]), ALU.add
                                ).then_inc(sem("v"), 1)
                wait(dve, "scores", b + 1)
                wait(dve, "prob", GT * b)
                v.tensor_reduce(neg_max[:, :], late[0][:, 0:GT * LC].rearrange("p (t l) -> p t l", t=GT),
                                AX_X, ALU.max, negate=True).then_inc(sem("neg_max"), 1)

            def attend_b(b, p):
                wait(dve, "prob", GT * (b + 1))
                wait(dve, "res2", GT * b)
                v.reciprocal(prob_rsum[:, :], prob_sum[:, :]).then_inc(sem("prob_rsum"), 1)
                wait(dve, "attended", b + 1)
                wait(dve, "prob_rsum", b + 1)
                for t in range(GT):
                    v.scalar_tensor_tensor(res2[:, t, :], late[0][:, t * D:(t + 1) * D], prob_rsum[:, t:t + 1],
                                           x1[p][:, t, :], ALU.mult, ALU.add).then_inc(sem("res2"), 1)
                if not isinstance(b, int) or b >= 2:
                    dve.wait_ge(sem(f"x2_stored{p}"), 8 * (b - p))
                wait(dve, "x2T_ps", b - 1)
                wait(dve, "row_low", b - 1)
                wait(dve, "row_high", b - 1)
                layer_norm(1, b, res2, "res2", x2[p], "x2")

            def route_a(c, p):
                for n in range(2):
                    wait(dve, "w1_high", 2 * c + n + 1)
                    hi = w1_hi[:, bass.ds(2 * c + n, 1), :, :].rearrange("p e f m -> p (e f m)")
                    lo = w1_lo[:, bass.ds(2 * c + n, 1), :, :].rearrange("p e f m -> p (e f m)")
                    v.scalar_tensor_tensor(lo, w1_stage[n][:, :], W_SCALE, hi, ALU.mult, ALU.subtract
                                           ).then_inc(sem("w1_low"), 1)
                wait(dve, "logits", c + 1)
                v.tensor_tensor(logit[:, :, :], late[1][:, 0:GT * E].rearrange("p (t e) -> p t e", t=GT),
                                route_b[:, :].unsqueeze(1).to_broadcast([P, GT, E]), ALU.add
                                ).then_inc(sem("logit"), 1)
                wait(dve, "row_high", c + 1)
                v.tensor_tensor(rows[p][:, :, 0, D // 2:D].bitcast(F16), x2[p][:, :, :],
                                rows[p][:, :, 0, 0:D // 2].bitcast(F16), ALU.subtract
                                ).then_inc(sem("row_low"), 1)
                wait(dve, "logit", c + 1)
                dve.sem_inc(sem("dve_gate"), 1)
                for t in range(GT):
                    ins = v.max(top8[:, t, :], logit[:, t, :])
                ins.then_inc(sem("top8"), 1)
                wait(dve, "top8", c + 1)
                dve.sem_inc(sem("dve_gate"), 1)
                for t in range(GT):
                    ins = v.max_index(idx8[:, t, :], top8[:, t, :], logit[:, t, :])
                ins.then_inc(sem("idx8"), 1)
                v.tensor_tensor(d4[:, :, :], top8[:, :, 0:TOPK], top8[:, :, 0:1].to_broadcast([P, GT, TOPK]),
                                ALU.subtract).then_inc(sem("top_diff"), 1)
                wait(dve, "idx8", c + 1)
                v.tensor_copy(idx_f[:, :, :], idx8[:, :, 0:TOPK]).then_inc(sem("idx_f"), 1)
                wait(dve, "dst_next", c)
                v.tensor_scalar(rows[p][:, :, :, DST_COL].bitcast(U32),
                                dst_of[p][:, :].rearrange("p (t k) -> p t k", k=TOPK), 0.0, None, ALU.add
                                ).then_inc(sem("row_dst"), 1)
                v.tensor_scalar(dst_of[1 - p][:, :], dst_of[p][:, :], float(GTOK), None, ALU.add
                                ).then_inc(sem("dst_next"), 1)
                wait(dve, "idx_f", c + 1)
                v.tensor_tensor(onehot[:, :, :],
                                idx_f[:, :, :].rearrange("p t k -> p (t k)").unsqueeze(2).to_broadcast(
                                    [P, GT * TOPK, E]),
                                iota_e[:, :].unsqueeze(1).to_broadcast([P, GT * TOPK, E]), ALU.is_equal
                                ).then_inc(sem("onehot"), 1)
                wait(dve, "onehot", c + 1)
                wait(dve, "ranks", c)
                with nc.allow_low_precision(reason="zeros and ones"):
                    v.tensor_reduce(picked[:, :, :], onehot[:, :, :].rearrange("p (t k) e -> p t e k", t=GT),
                                    AX_X, ALU.add).then_inc(sem("picked"), 1)

            def route_b_(c, p):
                wait(dve, "top_exp", c + 1)
                v.tensor_reduce(s4[:, :], e4[:, :, :], AX_X, ALU.add).then_inc(sem("top_sum"), 1)
                wait(dve, "picked", c + 1)
                v.tensor_reduce(group_n[:, :], picked[:, :, :].rearrange("p t e -> p e t"), AX_X, ALU.add
                                ).then_inc(sem("group_n"), 1)
                wait(dve, "top_sum", c + 1)
                v.reciprocal(r4[:, :], s4[:, :]).then_inc(sem("top_recip"), 1)
                wait(dve, "group_n", c + 1)
                v.tensor_tensor(carry16[p][:, :], carry16[1 - p][:, :], group_n[:, :], ALU.add
                                ).then_inc(sem("carry"), 1)
                wait(dve, "top_recip", c + 1)
                v.tensor_tensor(rows[p][:, :, :, W_COL], e4[:, :, :],
                                r4[:, :].unsqueeze(2).to_broadcast([P, GT, TOPK]), ALU.mult
                                ).then_inc(sem("row_w"), 1)
                wait(dve, "ranks", c + 1)
                v.tensor_tensor(slot[:, :, :], late[1][:, 0:GT * E].rearrange("p (t e) -> p t e", t=GT),
                                region_of[:, :].unsqueeze(1).to_broadcast([P, GT, E]), ALU.add
                                ).then_inc(sem("slot"), 1)
                wait(dve, "slot", c + 1)
                v.tensor_tensor(onehot[:, :, :].rearrange("p (t k) e -> p t k e", t=GT),
                                onehot[:, :, :].rearrange("p (t k) e -> p t k e", t=GT),
                                slot[:, :, :].unsqueeze(2).to_broadcast([P, GT, TOPK, E]), ALU.mult
                                ).then_inc(sem("chosen"), 1)
                wait(dve, "chosen", c + 1)
                v.tensor_reduce(pos_f[:, :], onehot[:, :, :], AX_X, ALU.add).then_inc(sem("pos_f"), 1)
                wait(dve, "pos_f", c + 1)
                v.tensor_copy(pos[p][:, :], pos_f[:, :]).then_inc(sem("pos"), 1)

            group_loop(dve, {"Aa": conv_out, "Ca": route_a, "Ba": attend_a, "Cb": route_b_,
                             "Ab": scan, "Bb": attend_b, "Ac": mixer_out})

            plan, n_plan = sem("plan"), [0]

            def planned(ins):
                ins.then_inc(plan, 1)
                n_plan[0] += 1
                dve.wait_ge(plan, n_plan[0])

            dve.wait_ge(sem("counts"), 1)
            planned(v.tensor_copy(cnt[:, :], banks[0][0:1, 0:E]))
            planned(v.tensor_tensor(pad_f[:, :], cnt[:, :], region_of[0:1, :], ALU.add))
            planned(v.tensor_copy(pad_at[:, :], pad_f[:, :]))
            planned(v.tensor_tensor(over[:, :, :], cnt[:, :].unsqueeze(2).to_broadcast([1, E, E]),
                                    multiples[:, :].unsqueeze(1).to_broadcast([1, E, E]), ALU.is_gt))
            planned(v.tensor_reduce(n_steps[:, :], over[:, :, :], AX_X, ALU.add))
            planned(v.tensor_tensor(over[:, :, :], n_steps[:, :].unsqueeze(1).to_broadcast([1, E, E]),
                                    upto[:, :, :], ALU.mult))
            planned(v.tensor_reduce(last_step[:, :], over[:, :, :], AX_X, ALU.add))
            planned(v.tensor_tensor(done[:, :, :], last_step[:, :].unsqueeze(1).to_broadcast([1, STEPS, E]),
                                    step_no[:, :].unsqueeze(2).to_broadcast([1, STEPS, E]), ALU.is_le))
            planned(v.tensor_reduce(step_ef[:, :], done[:, :, :], AX_X, ALU.add))
            planned(v.tensor_tensor(done[:, :, :], done[:, :, :],
                                    n_steps[:, :].unsqueeze(1).to_broadcast([1, STEPS, E]), ALU.mult))
            planned(v.tensor_reduce(steps_before[:, :], done[:, :, :], AX_X, ALU.add))
            planned(v.tensor_tensor(row_f[:, :], step_no[:, :], steps_before[:, :], ALU.subtract))
            planned(v.tensor_scalar(row_f[:, :], row_f[:, :], float(STEP), None, ALU.mult))
            planned(v.scalar_tensor_tensor(row_f[:, :], step_ef[:, :], float(REGION), row_f[:, :],
                                           ALU.mult, ALU.add))
            planned(v.tensor_scalar(step_row[:, :], row_f[:, :], float(E * REGION), None, ALU.min))
            planned(v.tensor_scalar(step_e[:, :], step_ef[:, :], float(E - 1), None, ALU.min))
            assert n_plan[0] == N_PLAN

            def turned(j, p):
                dve.wait_ge(sem("rows_turned"), j + 1)
                wait(dve, "up", 2 * (j - 1))
                v.tensor_copy(xgT[p], turn_ps[p]).then_inc(sem("xgT"), 1)

            def scaled(j, p, b):
                if not isinstance(j, int) or j >= 2:
                    q, at = (b - 2) % 4, (j - 2 - (b - 2) % 4)
                    dve.wait_ge(sem(f"parts_sent{q}"), 8 * at + 32)
                for i in range(HALVES):
                    dve.wait_ge(sem("down"), j + 1)
                    v.tensor_scalar(y_s[p][:, i, :], banks[6 + p][:, i * D:(i + 1) * D],
                                    xg[b][:, i, W_COL:W_COL + 1], None, ALU.mult).then_inc(sem("y_scaled"), 1)

            turned(0, 0)
            turned(1, 1)
            scaled(0, 0, 0)
            turned(2, 0)
            scaled(1, 1, 1)
            turned(3, 1)
            scaled(2, 0, 2)
            turned(4, 0)
            scaled(3, 1, 3)
            with dve.Fori(1, STEPS // 4 - 1) as i:
                for b in range(4):
                    turned(4 * i + b + 1, (b + 1) % 2)
                    scaled(4 * i + b, b % 2, b)
            for b in range(4):
                j = STEPS - 4 + b
                if j + 1 < STEPS:
                    turned(j + 1, (b + 1) % 2)
                scaled(j, b % 2, b)

            def last(i):
                for p in range(2):
                    f = 2 * i + p
                    dve.wait_ge(sem(f"parts_loaded{p}"), 16 * (TOPK + 1) * (i + 1))
                    tot = total[p].rearrange("p t d -> p (t d)")
                    v.tensor_tensor(tot, x2_back[p].rearrange("p t d -> p (t d)"), parts[p][:, 0, :], ALU.add
                                    ).then_inc(sem("sum"), 1)
                    for k in range(1, TOPK):
                        dve.wait_ge(sem("sum"), TOPK * f + k)
                        v.tensor_tensor(tot, tot, parts[p][:, k, :], ALU.add).then_inc(sem("sum"), 1)
                    dve.wait_ge(sem("sum"), TOPK * f + TOPK)
                    for t in range(GT):
                        v.bn_stats(stats[2][:, t, :], total[p][:, t, :]).then_inc(sem("stats2"), 1)
                    dve.wait_ge(sem("stats2"), GT * (f + 1))
                    wait(dve, "rstd2_e", f)
                    dve.sem_inc(sem("dve_gate"), 1)
                    for t in range(GT):
                        ins = v.bn_aggr(mv[2][:, t, :], stats[2][:, t, :])
                    ins.then_inc(sem("mv2"), 1)
                    dve.wait_ge(sem("mv2"), f + 1)
                    dve.wait_ge(sem("rstd2"), f + 1)
                    wait(dve, f"stored{p}", 16 * i)
                    for t in range(GT):
                        ins = v.tensor_scalar(y_out[p][:, t, :], total[p][:, t, :], mv[2][:, t, 0:1],
                                              rstd[2][:, t:t + 1], ALU.subtract, ALU.mult)
                    ins.then_inc(sem(f"normed{p}"), 1)

            last(0)
            with dve.Fori(1, GROUPS // 2) as i:
                last(i)

        @block.tensor
        def _(pe):
            mm = nc.tensor.matmul

            def three(ps, lhi, llo, rhi, rlo, start=True, stop=True):
                mm(ps, lhi, rlo, start=start, stop=False)
                mm(ps, llo, rhi, start=False, stop=False)
                return mm(ps, lhi, rhi, start=False, stop=stop)

            pe.wait_ge(sem("xT_loaded"), 64)
            pe.wait_ge(sem("weights"), 16 * N_WEIGHTS)
            for n in range(SEQS):
                ins = mm(banks[0][:, HEADS * n:HEADS * (n + 1)], xT_all[:, n, :], in_w[:, INNER + CONV:],
                         start=True, stop=True)
            ins.then_inc(sem("dt_proj"), 1)
            pe.wait_ge(sem("constants"), N_CONST)
            pe.wait_ge(sem("keys_sq"), 1)
            mm(banks[1][:, 0:E], ones[:, :], keys_sq[:, :], start=True, stop=True).then_inc(sem("keys_norm"), 1)
            pe.wait_ge(sem("conv_low"), 1)
            pe.wait_ge(sem("z_low"), 1)
            pe.wait_ge(sem("masks"), 2)
            pe.wait_ge(sem("scaled"), N_SCALED)

            def conv(g, p):
                wait(pe, "x_hi", g + 1)
                wait(pe, "x_lo", g + 1)
                for c in range(4):
                    if c < 2:
                        wait(pe, "xdt", 2 * (g - 1) + c + 1)
                    else:
                        wait(pe, "conv_tanh", 4 * g + c - 1)
                    ps = front[c % 2][:, :]
                    for j in range(TAPS):
                        w = slice(c * P, (c + 1) * P)
                        ins = three(ps, conv_hi[:, j, w], conv_lo[:, j, w], x_hi[p][:, :, j:j + L],
                                    x_lo[p][:, :, j:j + L], start=(j == 0), stop=(j == TAPS - 1))
                    ins.then_inc(sem("conv"), 1)
                for h in range(2):
                    wait(pe, "conv_tanh", 4 * g + 3 + h)
                    for t in (2 * h, 2 * h + 1):
                        ins = three(front[h][:, (t % 2) * INNER:(t % 2 + 1) * INNER],
                                    x_hi[p][:, t, OFF:OFF + L], x_lo[p][:, t, OFF:OFF + L],
                                    z_hi[:, :], z_lo[:, :])
                    ins.then_inc(sem("z_proj"), 1)

            def scan(g, p):
                wait(pe, "xbc", 4 * g + 2)
                for h in range(2):
                    wait(pe, "z_gate", 2 * g + h + 1)
                    for t in (2 * h, 2 * h + 1):
                        for c in range(2):
                            at = (t % 2) * INNER + c * P
                            ins = nc.tensor.transpose(front[h][:, at:at + P], xbc[:, c, t * L:(t + 1) * L],
                                                      ident[:, :])
                    ins.then_inc(sem("x_turned"), 1)

                def segments(t):
                    wait(pe, "adt", 4 * g + 2 * (t // 2) + 2)
                    wait(pe, "decay", GT * g + t - 1)
                    hs = slice(HEADS * (t % 2), HEADS * (t % 2 + 1))
                    mm(segs[t % 2][:, :], after[:, :], adt_hi[:, hs, :], start=True, stop=False)
                    mm(segs[t % 2][:, :], after[:, :], adt_lo[:, hs, :], start=False, stop=True
                       ).then_inc(sem("seg"), 1)

                def outputs(t):
                    wait(pe, "xdt", 2 * g + t // 2 + 1)
                    wait(pe, "mix", GT * g + t + 1)
                    if t == 0:
                        wait(pe, "res1", GT * g)
                    if t == 2:
                        wait(pe, "cb_masked", g + 1)
                    ps = mids[1 - t // 2]
                    for c in range(2):
                        at = (t % 2) * INNER + c * P
                        mm(ps[:, at:at + P], xbc[:, c, t * L:(t + 1) * L], d_diag[:, c, :], start=True, stop=False)
                        for h in (2 * c, 2 * c + 1):
                            at = (t % 2) * INNER + h * HD
                            ins = mm(ps[:, at:at + HD], decay[t % 2][:, h, :], xdt[:, t, h * HD:(h + 1) * HD],
                                     start=False, stop=(h == 2 * c + 1))
                    ins.then_inc(sem("y"), 1)

                segments(0)
                segments(1)
                wait(pe, "xbc", 4 * g + 4)
                wait(pe, "gatedT", 2 * g)
                for t in range(GT):
                    ts = slice(t * L, (t + 1) * L)
                    ins = mm(mids[0][:, ts], xbc[:, 2, ts], xbc[:, 3, ts], start=True, stop=True)
                ins.then_inc(sem("cb"), 1)
                outputs(0)
                segments(2)
                outputs(1)
                segments(3)
                outputs(2)
                outputs(3)

            def mixer_out(g, p):
                for h in range(2):
                    wait(pe, "gated", 2 * g + h + 1)
                    for t in (2 * h, 2 * h + 1):
                        for c in range(2):
                            at = (t % 2) * INNER + c * P
                            ins = nc.tensor.transpose(mids[1 - h][:, at:at + P], z_gate[:, t, c * P:(c + 1) * P],
                                                      ident[:, :])
                    ins.then_inc(sem("gatedT_ps"), 1)
                wait(pe, "gatedT", 2 * g + 2)
                for t in range(GT):
                    for c in range(2):
                        ins = mm(mids[1][:, t * D:(t + 1) * D], gatedT[:, t, c, :], out_wn[:, c, :],
                                 start=(c == 0), stop=(c == 1))
                ins.then_inc(sem("mixed"), 1)

            def attend_a(b, p):
                wait_load(pe, f"ctx_loaded{p}", b, p)
                wait(pe, "logit", b)
                mm(late[1][:, 0:GT * LC], wk_s[:, :], ctx_s[p][:, :, 0:LC], start=True, stop=True
                   ).then_inc(sem("k_proj"), 1)
                wait(pe, "x1", b + 1)
                wait(pe, "x2T", b)
                for t in range(GT):
                    ins = nc.tensor.transpose(late[0][:, t * L:(t + 1) * L], x1[p][:, t, :], ident[:, :])
                ins.then_inc(sem("x1T_ps"), 1)
                wait(pe, "kT", b + 1)
                wait(pe, "x1T", b + 1)
                mm(late[1][:, :], wq_s[:, :], x1T_s[:, :], start=True, stop=True).then_inc(sem("q_proj"), 1)
                for t in range(GT):
                    ins = mm(late[0][0:LC, t * D:(t + 1) * D], ctx_s[p][:, t, 0:LC], wv_n[:, :],
                             start=True, stop=True)
                ins.then_inc(sem("v_proj"), 1)
                wait(pe, "qT", b + 1)
                wait(pe, "v", b + 1)
                for t in range(GT):
                    ins = mm(late[0][:, t * LC:(t + 1) * LC], qT_s[:, t * L:(t + 1) * L], kT_s[:, t, :],
                             start=True, stop=True)
                ins.then_inc(sem("scores"), 1)

            def attend_b(b, p):
                wait(pe, "prob", GT * (b + 1))
                wait(pe, "slot", b)
                for t in range(GT):
                    ins = nc.tensor.transpose(late[1][0:LC, t * L:(t + 1) * L], prob[:, t, :], ident[:, :])
                ins.then_inc(sem("probT_ps"), 1)
                wait(pe, "probT", b + 1)
                for t in range(GT):
                    ins = mm(late[0][:, t * D:(t + 1) * D], probT[0:LC, t, :], v_s[0:LC, t, :],
                             start=True, stop=True)
                ins.then_inc(sem("attended"), 1)

            def route_a(c, p):
                wait(pe, "x2", c + 1)
                for t in range(GT):
                    ins = nc.tensor.transpose(late[0][:, t * L:(t + 1) * L], x2[p][:, t, :], ident[:, :])
                ins.then_inc(sem("x2T_ps"), 1)
                wait(pe, "x2T", c + 1)
                for t in range(GT):
                    ins = mm(late[1][:, t * E:(t + 1) * E], x2T_s[:, t * L:(t + 1) * L], route_w[:, :],
                             start=True, stop=True)
                ins.then_inc(sem("logits"), 1)

            def route_b_(c, p):
                wait(pe, "picked", c + 1)
                wait(pe, "carry", c)
                if not isinstance(c, int) or c + 1 < GROUPS:
                    wait(pe, "qT", c + 2)
                ps = late[1]
                flat = picked[:, :, :].rearrange("p t e -> p (t e)")
                mm(ps[:, 0:GT * E], before16[:, :], flat, start=True, stop=False)
                for t in range(GT - 1):
                    n = GT - 1 - t
                    mm(ps[:, (t + 1) * E:GT * E].rearrange("p (t e) -> p t e", e=E), ones16[:, :],
                       picked[:, t:t + 1, :].to_broadcast([P, n, E]), start=False, stop=False)
                mm(ps[:, 0:GT * E].rearrange("p (t e) -> p t e", e=E), ones16[:, :],
                   carry16[1 - p][:, :].unsqueeze(1).to_broadcast([P, GT, E]), start=False, stop=True
                   ).then_inc(sem("ranks"), 1)

            group_loop(pe, {"Aa": conv, "Ca": route_a, "Ba": attend_a, "Cb": route_b_,
                            "Ab": scan, "Bb": attend_b, "Ac": mixer_out})

            pe.wait_ge(sem("carry"), GROUPS)
            pe.wait_ge(sem("xdt"), 2 * GROUPS)
            mm(banks[0][:, 0:E], ones16[:, :], carry16[(GROUPS - 1) % 2][:, :], start=True, stop=True
               ).then_inc(sem("counts"), 1)

            pe.wait_ge(sem("plan"), N_PLAN)
            pe.wait_ge(sem("w1_low"), E)
            pe.wait_ge(sem("w2_loaded"), 64)
            pe.wait_ge(sem("b2_split"), 16)
            pe.wait_ge(sem("x2"), GROUPS)

            def turn(j, p, b):
                if isinstance(j, int) and j < 4:
                    pe.wait_ge(sem(f"xg_loaded{b}"), 16)
                else:
                    pe.wait_ge(sem(f"xg_loaded{b}"), 4 * (j - b) + 16)
                wait(pe, "xgT", j - 1)
                for hl in range(2):
                    for i in range(HALVES):
                        ins = nc.tensor.transpose(turn_ps[p][:, hl, i * P:(i + 1) * P],
                                                  xg[b][:, i, hl * D // 2:(hl + 1) * D // 2].bitcast(F16),
                                                  ident16[:, :])
                ins.then_inc(sem("rows_turned"), 1)

            def up(j, p):
                ex = pe.value_load(step_e[0:1, bass.ds(j, 1)], min_val=0, max_val=E - 1)
                wait(pe, "xgT", j + 1)
                for f in range(NF):
                    wait(pe, "hidden", NF * (j - 2) + 2 * (f // 2) + 2)
                    ps = banks[2 + 2 * p + f // 2][:, (f % 2) * STEP:(f % 2 + 1) * STEP]
                    wh = w1_hi[:, bass.ds(ex, 1), f, :].rearrange("p e m -> p (e m)")
                    wl = w1_lo[:, bass.ds(ex, 1), f, :].rearrange("p e m -> p (e m)")
                    ins = three(ps, wh, wl, xgT[p][:, 0, :], xgT[p][:, 1, :])
                    if f % 2:
                        ins.then_inc(sem("up"), 1)

            def down(j, p):
                ex = pe.value_load(step_e[0:1, bass.ds(j, 1)], min_val=0, max_val=E - 1)
                wait(pe, "y_scaled", HALVES * (j - 1))
                for i in range(HALVES):
                    ps = banks[6 + p][:, i * D:(i + 1) * D]
                    for f in range(NF):
                        if i == 0:
                            pe.wait_ge(sem("hidden"), NF * j + f + 1)
                        ins = mm(ps, hid[p][:, f, i * P:(i + 1) * P],
                                 w2_s[:, bass.ds(ex, 1), f, :].rearrange("p e m -> p (e m)"),
                                 start=(f == 0), stop=False)
                    ins = mm(ps, unscale16[:, :], b2_16[:, bass.ds(ex, 1), :].rearrange("p e m -> p (e m)"),
                             start=False, stop=True)
                ins.then_inc(sem("down"), 1)

            turn(0, 0, 0)
            turn(1, 1, 1)
            up(0, 0)
            turn(2, 0, 2)
            up(1, 1)
            down(0, 0)
            turn(3, 1, 3)
            up(2, 0)
            down(1, 1)
            turn(4, 0, 0)
            up(3, 1)
            down(2, 0)
            with pe.Fori(1, STEPS // 4 - 1) as i:
                for b in range(4):
                    turn(4 * i + b + 1, (b + 1) % 2, (b + 1) % 4)
                    up(4 * i + b, b % 2)
                    down(4 * i + b - 1, (b + 1) % 2)
            for b in range(4):
                j = STEPS - 4 + b
                if j + 1 < STEPS:
                    turn(j + 1, (b + 1) % 2, (b + 1) % 4)
                up(j, b % 2)
                down(j - 1, (b + 1) % 2)
            down(STEPS - 1, (STEPS - 1) % 2)


_INS = ["x", "xT", "ctxT", "in_wT", "conv_w", "conv_b", "norm_w", "out_wT", "dt_bias", "a_log", "d_param",
        "wq", "bq", "wk", "bk", "wv", "bv", "keysT", "w1T", "b1T", "w2T", "b2", "rwT", "rb"]


def kernel(x, ctx_1024, L0_attn_in_proj_w, L0_attn_conv_w, L0_attn_conv_b, L0_attn_norm_w, L0_attn_out_proj_w,
           L0_attn_dt_bias, L0_attn_A_log, L0_attn_D_param, L0_xattn_Wq, L0_xattn_bq, L0_xattn_Wk, L0_xattn_bk,
           L0_xattn_Wv, L0_xattn_bv, L0_ffn_keys, L0_ffn_w1, L0_ffn_b1, L0_ffn_w2, L0_ffn_b2, L0_ffn_rw,
           L0_ffn_rb):
    import concourse.bacc as _bacc
    from concourse.bass_utils import run_bass_kernel_spmd as _run

    a = [np.asarray(v) for v in (
        x, ctx_1024, L0_attn_in_proj_w, L0_attn_conv_w, L0_attn_conv_b, L0_attn_norm_w, L0_attn_out_proj_w,
        L0_attn_dt_bias, L0_attn_A_log, L0_attn_D_param, L0_xattn_Wq, L0_xattn_bq, L0_xattn_Wk, L0_xattn_bk,
        L0_xattn_Wv, L0_xattn_bv, L0_ffn_keys, L0_ffn_w1, L0_ffn_b1, L0_ffn_w2, L0_ffn_b2, L0_ffn_rw, L0_ffn_rb)]
    (xx, cc, inw, cw, cb, nw, ow, dtb, al, dp, wq, bq, wk, bk, wv, bv, keys, w1, b1, w2, b2, rw, rb) = a
    laid = dict(
        x=xx, xT=xx.reshape(TOKENS, D).T, ctxT=cc.transpose(2, 0, 1), in_wT=inw.T,
        conv_w=cw.reshape(CONV, TAPS).T.reshape(-1), conv_b=cb.reshape(4, P).T, norm_w=nw.reshape(2, P).T,
        out_wT=ow.T.reshape(2, P, D).transpose(1, 0, 2), dt_bias=dtb, a_log=al, d_param=dp,
        wq=wq, bq=bq.reshape(P, 1), wk=wk, bk=bk.reshape(P, 1), wv=wv, bv=bv, keysT=keys.T,
        w1T=w1.transpose(2, 0, 1), b1T=b1.reshape(E, NF, P).transpose(2, 0, 1),
        w2T=w2.reshape(E, D, NF, P).transpose(3, 0, 2, 1), b2=b2.reshape(1, E * D), rwT=rw.T, rb=rb)
    nc = _bacc.Bacc("TRN2", target_bir_lowering=False, num_devices=1)
    arrays, args = {}, []
    for name in _INS:
        v = np.ascontiguousarray(laid[name])
        arrays[f"in_{name}_dram"] = v
        args.append(nc.dram_tensor(f"in_{name}_dram", v.shape, mybir.dt.from_np(v.dtype), kind="ExternalInput").ap())
    out = nc.dram_tensor("out_dram", (SEQS, L, D), F32, kind="ExternalOutput").ap()
    decoder_layer(nc, *args, out)
    r = _run(nc, [arrays], core_ids=[0])
    return r.results[0]["out_dram"]
```

```python
from contextlib import ExitStack

import numpy as np

import concourse.bass as bass
from concourse import mybir

F32 = mybir.dt.float32
F32R = mybir.dt.float32r
F16 = mybir.dt.float16
BF16 = mybir.dt.bfloat16
I32 = mybir.dt.int32
U32 = mybir.dt.uint32
ALU = mybir.AluOpType
ACT = mybir.ActivationFunctionType
AX_X = mybir.AxisListType.X

P = 128
SEQS, L, D = 32, 128, 128
TOKENS = SEQS * L
LC = 77
HEADS, HD = 4, 64
INNER = HEADS * HD
CONV = INNER + 2 * P
TAPS = 4
E, TOPK, FF = 16, 4, 512
NF = FF // P
EPS = 1e-5
GT = 4
GROUPS = SEQS // GT
GTOK = GT * L
PADT = 132
OFF = TAPS - 1
STEP = 256
HALVES = STEP // P
STEPS = -(-(TOPK * TOKENS + E * (STEP - 1)) // STEP)
ROWS_RING, Y_RING = 8, 4
STEPS += -STEPS % ROWS_RING
REGION = TOKENS + STEP
ROW_W = 130
W_COL, DST_COL = 128, 129
W_SCALE = 64.0
SKIP_DST = 1 << 20
NORM_FACT = float(1.0 / np.sqrt(np.float32(D)))
N_CONST = 21
N_WEIGHTS = 21
N_SCALED = 9
N_PLAN = 16


def decoder_layer(nc, x, xT, ctxT, in_wT, conv_w, conv_b, norm_w, out_wT, dt_bias, a_log, d_param,
                  wq, bq, wk, bk, wv, bv, keysT, w1T, b1T, w2T, b2, rwT, rb, out):
    with ExitStack() as ctx:
        def sb(name, shape, dt=F32):
            return ctx.enter_context(nc.sbuf_tensor(name, shape, dt))

        def bank(name):
            return ctx.enter_context(nc.psum_tensor(name, [P, 512], F32))

        sems = {}

        def sem(name):
            if name not in sems:
                sems[name] = ctx.enter_context(nc.semaphore(name))
            return sems[name]

        def wait(eng, name, count):
            if not (isinstance(count, int) and count <= 0):
                eng.wait_ge(sem(name), count)

        def wait_load(eng, name, g, p):
            if p is None:
                wait(eng, name, 16 * g + 16)
            else:
                wait(eng, name, 8 * (g - p) + 16)

        rows_dram = nc.dram_tensor("rows_dram", [E * REGION + STEP, ROW_W], F32).ap()
        parts_dram = nc.dram_tensor("parts_dram", [TOPK * TOKENS, D], F32).ap()
        x2_dram = nc.dram_tensor("x2_dram", [SEQS, L, D], F32).ap()

        ident = sb("ident", [P, P])
        ident16 = sb("ident16", [P, P], F16)
        causal = sb("causal", [P, P])
        after = sb("after", [P, P], F32R)
        before16 = sb("before16", [P, P], BF16)
        ones16 = sb("ones16", [P, P], BF16)
        ones = sb("ones", [P, P])
        unscale16 = sb("unscale16", [2, P], F16)
        iota_e = sb("iota_e", [P, E])
        region_of = sb("region_of", [P, E])
        dst_of = [sb(f"dst_of{n}", [P, GT * TOPK]) for n in range(2)]
        multiples = sb("multiples", [1, E])
        step_no = sb("step_no", [1, STEPS])
        upto = sb("upto", [1, E, E])
        minus_half = sb("minus_half", [P, GT])
        eps4 = sb("eps4", [P, GT])
        pad_rows = sb("pad_rows", [P, HALVES, ROW_W])

        conv_hi = sb("conv_hi", [P, TAPS, CONV], F32R)
        conv_lo = sb("conv_lo", [P, TAPS, CONV], F32R)
        z_hi = sb("z_hi", [P, INNER], F32R)
        z_lo = sb("z_lo", [P, INNER], F32R)
        convb = sb("convb", [P, 4])
        convb_half = sb("convb_half", [P, 4])
        out_wn = sb("out_wn", [P, 2, D])
        normw = sb("normw", [P, 2])
        dcol = sb("dcol", [P, 2])
        d_diag = sb("d_diag", [P, 2, P])
        dtb = sb("dtb", [P, HEADS])
        alog = sb("alog", [P, HEADS])
        a_exp = sb("a_exp", [P, HEADS])
        wq_s = sb("wq_s", [P, D])
        wk_s = sb("wk_s", [P, D])
        wv_n = sb("wv_n", [P, D])
        bq_s = sb("bq_s", [P, 1])
        bk_s = sb("bk_s", [P, 1])
        bv_n = sb("bv_n", [P, D])
        keys_s = sb("keys_s", [P, E])
        rw_s = sb("rw_s", [P, E])
        rb_s = sb("rb_s", [P, E])
        keys_sq = sb("keys_sq", [P, E])
        route_w = sb("route_w", [P, E])
        route_b = sb("route_b", [P, E])
        w1_hi = sb("w1_hi", [P, E, NF, P], F16)
        w1_lo = sb("w1_lo", [P, E, NF, P], F16)
        w2_s = sb("w2_s", [P, E, NF, D])
        b1_s = sb("b1_s", [P, E, NF])
        b2_16 = sb("b2_16", [2, E, D], F16)

        ARENA = 11430
        arena = sb("arena", [P, ARENA])
        used = {"at": 0}

        def take(*shape):
            n = int(np.prod(shape))
            v = arena[:, used["at"]:used["at"] + n]
            used["at"] += n
            assert used["at"] <= ARENA, used["at"]
            if len(shape) == 2:
                v = v.rearrange("p (a b) -> p a b", b=shape[1])
            if len(shape) == 3:
                v = v.rearrange("p (a b c) -> p a b c", b=shape[1], c=shape[2])
            return v

        in_w = take(CONV + INNER + HEADS)
        conv_wb = take(TAPS, CONV)
        conv_f = take(TAPS, CONV)
        z_half = take(INNER)
        xT_all = take(SEQS, L)
        dtw = take(8, SEQS * HEADS)
        after_f = take(P)
        before_f = take(P)
        out_w = take(2, D)
        wv_s = take(D)
        bv_s = take(D)
        b2_lo = xT_all[0:1, E:E + E // 2, :].rearrange("p e d -> p (e d)").bitcast(F16)
        b2_stage = xT_all[0:1, 0:E, :].rearrange("p e d -> p (e d)")
        used["at"] = 0
        x_tok = [take(GT, D) for _ in range(2)]
        ctx_s = [take(GT, LC + 1) for _ in range(2)]
        th = [take(GTOK) for _ in range(2)]
        xbc = take(4, GTOK)
        z_gate = take(GT, INNER)
        xdt = take(GT, INNER)
        cb_masked = take(GT, L)
        decay = [take(HEADS, L) for _ in range(2)]
        gatedT = take(GT, 2, P)
        res1 = take(GT, D)
        x1 = [take(GT, D) for _ in range(2)]
        junk = take(INNER)
        kT_s = take(GT, LC)
        used["at"] = 0
        xg = [take(HALVES, ROW_W) for _ in range(ROWS_RING)]
        xgT = [take(STEP).bitcast(F16).rearrange("p (a b) -> p a b", a=2) for _ in range(2)]
        hid = [take(NF, STEP) for _ in range(2)]
        y_s = [take(HALVES, D) for _ in range(Y_RING)]
        over = take(E, E)[0:1, :, :]
        done = take(STEPS, E)[0:1, :, :]
        used["at"] = 0
        x2_back = [take(GT, D) for _ in range(2)]
        parts = [take(TOPK, GT * D) for _ in range(2)]
        total = [take(GT, D) for _ in range(2)]
        y_out = [take(GT, D) for _ in range(2)]

        dta = sb("dta", [P, 3, SEQS * HEADS])
        dta_g = [sb(f"dta_g{p}", [P, 3, GT * HEADS]) for p in range(2)]
        xT_g = [sb(f"xT_g{p}", [P, GT, L]) for p in range(2)]
        x_hi = [sb(f"x_hi{p}", [P, GT, PADT], F32R) for p in range(2)]
        x_lo = [sb(f"x_lo{p}", [P, GT, PADT], F32R) for p in range(2)]
        adt_hi = sb("adt_hi", [P, 2 * HEADS, L], F32R)
        adt_lo = sb("adt_lo", [P, 2 * HEADS, L], F32R)
        x1T_s = sb("x1T_s", [P, GTOK])
        qT_s = sb("qT_s", [P, GTOK])
        v_s = sb("v_s", [P, GT, D])
        prob = sb("prob", [P, GT, LC])
        probT = sb("probT", [P, GT, L])
        res2 = sb("res2", [P, GT, D])
        x2 = [sb(f"x2_{p}", [P, GT, D]) for p in range(2)]
        x2T_s = sb("x2T_s", [P, GTOK])
        rows = [sb(f"rows{p}", [P, GT, TOPK, ROW_W]) for p in range(2)]
        w1_stage = [sb(f"w1_stage{p}", [P, FF]) for p in range(2)]

        ss = sb("ss", [P, GT])
        stats = [sb(f"stats{n}", [P, GT, 6]) for n in range(3)]
        mv = [sb(f"mv{n}", [P, GT, 2]) for n in range(3)]
        var_e = [sb(f"var_e{n}", [P, GT]) for n in range(3)]
        rstd = [sb(f"rstd{n}", [P, GT]) for n in range(3)]
        neg_max = sb("neg_max", [P, GT])
        prob_sum = sb("prob_sum", [P, GT])
        prob_rsum = sb("prob_rsum", [P, GT])
        logit = sb("logit", [P, GT, E])
        top8 = sb("top8", [P, GT, 8])
        idx8 = sb("idx8", [P, GT, 8], U32)
        idx_f = sb("idx_f", [P, GT, TOPK])
        d4 = sb("d4", [P, GT, TOPK])
        e4 = sb("e4", [P, GT, TOPK])
        s4 = sb("s4", [P, GT])
        r4 = sb("r4", [P, GT])
        onehot = sb("onehot", [P, GT * TOPK, E])
        picked = sb("picked", [P, GT, E], BF16)
        group_n = sb("group_n", [P, E])
        carry16 = [sb(f"carry16_{n}", [P, E], BF16) for n in range(2)]
        slot = sb("slot", [P, GT, E])
        pos_f = sb("pos_f", [P, GT * TOPK])
        pos = [sb(f"pos{p}", [P, GT * TOPK], U32) for p in range(2)]

        cnt = sb("cnt", [1, E])
        n_steps = sb("n_steps", [1, E])
        last_step = sb("last_step", [1, E])
        step_ef = sb("step_ef", [1, STEPS])
        steps_before = sb("steps_before", [1, STEPS])
        row_f = sb("row_f", [1, STEPS])
        step_row = sb("step_row", [1, STEPS], I32)
        step_e = sb("step_e", [1, STEPS], I32)
        pad_f = sb("pad_f", [1, E])
        pad_at = sb("pad_at", [1, E], I32)

        banks = [bank(f"bank{n}") for n in range(8)]
        turn_ps = [banks[p][:, 0:STEP].bitcast(F16).rearrange("p (a b) -> p a b", a=2) for p in range(2)]
        front, segs, mids = banks[0:2], banks[2:4], banks[4:6]
        late = banks[6:8]

        block = ctx.enter_context(nc.Block())

        SCHEDULE = (
            ("load_x", -1), ("load_ctx", 0), ("load_w1", 1),
            ("conv0", 0), ("gate_T", 1), ("conv1", 0), ("silu0", 0), ("gate_T_out", 1), ("norm1", 2), ("xbc0", 0),
            ("mixed", 1), ("x2_T", 2), ("silu1", 0), ("x2_T_out", 2), ("dt", 0), ("xbc1", 0), ("res1", 1),
            ("conv2", 0), ("silu2", 0), ("row_high", 2), ("xbc2", 0),
            ("logits", 2), ("conv3", 0), ("norm0", 1), ("top", 2), ("silu3", 0),
            ("k", 1), ("z0", 0), ("k_out", 1), ("xbc3", 0), ("z_tanh0", 0), ("z_gate0", 0), ("chosen", 2),
            ("v", 1), ("z1", 0), ("z_tanh1", 0), ("z_gate1", 0), ("top_exp", 2), ("v_out", 1),
            ("ranks", 2), ("turn_x", 0), ("seg0", 0), ("decay0", 0), ("xdt", 0), ("weight", 2),
            ("seg1", 0), ("decay1", 0), ("x1_T", 1), ("x1_T_out", 1), ("cb", 0), ("cb_masked", 0), ("slots", 2),
            ("q", 1), ("q_out", 1), ("mix0", 0), ("y0", 0), ("seg2", 0), ("mix1", 0), ("y1", 0), ("decay2", 0),
            ("scores", 1), ("seg3", 0), ("decay3", 0), ("neg_max", 1), ("gate0", 0), ("softmax", 1),
            ("mix2", 0), ("y2", 0), ("mix3", 0), ("prob_T", 1), ("prob_T_out", 1), ("y3", 0), ("gate1", 0),
            ("sumsq", 0), ("attended", 1), ("w1_high", 2), ("w1_low", 2), ("res2", 1), ("split_x", -1))
        POOL_SCHEDULE = (
            ("norm_y", 1), ("norm_b", 2), ("adt0", 0), ("send2", 3), ("norm_a", 1), ("send3", 3),
            ("adt1", 0), ("send0", 2), ("split_x", -1), ("send1", 2))
        FIRST_LOOPED = 3

        def group_loop(eng, parts_of, schedule=SCHEDULE):
            def iteration(g, p):
                for part, lag in schedule:
                    if part not in parts_of or isinstance(g, int) and not 0 <= g - lag < GROUPS:
                        continue
                    parts_of[part](g - lag, (p - lag) % 2)

            for g in range(-1, FIRST_LOOPED):
                iteration(g, g % 2)
            with eng.Fori(FIRST_LOOPED // 2, (GROUPS - 1) // 2) as i:
                iteration(2 * i + 1, 1)
                iteration(2 * i + 2, 0)
            for g in range(GROUPS - 1, GROUPS + 3):
                iteration(g, g % 2)

        @block.sync
        def _(sp):
            for q in range(4):
                n = SEQS // 4
                sp.dma_start(xT_all[:, n * q:n * q + n, :],
                             xT[:, n * L * q:n * L * (q + 1)].rearrange("d (s l) -> d s l", l=L)
                             ).then_inc(sem("xT_loaded"), 16)

            def load_x(g, p):
                wait(sp, "x_lo", g - 1)
                sp.dma_start(xT_g[p][:, :, :], xT3[:, bass.ds(GT * g, GT), :]).then_inc(sem(f"xT_loaded{p}"), 16)
                wait(sp, "res1", GT * (g - 1))
                sp.dma_start(x_tok[p], x[bass.ds(GT * g, GT), :, :].rearrange("s l d -> l s d")
                             ).then_inc(sem(f"x_loaded{p}"), 16)

            def load_ctx(g, p):
                wait(sp, "v_proj", g - 1)
                wait(sp, "k_proj", g - 1)
                sp.dma_start(ctx_s[p][:, :, 0:LC],
                             ctxT[:, bass.ds(GT * g, GT), :]).then_inc(sem(f"ctx_loaded{p}"), 16)

            def load_w1(c, p):
                for n in range(2):
                    wait(sp, "w1_low", 2 * c + n - 1)
                    sp.dma_start(w1_stage[n][:, :], w1T[:, bass.ds(2 * c + n, 1), :].rearrange("d e f -> d (e f)")
                                 ).then_inc(sem(f"w1_loaded{n}"), 16)

            sp.wait_ge(sem("dt_proj"), 1)
            sp.dma_start(b2_stage, b2).then_inc(sem("b2_loaded"), 16)
            xT3 = xT.rearrange("d (s l) -> d s l", l=L)
            sp.wait_ge(sem("conv_low"), 1)
            sp.wait_ge(sem("z_low"), 1)
            sp.wait_ge(sem("dt_split"), 3)
            sp.wait_ge(sem("b2_low"), 1)
            sp.dma_start(b2_16[1:2, :, :].rearrange("p e d -> p (e d)"), b2_lo).then_inc(sem("b2_split"), 16)
            sp.wait_ge(sem("b2_split"), 16)
            sp.wait_ge(sem("masks"), 2)
            sp.wait_ge(sem("scaled"), N_SCALED)
            group_loop(sp, {"load_x": load_x, "load_w1": load_w1, "load_ctx": load_ctx})

            sp.wait_ge(sem("plan"), N_PLAN)
            for p in range(2):
                sp.wait_ge(sem(f"rows_sent{p}"), 16 * GT * TOPK * GROUPS // 2 + 16)
            with sp.Fori(0, E) as e:
                at = sp.value_load(pad_at[0:1, bass.ds(e, 1)], min_val=0, max_val=E * REGION - STEP)
                sp.dma_start(rows_dram[bass.ds(at, STEP), :].rearrange("(i p) w -> p i w", p=P),
                             pad_rows[:, :, :]).then_inc(sem("padded"), 16)
            sp.wait_ge(sem("padded"), 16 * E)

            def load_rows(j, b):
                at = sp.value_load(step_row[0:1, bass.ds(j, 1)], min_val=0, max_val=E * REGION)
                sp.dma_start(xg[b], rows_dram[bass.ds(at, STEP), :].rearrange("(i p) w -> p i w", p=P)
                             ).then_inc(sem(f"xg_loaded{b}"), 16)

            for b in range(ROWS_RING):
                load_rows(b, b)
            with sp.Fori(1, STEPS // ROWS_RING) as i:
                for b in range(ROWS_RING):
                    sp.wait_ge(sem(f"parts_sent{b % Y_RING}"), 32 * (ROWS_RING // Y_RING * (i - 1) + b // Y_RING + 1))
                    load_rows(ROWS_RING * i + b, b)

            for q in range(Y_RING):
                sp.wait_ge(sem(f"parts_sent{q}"), 32 * (STEPS // Y_RING))
            for p in range(2):
                sp.wait_ge(sem(f"x2_stored{p}"), 16 * (GROUPS // 2))
            parts_v = parts_dram.rearrange("(k n p) d -> p k n d", k=TOPK, p=P)

            def load_parts(i):
                for p in range(2):
                    wait(sp, f"normed{p}", i)
                    sp.dma_start(x2_back[p], x2_dram[bass.ds(GT * (2 * i + p), GT), :, :].rearrange("s l d -> l s d")
                                 ).then_inc(sem(f"parts_loaded{p}"), 16)
                    for k in range(TOPK):
                        sp.dma_start(parts[p][:, k, :].rearrange("p (t d) -> p t d", d=D),
                                     parts_v[:, k, bass.ds(GT * (2 * i + p), GT), :]
                                     ).then_inc(sem(f"parts_loaded{p}"), 16)

            load_parts(0)
            with sp.Fori(1, GROUPS // 2) as i:
                load_parts(i)
            for p in range(2):
                sp.wait_ge(sem(f"stored{p}"), 16 * (GROUPS // 2))

        @block.gpsimd
        def _(pool):
            pool.memset(ident[:, :], 0.0).then_inc(sem("const0"), 1)
            pool.memset(ident16[:, :], 0.0).then_inc(sem("const0"), 1)
            pool.memset(ones[:, :], 1.0).then_inc(sem("const0"), 1)
            pool.memset(pad_rows[:, :, :], 0.0).then_inc(sem("const0"), 1)
            pool.memset(upto[:, :, :], 1.0).then_inc(sem("const0"), 1)
            c = sem("constants")
            pool.memset(ones16[:, :], 1.0).then_inc(c, 1)
            pool.memset(unscale16[:, :], 1.0 / W_SCALE).then_inc(c, 1)
            pool.memset(minus_half[:, :], -0.5).then_inc(c, 1)
            pool.memset(eps4[:, :], EPS).then_inc(c, 1)
            pool.memset(carry16[1][:, :], 0.0).then_inc(c, 1)
            for p in range(2):
                pool.memset(x_hi[p][:, :, :].bitcast(F32), 0.0).then_inc(c, 1)
                pool.memset(x_lo[p][:, :, :].bitcast(F32), 0.0).then_inc(c, 1)
            pool.iota(iota_e[:, :], [[1, E]], base=0, channel_multiplier=0,
                      allow_small_or_imprecise_dtypes=True).then_inc(c, 1)
            pool.iota(region_of[:, :], [[REGION, E]], base=0, channel_multiplier=0,
                      allow_small_or_imprecise_dtypes=True).then_inc(c, 1)
            pool.iota(dst_of[0][:, :], [[L, GT], [TOKENS, TOPK]], base=0, channel_multiplier=1,
                      allow_small_or_imprecise_dtypes=True).then_inc(c, 1)
            pool.iota(multiples[:, :], [[STEP, E]], base=0, channel_multiplier=0,
                      allow_small_or_imprecise_dtypes=True).then_inc(c, 1)
            pool.iota(step_no[:, :], [[1, STEPS]], base=0, channel_multiplier=0,
                      allow_small_or_imprecise_dtypes=True).then_inc(c, 1)
            pool.wait_ge(sem("const0"), 5)
            for m in (ident, ident16):
                pool.affine_select(out=m[:, :], in_=m[:, :], compare_op=ALU.not_equal, fill=1.0, base=0,
                                   pattern=[[-1, P]], channel_multiplier=1).then_inc(c, 1)
            pool.affine_select(out=causal[:, :], in_=ones[:, :], compare_op=ALU.is_ge, fill=0.0, base=0,
                               pattern=[[1, P]], channel_multiplier=-1).then_inc(c, 1)
            pool.affine_select(out=after_f, in_=ones[:, :], compare_op=ALU.is_gt, fill=0.0, base=0,
                               pattern=[[-1, P]], channel_multiplier=1).then_inc(c, 1)
            pool.affine_select(out=before_f, in_=ones[:, :], compare_op=ALU.is_gt, fill=0.0, base=0,
                               pattern=[[1, P]], channel_multiplier=-1).then_inc(c, 1)
            pool.affine_select(out=upto[:, :, :], in_=upto[:, :, :], compare_op=ALU.is_ge, fill=0.0, base=0,
                               pattern=[[1, E], [-1, E]], channel_multiplier=0).then_inc(c, 1)
            pool.iota(pad_rows[:, :, DST_COL:DST_COL + 1].bitcast(I32), [[0, HALVES]], base=SKIP_DST,
                      channel_multiplier=0).then_inc(c, 1)

            def gate():
                pool.sem_inc(sem("pool_gate"), 1)

            def split_x(g, p):
                wait(pool, "x_hi", g + 1)
                wait(pool, "z_proj", 2 * (g - 1))
                pool.tensor_tensor(x_lo[p][:, :, OFF:OFF + L], xT_g[p][:, :, :],
                                   x_hi[p][:, :, OFF:OFF + L].bitcast(F32), ALU.subtract
                                   ).then_inc(sem("x_lo"), 1)

            def spread_adt(g, p, h):
                wait(pool, "dta_g", g + 1)
                wait(pool, "seg", GT * g + 2 * h)
                gate()
                for n, dst in ((1, adt_hi), (2, adt_lo)):
                    col = dta_g[p][:, n, 2 * HEADS * h:2 * HEADS * (h + 1)]
                    pool.affine_select(out=dst[:, :, :], in_=col.unsqueeze(2).to_broadcast([P, 2 * HEADS, L]),
                                       compare_op=ALU.is_ge, fill=0.0, base=0,
                                       pattern=[[0, 2 * HEADS], [1, L]], channel_multiplier=-1
                                       ).then_inc(sem("adt"), 1)

            def inv_sqrt(n, src, name_in, count, name_out, done_count):
                wait(pool, name_in, count)
                pool.tensor_tensor(var_e[n][:, :], src, eps4[:, :], ALU.add).then_inc(sem(name_out + "_e"), 1)
                wait(pool, name_out + "_e", done_count)
                pool.tensor_tensor(rstd[n][:, :], var_e[n][:, :], minus_half[:, :], ALU.pow).then_inc(sem(name_out), 1)

            pool.wait_ge(c, N_CONST)
            for p in range(HALVES):
                pool.dma_start(rows_dram[E * REGION + p * P:E * REGION + (p + 1) * P, :], pad_rows[:, p, :]
                               ).then_inc(sem(f"rows_sent{p}"), 16)

            def norm_y(g, p):
                inv_sqrt(2, ss[:, :], "sumsq", GT * (g + 1), "rms", g + 1)

            def norm_a(g, p):
                inv_sqrt(0, mv[0][:, :, 1], "mv0", g + 1, "rstd0", g + 1)

            def norm_b(b, p):
                inv_sqrt(1, mv[1][:, :, 1], "mv1", b + 1, "rstd1", b + 1)

            def send_rows(c_, p, t):
                wait(pool, "pos", c_ + 1)
                wait(pool, "row_copies", c_ + 1)
                wait(pool, "row_w", c_ + 1)
                wait(pool, "row_dst", c_ + 1)
                gate()
                for k in range(TOPK):
                    n = TOPK * t + k
                    pool.indirect_dma_start(rows_dram, bass.IndirectOffsetOnAxis(ap=pos[p][:, n:n + 1], axis=0),
                                            rows[p][:, t, k, :], None).then_inc(sem(f"rows_sent{p}"), 16)

            def rows_of(t):
                return lambda c_, p: send_rows(c_, p, t)

            group_loop(pool, {"split_x": split_x, "adt0": lambda g, p: spread_adt(g, p, 0),
                              "adt1": lambda g, p: spread_adt(g, p, 1), "norm_y": norm_y, "norm_a": norm_a,
                              "norm_b": norm_b} | {f"send{t}": rows_of(t) for t in range(GT)}, POOL_SCHEDULE)

            limit = pool.to_reg(TOPK * TOKENS - 1)

            def send_parts(j, b):
                pool.wait_ge(sem("y_scaled"), HALVES * (j + 1))
                gate()
                for i in range(HALVES):
                    dst = xg[b][:, i, DST_COL:DST_COL + 1].bitcast(U32)
                    pool.indirect_dma_start(parts_dram, bass.IndirectOffsetOnAxis(ap=dst, axis=0),
                                            y_s[b % Y_RING][:, i, :], None, bounds_check=limit, oob_is_err=False
                                            ).then_inc(sem(f"parts_sent{b % Y_RING}"), 16)

            with pool.Fori(0, STEPS // ROWS_RING) as i:
                for b in range(ROWS_RING):
                    send_parts(ROWS_RING * i + b, b)

            with pool.Fori(0, GROUPS // 2) as i:
                for p in range(2):
                    f = 2 * i + p
                    inv_sqrt(2, mv[2][:, :, 1], "mv2", f + 1, "rstd2", f + 1)

        @block.scalar
        def _(act):
            def load(dst, src, name="weights"):
                act.dma_start(dst, src).then_inc(sem(name), 16)

            load(in_w, in_wT)
            load(conv_wb.rearrange("p j c -> p (j c)"), conv_w.partition_broadcast(P))
            load(dtb[:, :], dt_bias.partition_broadcast(P))
            load(alog[:, :], a_log.partition_broadcast(P))
            load(convb[:, :], conv_b)
            load(out_w, out_wT)
            load(normw[:, :], norm_w)
            for h in range(HEADS):
                load(dcol[HD * (h % 2):HD * (h % 2) + HD, h // 2:h // 2 + 1],
                     d_param[h:h + 1].partition_broadcast(HD))
            load(wq_s[:, :], wq)
            load(wk_s[:, :], wk)
            load(wv_s, wv)
            load(bq_s[:, :], bq)
            load(bk_s[:, :], bk)
            load(bv_s, bv.partition_broadcast(P))
            load(keys_s[:, :], keysT)
            load(rw_s[:, :], rwT)
            load(rb_s[:, :], rb.partition_broadcast(P))
            load(b1_s[:, :, :], b1T)
            for q in range(4):
                load(w2_s[:, 4 * q:4 * q + 4, :, :], w2T[:, 4 * q:4 * q + 4, :, :], "w2_loaded")

            act.wait_ge(sem("dt_negabs"), 1)
            act.activation(dtw[:, 2, :], dtw[:, 1, :], ACT.Exp).then_inc(sem("dt_exp"), 1)
            act.activation(a_exp[:, :], alog[:, :], ACT.Exp).then_inc(sem("a_exp"), 1)
            act.wait_ge(sem("dt_onep"), 1)
            act.activation(dtw[:, 4, :], dtw[:, 3, :], ACT.Ln).then_inc(sem("dt_ln"), 1)
            act.wait_ge(sem("conv_full"), 1)
            act.activation(conv_hi[:, :, :], conv_f, ACT.Copy).then_inc(sem("conv_high"), 1)
            act.wait_ge(sem("z_full"), 1)
            act.activation(z_hi[:, :], z_half, ACT.Copy).then_inc(sem("z_high"), 1)

            act.wait_ge(sem("constants"), N_CONST)

            def split_x(g, p):
                wait_load(act, f"xT_loaded{p}", g, p)
                wait(act, "z_proj", 2 * (g - 1))
                wait(act, "x_lo", g - 1)
                act.activation(x_hi[p][:, :, OFF:OFF + L], xT_g[p][:, :, :], ACT.Copy).then_inc(sem("x_hi"), 1)

            def silu(c):
                def run(g, p):
                    if c == 0:
                        wait(act, "y", GT * g)
                    wait(act, "conv", 4 * g + c + 1)
                    act.activation(xbc[:, c, :], front[c % 2][:, :], ACT.Identity, bias=convb_half[:, c:c + 1]
                                   ).then_inc(sem("conv_val"), 1)
                    wait(act, "xbc", 4 * g + c - 1)
                    act.activation(th[c % 2], front[c % 2][:, :], ACT.Tanh, bias=convb_half[:, c:c + 1]
                                   ).then_inc(sem("conv_tanh"), 1)
                return run

            def z_tanh(h):
                def run(g, p):
                    wait(act, "gatedT_ps", 2 * g)
                    wait(act, "sumsq", GT * g)
                    wait(act, "z_proj", 2 * g + h + 1)
                    act.activation(z_gate[:, 2 * h:2 * h + 2, :],
                                   front[h][:, :].rearrange("p (t n) -> p t n", t=2), ACT.Tanh
                                   ).then_inc(sem("z_tanh"), 1)
                return run

            def decays(t):
                def run(g, p):
                    wait(act, "seg", GT * g + t + 1)
                    wait(act, "y", GT * g + t - 1)
                    act.activation(decay[t % 2], segs[t % 2][:, :].rearrange("p (h l) -> p h l", h=HEADS),
                                   ACT.Exp).then_inc(sem("decay"), 1)
                return run

            def sum_squares(g, p):
                wait(act, "rms", g)
                for t in range(GT):
                    wait(act, "gated", 2 * g + t // 2 + 1)
                    wait(act, "sumsq", GT * g + t)
                    act.activation(junk, z_gate[:, t, :], ACT.Square, scale=INNER ** -0.5,
                                   accum_out=ss[:, t:t + 1]).then_inc(sem("sumsq"), 1)

            def gate_T(g, p):
                wait(act, "mixed", g)
                for h in range(2):
                    wait(act, "gatedT_ps", 2 * g + h + 1)
                    act.activation(gatedT[:, 2 * h:2 * h + 2, :, :],
                                   mids[1 - h][:, :].rearrange("p (t c l) -> p t c l", t=2, c=2), ACT.Copy
                                   ).then_inc(sem("gatedT"), 1)

            def k_out(b, p):
                wait(act, "k_proj", b + 1)
                wait(act, "scores", b)
                act.activation(kT_s, late[1][:, 0:GT * LC].rearrange("p (t l) -> p t l", t=GT),
                               ACT.Identity, bias=bk_s[:, 0:1]).then_inc(sem("kT"), 1)

            def x1_T(b, p):
                wait(act, "x1T_ps", b + 1)
                wait(act, "q_proj", b)
                act.activation(x1T_s[:, :], late[0][:, :], ACT.Copy).then_inc(sem("x1T"), 1)

            def q_out(b, p):
                wait(act, "q_proj", b + 1)
                wait(act, "scores", b)
                act.activation(qT_s[:, :], late[1][:, :], ACT.Identity, bias=bq_s[:, 0:1]).then_inc(sem("qT"), 1)

            def softmax(b, p):
                wait(act, "neg_max", b + 1)
                wait(act, "probT_ps", b)
                wait(act, "prob_rsum", b)
                for t in range(GT):
                    act.activation(prob[:, t, :], late[0][:, t * LC:(t + 1) * LC], ACT.Exp,
                                   bias=neg_max[:, t:t + 1], accum_out=prob_sum[:, t:t + 1]
                                   ).then_inc(sem("prob"), 1)

            def prob_T(b, p):
                wait(act, "probT_ps", b + 1)
                wait(act, "attended", b)
                act.activation(probT[0:LC, :, :], late[1][0:LC, :].rearrange("p (t l) -> p t l", t=GT),
                               ACT.Copy).then_inc(sem("probT"), 1)

            def x2_T(c, p):
                wait(act, "x2T_ps", c + 1)
                wait(act, "logits", c)
                act.activation(x2T_s[:, :], late[0][:, :], ACT.Copy).then_inc(sem("x2T"), 1)

            def row_high(c, p):
                wait(act, "x2", c + 1)
                act.wait_ge(sem(f"rows_sent{p}"), 8 * GT * TOPK * (c - p) + 16)
                act.activation(rows[p][:, :, 0, 0:D // 2].bitcast(F16), x2[p][:, :, :], ACT.Copy
                               ).then_inc(sem("row_high"), 1)
                act.dma_start(x2_dram[bass.ds(GT * c, GT), :, :].rearrange("s l d -> l s d"), x2[p][:, :, :]
                              ).then_inc(sem(f"x2_stored{p}"), 16)

            def w1_high(c, p):
                for n in range(2):
                    wait_load(act, f"w1_loaded{n}", c, None)
                    act.activation(w1_hi[:, bass.ds(2 * c + n, 1), :, :].rearrange("p e f m -> p (e f m)"),
                                   w1_stage[n][:, :], ACT.Copy, scale=W_SCALE).then_inc(sem("w1_high"), 1)

            def top_exp(c, p):
                wait(act, "top_diff", c + 1)
                wait(act, "row_w", c)
                act.activation(e4[:, :, :], d4[:, :, :], ACT.Exp).then_inc(sem("top_exp"), 1)
                wait(act, "row_low", c + 1)
                act.activation(rows[p][:, :, 1:TOPK, 0:D],
                               rows[p][:, :, 0:1, 0:D].to_broadcast([P, GT, TOPK - 1, D]), ACT.Copy
                               ).then_inc(sem("row_copies"), 1)

            group_loop(act, {"split_x": split_x, "gate_T_out": gate_T, "x2_T_out": x2_T, "row_high": row_high,
                             "k_out": k_out, "top_exp": top_exp, "x1_T_out": x1_T, "q_out": q_out,
                             "softmax": softmax, "prob_T_out": prob_T, "sumsq": sum_squares, "w1_high": w1_high}
                       | {f"silu{c}": silu(c) for c in range(4)} | {f"z_tanh{h}": z_tanh(h) for h in range(2)}
                       | {f"decay{t}": decays(t) for t in range(GT)})

            def gelus(j, p, b):
                ex = act.value_load(step_e[0:1, bass.ds(j, 1)], min_val=0, max_val=E - 1)
                wait(act, "down", j - 1)
                for f in range(NF):
                    act.wait_ge(sem("up"), 2 * j + f // 2 + 1)
                    hb = banks[2 + 2 * p + f // 2]
                    act.activation(hid[p][:, f, :], hb[:, (f % 2) * STEP:(f % 2 + 1) * STEP], ACT.Gelu,
                                   bias=b1_s[:, bass.ds(ex, 1), f:f + 1].rearrange("p e f -> p (e f)"),
                                   scale=1.0 / W_SCALE).then_inc(sem("hidden"), 1)

            act.wait_ge(sem("plan"), N_PLAN)
            for j in range(2):
                gelus(j, j, 0)
            with act.Fori(1, STEPS // 2) as i:
                for p in range(2):
                    gelus(2 * i + p, p, 0)

            with act.Fori(0, GROUPS // 2) as i:
                for p in range(2):
                    act.wait_ge(sem(f"normed{p}"), i + 1)
                    act.dma_start(out[bass.ds(GT * (2 * i + p), GT), :, :].rearrange("s l d -> l s d"), y_out[p]
                                  ).then_inc(sem(f"stored{p}"), 16)

        @block.vector
        def _(dve):
            v = nc.vector
            dve.wait_ge(sem("weights"), 16 * N_WEIGHTS)
            dve.wait_ge(sem("constants"), N_CONST)
            dve.wait_ge(sem("dt_proj"), 1)
            dtv = banks[0][:, 0:SEQS * HEADS].rearrange("p (s h) -> p s h", h=HEADS)
            dt3 = dtw.rearrange("p n (s h) -> p n s h", h=HEADS)
            v.tensor_tensor(dt3[:, 0, :, :], dtv, dtb[:, :].unsqueeze(1).to_broadcast([P, SEQS, HEADS]), ALU.add
                            ).then_inc(sem("dt_u"), 1)
            v.tensor_copy(after[:, :], after_f).then_inc(sem("masks"), 1)
            v.tensor_copy(before16[:, :], before_f).then_inc(sem("masks"), 1)
            dve.wait_ge(sem("dt_u"), 1)
            v.scalar_tensor_tensor(dtw[:, 1, :], dtw[:, 0, :], -1.0, dtw[:, 0, :], ALU.mult, ALU.min
                                   ).then_inc(sem("dt_negabs"), 1)
            v.scalar_tensor_tensor(conv_f, conv_wb, 0.5, in_w[:, INNER:INNER + CONV].unsqueeze(1).to_broadcast(
                [P, TAPS, CONV]), ALU.mult, ALU.mult).then_inc(sem("conv_full"), 1)
            dve.wait_ge(sem("dt_exp"), 1)
            v.tensor_scalar(dtw[:, 3, :], dtw[:, 2, :], 1.0, None, ALU.add).then_inc(sem("dt_onep"), 1)
            v.tensor_scalar(z_half, in_w[:, 0:INNER], 0.5, None, ALU.mult).then_inc(sem("z_full"), 1)
            dve.wait_ge(sem("dt_onep"), 1)
            v.tensor_scalar(dtw[:, 5, :], dtw[:, 3, :], -1.0, None, ALU.add).then_inc(sem("dt_log"), 1)
            dve.wait_ge(sem("dt_log"), 1)
            v.scalar_tensor_tensor(dtw[:, 6, :], dtw[:, 5, :], 0.0, dtw[:, 2, :], ALU.is_equal, ALU.mult
                                   ).then_inc(sem("dt_log"), 1)
            v.tensor_scalar(dtw[:, 7, :], dtw[:, 5, :], 1e-30, None, ALU.max).then_inc(sem("dt_log"), 1)
            dve.wait_ge(sem("dt_log"), 3)
            v.reciprocal(dtw[:, 5, :], dtw[:, 7, :]).then_inc(sem("dt_log"), 1)
            dve.wait_ge(sem("dt_log"), 4)
            v.tensor_tensor(dtw[:, 7, :], dtw[:, 5, :], dtw[:, 2, :], ALU.mult).then_inc(sem("dt_log"), 1)
            dve.wait_ge(sem("dt_log"), 5)
            dve.wait_ge(sem("dt_ln"), 1)
            v.tensor_tensor(dtw[:, 5, :], dtw[:, 7, :], dtw[:, 4, :], ALU.mult).then_inc(sem("dt_log"), 1)
            dve.wait_ge(sem("dt_log"), 6)
            v.tensor_tensor(dtw[:, 7, :], dtw[:, 5, :], dtw[:, 6, :], ALU.add).then_inc(sem("dt_log"), 1)
            dve.wait_ge(sem("dt_log"), 7)
            v.scalar_tensor_tensor(dta[:, 0, :], dtw[:, 0, :], 0.0, dtw[:, 7, :], ALU.max, ALU.add
                                   ).then_inc(sem("dt_split"), 1)
            dve.wait_ge(sem("dt_split"), 1)
            dve.wait_ge(sem("a_exp"), 1)
            v.scalar_tensor_tensor(dt3[:, 1, :, :], dta[:, 0, :].rearrange("p (s h) -> p s h", h=HEADS), -1.0,
                                   a_exp[:, :].unsqueeze(1).to_broadcast([P, SEQS, HEADS]), ALU.mult, ALU.mult
                                   ).then_inc(sem("adt_full"), 1)
            dve.wait_ge(sem("adt_full"), 1)
            v.tensor_copy(dta[:, 1, :].bitcast(F32R), dtw[:, 1, :]).then_inc(sem("dt_split"), 1)
            dve.wait_ge(sem("dt_split"), 2)
            v.tensor_tensor(dta[:, 2, :].bitcast(F32R), dtw[:, 1, :], dta[:, 1, :], ALU.subtract
                            ).then_inc(sem("dt_split"), 1)
            dve.wait_ge(sem("conv_high"), 1)
            v.tensor_tensor(conv_lo[:, :, :], conv_f, conv_hi[:, :, :].bitcast(F32), ALU.subtract
                            ).then_inc(sem("conv_low"), 1)
            dve.wait_ge(sem("z_high"), 1)
            v.tensor_tensor(z_lo[:, :], z_half, z_hi[:, :].bitcast(F32), ALU.subtract).then_inc(sem("z_low"), 1)
            s = sem("scaled")
            v.tensor_scalar(convb_half[:, :], convb[:, :], 0.5, None, ALU.mult).then_inc(s, 1)
            for c in range(2):
                v.tensor_scalar(out_wn[:, c, :], out_w[:, c, :], normw[:, c:c + 1], None, ALU.mult).then_inc(s, 1)
                v.tensor_scalar(d_diag[:, c, :], ident[:, :], dcol[:, c:c + 1], None, ALU.mult).then_inc(s, 1)
            v.tensor_scalar(wv_n[:, :], wv_s, NORM_FACT, None, ALU.mult).then_inc(s, 1)
            v.tensor_scalar(bv_n[:, :], bv_s, NORM_FACT, None, ALU.mult).then_inc(s, 1)
            v.scalar_tensor_tensor(route_w[:, :], keys_s[:, :], 2.0, rw_s[:, :], ALU.mult, ALU.add).then_inc(s, 1)
            v.tensor_tensor(keys_sq[:, :], keys_s[:, :], keys_s[:, :], ALU.mult).then_inc(sem("keys_sq"), 1)
            dve.wait_ge(sem("keys_norm"), 1)
            v.tensor_tensor(route_b[:, :], rb_s[:, :], banks[1][:, 0:E], ALU.subtract).then_inc(s, 1)
            dve.wait_ge(sem("dt_split"), 3)
            dve.wait_ge(sem("b2_loaded"), 16)
            b2_hi = b2_16[0:1, :, :].rearrange("p e d -> p (e d)")
            v.tensor_scalar(b2_hi, b2_stage, W_SCALE, None, ALU.mult).then_inc(sem("b2_high"), 1)
            dve.wait_ge(sem("b2_high"), 1)
            v.scalar_tensor_tensor(b2_lo, b2_stage, W_SCALE, b2_hi, ALU.mult, ALU.subtract).then_inc(sem("b2_low"), 1)

            def group_dt(g, p):
                wait(dve, "adt", 4 * (g - 1))
                v.tensor_copy(dta_g[p][:, :, :], dta[:, :, bass.ds(GT * HEADS * g, GT * HEADS)]
                              ).then_inc(sem("dta_g"), 1)

            def silu(c):
                def run(g, p):
                    wait(dve, "conv_tanh", 4 * g + c + 1)
                    v.scalar_tensor_tensor(xbc[:, c, :], th[c % 2], 1.0, xbc[:, c, :], ALU.add, ALU.mult
                                           ).then_inc(sem("xbc"), 1)
                return run

            def z_gates(h):
                def run(g, p):
                    wait(dve, "z_tanh", 2 * g + h + 1)
                    zz = z_gate[:, 2 * h:2 * h + 2, :].rearrange("p t n -> p (t n)")
                    v.scalar_tensor_tensor(zz, zz, 1.0, front[h][:, :], ALU.add, ALU.mult
                                           ).then_inc(sem("z_gate"), 1)
                return run

            def times_dt(g, p):
                wait(dve, "dta_g", g + 1)
                wait(dve, "y", GT * g)
                for h in range(2):
                    wait(dve, "x_turned", 2 * g + h + 1)
                    dtc = dta_g[p][:, 0, 2 * HEADS * h:2 * HEADS * (h + 1)]
                    v.tensor_tensor(xdt[:, 2 * h:2 * h + 2, :].rearrange("p t (h n) -> p (t h) n", n=HD),
                                    front[h][:, :].rearrange("p (a n) -> p a n", n=HD),
                                    dtc.unsqueeze(2).to_broadcast([P, 2 * HEADS, HD]), ALU.mult
                                    ).then_inc(sem("xdt"), 1)

            def mask_cb(g, p):
                wait(dve, "cb", g + 1)
                v.tensor_tensor(cb_masked, mids[0][:, :].rearrange("p (t l) -> p t l", t=GT),
                                causal[:, :].unsqueeze(1).to_broadcast([P, GT, L]), ALU.mult
                                ).then_inc(sem("cb_masked"), 1)

            def mix(t):
                def run(g, p):
                    wait(dve, "cb_masked", g + 1)
                    wait(dve, "decay", GT * g + t + 1)
                    v.tensor_tensor(decay[t % 2], decay[t % 2],
                                    cb_masked[:, t:t + 1, :].to_broadcast([P, HEADS, L]), ALU.mult
                                    ).then_inc(sem("mix"), 1)
                return run

            def gates(h):
                def run(g, p):
                    wait(dve, "y", GT * g + 2 * h + 2)
                    wait(dve, "z_gate", 2 * g + h + 1)
                    zz = z_gate[:, 2 * h:2 * h + 2, :].rearrange("p t n -> p (t n)")
                    v.tensor_tensor(zz, mids[1 - h][:, :], zz, ALU.mult).then_inc(sem("gated"), 1)
                return run

            def moments(n, g, res, res_name):
                for t in range(GT):
                    wait(dve, res_name, GT * g + t + 1)
                    v.bn_stats(stats[n][:, t, :], res[:, t, :]).then_inc(sem(f"stats{n}"), 1)
                wait(dve, f"stats{n}", GT * (g + 1))
                wait(dve, f"rstd{n}_e", g)
                dve.sem_inc(sem("dve_gate"), 1)
                for t in range(GT):
                    ins = v.bn_aggr(mv[n][:, t, :], stats[n][:, t, :])
                ins.then_inc(sem(f"mv{n}"), 1)

            def normalise(n, g, res, out_of, out_name):
                wait(dve, f"mv{n}", g + 1)
                wait(dve, f"rstd{n}", g + 1)
                for t in range(GT):
                    ins = v.tensor_scalar(out_of[:, t, :], res[:, t, :], mv[n][:, t, 0:1], rstd[n][:, t:t + 1],
                                          ALU.subtract, ALU.mult)
                ins.then_inc(sem(out_name), 1)

            def residual1(g, p):
                wait(dve, "mixed", g + 1)
                wait(dve, "rms", g + 1)
                wait_load(dve, f"x_loaded{p}", g, p)
                for t in range(GT):
                    v.scalar_tensor_tensor(res1[:, t, :], mids[1][:, t * D:(t + 1) * D], rstd[2][:, t:t + 1],
                                           x_tok[p][:, t, :], ALU.mult, ALU.add).then_inc(sem("res1"), 1)
                moments(0, g, res1, "res1")

            def norm0(g, p):
                wait(dve, "x1T_ps", g - 1)
                wait(dve, "res2", GT * (g - 1))
                normalise(0, g, res1, x1[p], "x1")

            def v_out(b, p):
                wait(dve, "v_proj", b + 1)
                wait(dve, "attended", b)
                v.tensor_tensor(v_s[0:LC, :, :], late[0][0:LC, :].rearrange("p (t d) -> p t d", t=GT),
                                bv_n[0:LC, :].unsqueeze(1).to_broadcast([LC, GT, D]), ALU.add
                                ).then_inc(sem("v"), 1)

            def row_max(b, p):
                wait(dve, "scores", b + 1)
                wait(dve, "prob", GT * b)
                v.tensor_reduce(neg_max[:, :], late[0][:, 0:GT * LC].rearrange("p (t l) -> p t l", t=GT),
                                AX_X, ALU.max, negate=True).then_inc(sem("neg_max"), 1)

            def residual2(b, p):
                wait(dve, "prob", GT * (b + 1))
                wait(dve, "res2", GT * b)
                v.reciprocal(prob_rsum[:, :], prob_sum[:, :]).then_inc(sem("prob_rsum"), 1)
                wait(dve, "attended", b + 1)
                wait(dve, "prob_rsum", b + 1)
                wait(dve, "x1", b + 1)
                for t in range(GT):
                    v.scalar_tensor_tensor(res2[:, t, :], late[0][:, t * D:(t + 1) * D], prob_rsum[:, t:t + 1],
                                           x1[p][:, t, :], ALU.mult, ALU.add).then_inc(sem("res2"), 1)
                moments(1, b, res2, "res2")

            def norm1(b, p):
                if not isinstance(b, int) or b >= 2:
                    dve.wait_ge(sem(f"x2_stored{p}"), 8 * (b - p))
                wait(dve, "x2T_ps", b - 1)
                wait(dve, "row_low", b - 1)
                wait(dve, "row_high", b - 1)
                normalise(1, b, res2, x2[p], "x2")

            def w1_low(c, p):
                for n in range(2):
                    wait(dve, "w1_high", 2 * c + n + 1)
                    hi = w1_hi[:, bass.ds(2 * c + n, 1), :, :].rearrange("p e f m -> p (e f m)")
                    lo = w1_lo[:, bass.ds(2 * c + n, 1), :, :].rearrange("p e f m -> p (e f m)")
                    v.scalar_tensor_tensor(lo, w1_stage[n][:, :], W_SCALE, hi, ALU.mult, ALU.subtract
                                           ).then_inc(sem("w1_low"), 1)

            def top_experts(c, p):
                wait(dve, "logits", c + 1)
                v.tensor_tensor(logit[:, :, :], late[1][:, 0:GT * E].rearrange("p (t e) -> p t e", t=GT),
                                route_b[:, :].unsqueeze(1).to_broadcast([P, GT, E]), ALU.add
                                ).then_inc(sem("logit"), 1)
                wait(dve, "row_high", c + 1)
                v.tensor_tensor(rows[p][:, :, 0, D // 2:D].bitcast(F16), x2[p][:, :, :],
                                rows[p][:, :, 0, 0:D // 2].bitcast(F16), ALU.subtract
                                ).then_inc(sem("row_low"), 1)
                wait(dve, "logit", c + 1)
                dve.sem_inc(sem("dve_gate"), 1)
                for t in range(GT):
                    ins = v.max(top8[:, t, :], logit[:, t, :])
                ins.then_inc(sem("top8"), 1)
                wait(dve, "top8", c + 1)
                dve.sem_inc(sem("dve_gate"), 1)
                for t in range(GT):
                    ins = v.max_index(idx8[:, t, :], top8[:, t, :], logit[:, t, :])
                ins.then_inc(sem("idx8"), 1)
                v.tensor_tensor(d4[:, :, :], top8[:, :, 0:TOPK], top8[:, :, 0:1].to_broadcast([P, GT, TOPK]),
                                ALU.subtract).then_inc(sem("top_diff"), 1)

            def chosen(c, p):
                wait(dve, "idx8", c + 1)
                v.tensor_copy(idx_f[:, :, :], idx8[:, :, 0:TOPK]).then_inc(sem("idx_f"), 1)
                wait(dve, "dst_next", c)
                v.tensor_scalar(rows[p][:, :, :, DST_COL].bitcast(U32),
                                dst_of[p][:, :].rearrange("p (t k) -> p t k", k=TOPK), 0.0, None, ALU.add
                                ).then_inc(sem("row_dst"), 1)
                v.tensor_scalar(dst_of[1 - p][:, :], dst_of[p][:, :], float(GTOK), None, ALU.add
                                ).then_inc(sem("dst_next"), 1)
                wait(dve, "idx_f", c + 1)
                v.tensor_tensor(onehot[:, :, :],
                                idx_f[:, :, :].rearrange("p t k -> p (t k)").unsqueeze(2).to_broadcast(
                                    [P, GT * TOPK, E]),
                                iota_e[:, :].unsqueeze(1).to_broadcast([P, GT * TOPK, E]), ALU.is_equal
                                ).then_inc(sem("onehot"), 1)
                wait(dve, "onehot", c + 1)
                wait(dve, "ranks", c)
                with nc.allow_low_precision(reason="zeros and ones"):
                    v.tensor_reduce(picked[:, :, :], onehot[:, :, :].rearrange("p (t k) e -> p t e k", t=GT),
                                    AX_X, ALU.add).then_inc(sem("picked"), 1)

            def weights(c, p):
                wait(dve, "top_exp", c + 1)
                v.tensor_reduce(s4[:, :], e4[:, :, :], AX_X, ALU.add).then_inc(sem("top_sum"), 1)
                wait(dve, "picked", c + 1)
                v.tensor_reduce(group_n[:, :], picked[:, :, :].rearrange("p t e -> p e t"), AX_X, ALU.add
                                ).then_inc(sem("group_n"), 1)
                wait(dve, "top_sum", c + 1)
                v.reciprocal(r4[:, :], s4[:, :]).then_inc(sem("top_recip"), 1)
                wait(dve, "group_n", c + 1)
                v.tensor_tensor(carry16[p][:, :], carry16[1 - p][:, :], group_n[:, :], ALU.add
                                ).then_inc(sem("carry"), 1)
                wait(dve, "top_recip", c + 1)
                v.tensor_tensor(rows[p][:, :, :, W_COL], e4[:, :, :],
                                r4[:, :].unsqueeze(2).to_broadcast([P, GT, TOPK]), ALU.mult
                                ).then_inc(sem("row_w"), 1)

            def slots(c, p):
                wait(dve, "ranks", c + 1)
                v.tensor_tensor(slot[:, :, :], late[1][:, 0:GT * E].rearrange("p (t e) -> p t e", t=GT),
                                region_of[:, :].unsqueeze(1).to_broadcast([P, GT, E]), ALU.add
                                ).then_inc(sem("slot"), 1)
                wait(dve, "slot", c + 1)
                v.tensor_tensor(onehot[:, :, :].rearrange("p (t k) e -> p t k e", t=GT),
                                onehot[:, :, :].rearrange("p (t k) e -> p t k e", t=GT),
                                slot[:, :, :].unsqueeze(2).to_broadcast([P, GT, TOPK, E]), ALU.mult
                                ).then_inc(sem("chosen"), 1)
                wait(dve, "chosen", c + 1)
                v.tensor_reduce(pos_f[:, :], onehot[:, :, :], AX_X, ALU.add).then_inc(sem("pos_f"), 1)
                wait(dve, "pos_f", c + 1)
                v.tensor_copy(pos[p][:, :], pos_f[:, :]).then_inc(sem("pos"), 1)

            group_loop(dve, {"dt": group_dt, "xdt": times_dt, "cb_masked": mask_cb, "res1": residual1,
                             "norm0": norm0, "v_out": v_out, "neg_max": row_max, "res2": residual2,
                             "norm1": norm1, "w1_low": w1_low, "top": top_experts, "chosen": chosen,
                             "weight": weights, "slots": slots}
                       | {f"xbc{c}": silu(c) for c in range(4)} | {f"z_gate{h}": z_gates(h) for h in range(2)}
                       | {f"mix{t}": mix(t) for t in range(GT)} | {f"gate{h}": gates(h) for h in range(2)})

            plan, n_plan = sem("plan"), [0]

            def planned(ins):
                ins.then_inc(plan, 1)
                n_plan[0] += 1
                dve.wait_ge(plan, n_plan[0])

            dve.wait_ge(sem("counts"), 1)
            planned(v.tensor_copy(cnt[:, :], banks[0][0:1, 0:E]))
            planned(v.tensor_tensor(pad_f[:, :], cnt[:, :], region_of[0:1, :], ALU.add))
            planned(v.tensor_copy(pad_at[:, :], pad_f[:, :]))
            planned(v.tensor_tensor(over[:, :, :], cnt[:, :].unsqueeze(2).to_broadcast([1, E, E]),
                                    multiples[:, :].unsqueeze(1).to_broadcast([1, E, E]), ALU.is_gt))
            planned(v.tensor_reduce(n_steps[:, :], over[:, :, :], AX_X, ALU.add))
            planned(v.tensor_tensor(over[:, :, :], n_steps[:, :].unsqueeze(1).to_broadcast([1, E, E]),
                                    upto[:, :, :], ALU.mult))
            planned(v.tensor_reduce(last_step[:, :], over[:, :, :], AX_X, ALU.add))
            planned(v.tensor_tensor(done[:, :, :], last_step[:, :].unsqueeze(1).to_broadcast([1, STEPS, E]),
                                    step_no[:, :].unsqueeze(2).to_broadcast([1, STEPS, E]), ALU.is_le))
            planned(v.tensor_reduce(step_ef[:, :], done[:, :, :], AX_X, ALU.add))
            planned(v.tensor_tensor(done[:, :, :], done[:, :, :],
                                    n_steps[:, :].unsqueeze(1).to_broadcast([1, STEPS, E]), ALU.mult))
            planned(v.tensor_reduce(steps_before[:, :], done[:, :, :], AX_X, ALU.add))
            planned(v.tensor_tensor(row_f[:, :], step_no[:, :], steps_before[:, :], ALU.subtract))
            planned(v.tensor_scalar(row_f[:, :], row_f[:, :], float(STEP), None, ALU.mult))
            planned(v.scalar_tensor_tensor(row_f[:, :], step_ef[:, :], float(REGION), row_f[:, :],
                                           ALU.mult, ALU.add))
            planned(v.tensor_scalar(step_row[:, :], row_f[:, :], float(E * REGION), None, ALU.min))
            planned(v.tensor_scalar(step_e[:, :], step_ef[:, :], float(E - 1), None, ALU.min))
            assert n_plan[0] == N_PLAN

            def turned(j, p):
                dve.wait_ge(sem("rows_turned"), j + 1)
                wait(dve, "up", 2 * (j - 1))
                v.tensor_copy(xgT[p], turn_ps[p]).then_inc(sem("xgT"), 1)

            def scaled(j, p, b):
                if not isinstance(j, int) or j >= Y_RING:
                    q = b % Y_RING
                    dve.wait_ge(sem(f"parts_sent{q}"), 32 // Y_RING * (j - q))
                for i in range(HALVES):
                    dve.wait_ge(sem("down"), j + 1)
                    v.tensor_scalar(y_s[b % Y_RING][:, i, :], banks[6 + p][:, i * D:(i + 1) * D],
                                    xg[b][:, i, W_COL:W_COL + 1], None, ALU.mult).then_inc(sem("y_scaled"), 1)

            def step(j, b):
                turned(j, b % 2)
                if not isinstance(j, int) or j >= 2:
                    scaled(j - 2, b % 2, (b - 2) % ROWS_RING)

            for j in range(ROWS_RING):
                step(j, j)
            with dve.Fori(1, STEPS // ROWS_RING) as i:
                for b in range(ROWS_RING):
                    step(ROWS_RING * i + b, b)
            for j in (STEPS - 2, STEPS - 1):
                scaled(j, j % 2, j % ROWS_RING)

            def last(i):
                for p in range(2):
                    f = 2 * i + p
                    dve.wait_ge(sem(f"parts_loaded{p}"), 16 * (TOPK + 1) * (i + 1))
                    tot = total[p].rearrange("p t d -> p (t d)")
                    v.tensor_tensor(tot, x2_back[p].rearrange("p t d -> p (t d)"), parts[p][:, 0, :], ALU.add
                                    ).then_inc(sem("sum"), 1)
                    for k in range(1, TOPK):
                        dve.wait_ge(sem("sum"), TOPK * f + k)
                        v.tensor_tensor(tot, tot, parts[p][:, k, :], ALU.add).then_inc(sem("sum"), 1)
                    dve.wait_ge(sem("sum"), TOPK * f + TOPK)
                    for t in range(GT):
                        v.bn_stats(stats[2][:, t, :], total[p][:, t, :]).then_inc(sem("stats2"), 1)
                    dve.wait_ge(sem("stats2"), GT * (f + 1))
                    wait(dve, "rstd2_e", f)
                    dve.sem_inc(sem("dve_gate"), 1)
                    for t in range(GT):
                        ins = v.bn_aggr(mv[2][:, t, :], stats[2][:, t, :])
                    ins.then_inc(sem("mv2"), 1)
                    dve.wait_ge(sem("mv2"), f + 1)
                    dve.wait_ge(sem("rstd2"), f + 1)
                    wait(dve, f"stored{p}", 16 * i)
                    for t in range(GT):
                        ins = v.tensor_scalar(y_out[p][:, t, :], total[p][:, t, :], mv[2][:, t, 0:1],
                                              rstd[2][:, t:t + 1], ALU.subtract, ALU.mult)
                    ins.then_inc(sem(f"normed{p}"), 1)

            last(0)
            with dve.Fori(1, GROUPS // 2) as i:
                last(i)

        @block.tensor
        def _(pe):
            mm = nc.tensor.matmul

            def three(ps, lhi, llo, rhi, rlo, start=True, stop=True):
                mm(ps, lhi, rlo, start=start, stop=False)
                mm(ps, llo, rhi, start=False, stop=False)
                return mm(ps, lhi, rhi, start=False, stop=stop)

            pe.wait_ge(sem("xT_loaded"), 64)
            pe.wait_ge(sem("weights"), 16 * N_WEIGHTS)
            for n in range(SEQS):
                ins = mm(banks[0][:, HEADS * n:HEADS * (n + 1)], xT_all[:, n, :], in_w[:, INNER + CONV:],
                         start=True, stop=True)
            ins.then_inc(sem("dt_proj"), 1)
            pe.wait_ge(sem("constants"), N_CONST)
            pe.wait_ge(sem("keys_sq"), 1)
            mm(banks[1][:, 0:E], ones[:, :], keys_sq[:, :], start=True, stop=True).then_inc(sem("keys_norm"), 1)
            pe.wait_ge(sem("conv_low"), 1)
            pe.wait_ge(sem("z_low"), 1)
            pe.wait_ge(sem("masks"), 2)
            pe.wait_ge(sem("scaled"), N_SCALED)

            def conv(c):
                def run(g, p):
                    if c == 0:
                        wait(pe, "x_hi", g + 1)
                        wait(pe, "x_lo", g + 1)
                    if c < 2:
                        wait(pe, "xdt", 2 * (g - 1) + c + 1)
                    else:
                        wait(pe, "conv_tanh", 4 * g + c - 1)
                    ps = front[c % 2][:, :]
                    w = slice(c * P, (c + 1) * P)
                    for j in range(TAPS):
                        ins = three(ps, conv_hi[:, j, w], conv_lo[:, j, w], x_hi[p][:, :, j:j + L],
                                    x_lo[p][:, :, j:j + L], start=(j == 0), stop=(j == TAPS - 1))
                    ins.then_inc(sem("conv"), 1)
                return run

            def z_proj(h):
                def run(g, p):
                    wait(pe, "conv_tanh", 4 * g + 3 + h)
                    for t in (2 * h, 2 * h + 1):
                        ins = three(front[h][:, (t % 2) * INNER:(t % 2 + 1) * INNER],
                                    x_hi[p][:, t, OFF:OFF + L], x_lo[p][:, t, OFF:OFF + L],
                                    z_hi[:, :], z_lo[:, :])
                    ins.then_inc(sem("z_proj"), 1)
                return run

            def turn_x(g, p):
                wait(pe, "xbc", 4 * g + 2)
                for h in range(2):
                    wait(pe, "z_gate", 2 * g + h + 1)
                    for t in (2 * h, 2 * h + 1):
                        for c in range(2):
                            at = (t % 2) * INNER + c * P
                            ins = nc.tensor.transpose(front[h][:, at:at + P], xbc[:, c, t * L:(t + 1) * L],
                                                      ident[:, :])
                    ins.then_inc(sem("x_turned"), 1)

            def segments(t):
                def run(g, p):
                    wait(pe, "adt", 4 * g + 2 * (t // 2) + 2)
                    wait(pe, "decay", GT * g + t - 1)
                    hs = slice(HEADS * (t % 2), HEADS * (t % 2 + 1))
                    mm(segs[t % 2][:, :], after[:, :], adt_hi[:, hs, :], start=True, stop=False)
                    mm(segs[t % 2][:, :], after[:, :], adt_lo[:, hs, :], start=False, stop=True
                       ).then_inc(sem("seg"), 1)
                return run

            def pair_products(g, p):
                wait(pe, "xbc", 4 * g + 4)
                wait(pe, "gatedT", 2 * g)
                for t in range(GT):
                    ts = slice(t * L, (t + 1) * L)
                    ins = mm(mids[0][:, ts], xbc[:, 2, ts], xbc[:, 3, ts], start=True, stop=True)
                ins.then_inc(sem("cb"), 1)

            def outputs(t):
                def run(g, p):
                    wait(pe, "xdt", 2 * g + t // 2 + 1)
                    if t == 0:
                        wait(pe, "res1", GT * g)
                    if t == 2:
                        wait(pe, "cb_masked", g + 1)
                    wait(pe, "mix", GT * g + t + 1)
                    ps = mids[1 - t // 2]
                    for c in range(2):
                        at = (t % 2) * INNER + c * P
                        mm(ps[:, at:at + P], xbc[:, c, t * L:(t + 1) * L], d_diag[:, c, :], start=True, stop=False)
                        for h in (2 * c, 2 * c + 1):
                            at = (t % 2) * INNER + h * HD
                            ins = mm(ps[:, at:at + HD], decay[t % 2][:, h, :], xdt[:, t, h * HD:(h + 1) * HD],
                                     start=False, stop=(h == 2 * c + 1))
                    ins.then_inc(sem("y"), 1)
                return run

            def gate_T(g, p):
                for h in range(2):
                    wait(pe, "gated", 2 * g + h + 1)
                    for t in (2 * h, 2 * h + 1):
                        for c in range(2):
                            at = (t % 2) * INNER + c * P
                            ins = nc.tensor.transpose(mids[1 - h][:, at:at + P], z_gate[:, t, c * P:(c + 1) * P],
                                                      ident[:, :])
                    ins.then_inc(sem("gatedT_ps"), 1)

            def mixed(g, p):
                wait(pe, "gatedT", 2 * g + 2)
                for t in range(GT):
                    for c in range(2):
                        ins = mm(mids[1][:, t * D:(t + 1) * D], gatedT[:, t, c, :], out_wn[:, c, :],
                                 start=(c == 0), stop=(c == 1))
                ins.then_inc(sem("mixed"), 1)

            def k_proj(b, p):
                wait_load(pe, f"ctx_loaded{p}", b, p)
                wait(pe, "logit", b)
                mm(late[1][:, 0:GT * LC], wk_s[:, :], ctx_s[p][:, :, 0:LC], start=True, stop=True
                   ).then_inc(sem("k_proj"), 1)

            def v_proj(b, p):
                wait(pe, "x2T", b)
                for t in range(GT):
                    ins = mm(late[0][0:LC, t * D:(t + 1) * D], ctx_s[p][:, t, 0:LC], wv_n[:, :],
                             start=True, stop=True)
                ins.then_inc(sem("v_proj"), 1)

            def x1_T(b, p):
                wait(pe, "x1", b + 1)
                wait(pe, "v", b + 1)
                for t in range(GT):
                    ins = nc.tensor.transpose(late[0][:, t * L:(t + 1) * L], x1[p][:, t, :], ident[:, :])
                ins.then_inc(sem("x1T_ps"), 1)

            def q_proj(b, p):
                wait(pe, "slot", b)
                wait(pe, "kT", b + 1)
                wait(pe, "x1T", b + 1)
                mm(late[1][:, :], wq_s[:, :], x1T_s[:, :], start=True, stop=True).then_inc(sem("q_proj"), 1)

            def scores(b, p):
                wait(pe, "qT", b + 1)
                for t in range(GT):
                    ins = mm(late[0][:, t * LC:(t + 1) * LC], qT_s[:, t * L:(t + 1) * L], kT_s[:, t, :],
                             start=True, stop=True)
                ins.then_inc(sem("scores"), 1)

            def prob_T(b, p):
                wait(pe, "prob", GT * (b + 1))
                for t in range(GT):
                    ins = nc.tensor.transpose(late[1][0:LC, t * L:(t + 1) * L], prob[:, t, :], ident[:, :])
                ins.then_inc(sem("probT_ps"), 1)

            def attended(b, p):
                wait(pe, "probT", b + 1)
                for t in range(GT):
                    ins = mm(late[0][:, t * D:(t + 1) * D], probT[0:LC, t, :], v_s[0:LC, t, :],
                             start=True, stop=True)
                ins.then_inc(sem("attended"), 1)

            def x2_T(c, p):
                wait(pe, "x2", c + 1)
                for t in range(GT):
                    ins = nc.tensor.transpose(late[0][:, t * L:(t + 1) * L], x2[p][:, t, :], ident[:, :])
                ins.then_inc(sem("x2T_ps"), 1)

            def logits(c, p):
                wait(pe, "x2T", c + 1)
                for t in range(GT):
                    ins = mm(late[1][:, t * E:(t + 1) * E], x2T_s[:, t * L:(t + 1) * L], route_w[:, :],
                             start=True, stop=True)
                ins.then_inc(sem("logits"), 1)

            def ranks(c, p):
                wait(pe, "picked", c + 1)
                wait(pe, "carry", c)
                if not isinstance(c, int) or c + 1 < GROUPS:
                    wait(pe, "kT", c + 2)
                ps = late[1]
                flat = picked[:, :, :].rearrange("p t e -> p (t e)")
                mm(ps[:, 0:GT * E], before16[:, :], flat, start=True, stop=False)
                for t in range(GT - 1):
                    n = GT - 1 - t
                    mm(ps[:, (t + 1) * E:GT * E].rearrange("p (t e) -> p t e", e=E), ones16[:, :],
                       picked[:, t:t + 1, :].to_broadcast([P, n, E]), start=False, stop=False)
                mm(ps[:, 0:GT * E].rearrange("p (t e) -> p t e", e=E), ones16[:, :],
                   carry16[1 - p][:, :].unsqueeze(1).to_broadcast([P, GT, E]), start=False, stop=True
                   ).then_inc(sem("ranks"), 1)

            group_loop(pe, {"turn_x": turn_x, "cb": pair_products, "gate_T": gate_T, "mixed": mixed,
                            "k": k_proj, "v": v_proj, "x1_T": x1_T, "q": q_proj, "scores": scores,
                            "prob_T": prob_T, "attended": attended, "x2_T": x2_T, "logits": logits,
                            "ranks": ranks}
                       | {f"conv{c}": conv(c) for c in range(4)} | {f"z{h}": z_proj(h) for h in range(2)}
                       | {f"seg{t}": segments(t) for t in range(GT)} | {f"y{t}": outputs(t) for t in range(GT)})

            pe.wait_ge(sem("carry"), GROUPS)
            pe.wait_ge(sem("xdt"), 2 * GROUPS)
            mm(banks[0][:, 0:E], ones16[:, :], carry16[(GROUPS - 1) % 2][:, :], start=True, stop=True
               ).then_inc(sem("counts"), 1)

            pe.wait_ge(sem("plan"), N_PLAN)
            pe.wait_ge(sem("w1_low"), E)
            pe.wait_ge(sem("w2_loaded"), 64)
            pe.wait_ge(sem("b2_split"), 16)
            pe.wait_ge(sem("x2"), GROUPS)

            def turn(j, p, b):
                pe.wait_ge(sem(f"xg_loaded{b}"), 16 // ROWS_RING * (j - b) + 16)
                wait(pe, "xgT", j - 1)
                for hl in range(2):
                    for i in range(HALVES):
                        ins = nc.tensor.transpose(turn_ps[p][:, hl, i * P:(i + 1) * P],
                                                  xg[b][:, i, hl * D // 2:(hl + 1) * D // 2].bitcast(F16),
                                                  ident16[:, :])
                ins.then_inc(sem("rows_turned"), 1)

            def up(j, p):
                ex = pe.value_load(step_e[0:1, bass.ds(j, 1)], min_val=0, max_val=E - 1)
                wait(pe, "xgT", j + 1)
                for f in range(NF):
                    wait(pe, "hidden", NF * (j - 2) + 2 * (f // 2) + 2)
                    ps = banks[2 + 2 * p + f // 2][:, (f % 2) * STEP:(f % 2 + 1) * STEP]
                    wh = w1_hi[:, bass.ds(ex, 1), f, :].rearrange("p e m -> p (e m)")
                    wl = w1_lo[:, bass.ds(ex, 1), f, :].rearrange("p e m -> p (e m)")
                    ins = three(ps, wh, wl, xgT[p][:, 0, :], xgT[p][:, 1, :])
                    if f % 2:
                        ins.then_inc(sem("up"), 1)

            def down(j, p):
                ex = pe.value_load(step_e[0:1, bass.ds(j, 1)], min_val=0, max_val=E - 1)
                wait(pe, "y_scaled", HALVES * (j - 1))
                for i in range(HALVES):
                    ps = banks[6 + p][:, i * D:(i + 1) * D]
                    for f in range(NF):
                        if i == 0:
                            pe.wait_ge(sem("hidden"), NF * j + f + 1)
                        ins = mm(ps, hid[p][:, f, i * P:(i + 1) * P],
                                 w2_s[:, bass.ds(ex, 1), f, :].rearrange("p e m -> p (e m)"),
                                 start=(f == 0), stop=False)
                    ins = mm(ps, unscale16[:, :], b2_16[:, bass.ds(ex, 1), :].rearrange("p e m -> p (e m)"),
                             start=False, stop=True)
                ins.then_inc(sem("down"), 1)

            def step(j, b):
                turn(j, b % 2, b)
                if not isinstance(j, int) or j >= 1:
                    up(j - 1, (b - 1) % 2)
                if not isinstance(j, int) or j >= 2:
                    down(j - 2, b % 2)

            for j in range(ROWS_RING):
                step(j, j)
            with pe.Fori(1, STEPS // ROWS_RING) as i:
                for b in range(ROWS_RING):
                    step(ROWS_RING * i + b, b)
            up(STEPS - 1, (STEPS - 1) % 2)
            down(STEPS - 2, (STEPS - 2) % 2)
            down(STEPS - 1, (STEPS - 1) % 2)


_INS = ["x", "xT", "ctxT", "in_wT", "conv_w", "conv_b", "norm_w", "out_wT", "dt_bias", "a_log", "d_param",
        "wq", "bq", "wk", "bk", "wv", "bv", "keysT", "w1T", "b1T", "w2T", "b2", "rwT", "rb"]


def kernel(x, ctx_1024, L0_attn_in_proj_w, L0_attn_conv_w, L0_attn_conv_b, L0_attn_norm_w, L0_attn_out_proj_w,
           L0_attn_dt_bias, L0_attn_A_log, L0_attn_D_param, L0_xattn_Wq, L0_xattn_bq, L0_xattn_Wk, L0_xattn_bk,
           L0_xattn_Wv, L0_xattn_bv, L0_ffn_keys, L0_ffn_w1, L0_ffn_b1, L0_ffn_w2, L0_ffn_b2, L0_ffn_rw,
           L0_ffn_rb):
    import concourse.bacc as _bacc
    from concourse.bass_utils import run_bass_kernel_spmd as _run

    a = [np.asarray(v) for v in (
        x, ctx_1024, L0_attn_in_proj_w, L0_attn_conv_w, L0_attn_conv_b, L0_attn_norm_w, L0_attn_out_proj_w,
        L0_attn_dt_bias, L0_attn_A_log, L0_attn_D_param, L0_xattn_Wq, L0_xattn_bq, L0_xattn_Wk, L0_xattn_bk,
        L0_xattn_Wv, L0_xattn_bv, L0_ffn_keys, L0_ffn_w1, L0_ffn_b1, L0_ffn_w2, L0_ffn_b2, L0_ffn_rw, L0_ffn_rb)]
    (xx, cc, inw, cw, cb, nw, ow, dtb, al, dp, wq, bq, wk, bk, wv, bv, keys, w1, b1, w2, b2, rw, rb) = a
    laid = dict(
        x=xx, xT=xx.reshape(TOKENS, D).T, ctxT=cc.transpose(2, 0, 1), in_wT=inw.T,
        conv_w=cw.reshape(CONV, TAPS).T.reshape(-1), conv_b=cb.reshape(4, P).T, norm_w=nw.reshape(2, P).T,
        out_wT=ow.T.reshape(2, P, D).transpose(1, 0, 2), dt_bias=dtb, a_log=al, d_param=dp,
        wq=wq, bq=bq.reshape(P, 1), wk=wk, bk=bk.reshape(P, 1), wv=wv, bv=bv, keysT=keys.T,
        w1T=w1.transpose(2, 0, 1), b1T=b1.reshape(E, NF, P).transpose(2, 0, 1),
        w2T=w2.reshape(E, D, NF, P).transpose(3, 0, 2, 1), b2=b2.reshape(1, E * D), rwT=rw.T, rb=rb)
    nc = _bacc.Bacc("TRN2", target_bir_lowering=False, num_devices=1)
    arrays, args = {}, []
    for name in _INS:
        v = np.ascontiguousarray(laid[name])
        arrays[f"in_{name}_dram"] = v
        args.append(nc.dram_tensor(f"in_{name}_dram", v.shape, mybir.dt.from_np(v.dtype), kind="ExternalInput").ap())
    out = nc.dram_tensor("out_dram", (SEQS, L, D), F32, kind="ExternalOutput").ap()
    decoder_layer(nc, *args, out)
    r = _run(nc, [arrays], core_ids=[0])
    return r.results[0]["out_dram"]
```

```python
from contextlib import ExitStack

import numpy as np

import concourse.bass as bass
from concourse import mybir

F32 = mybir.dt.float32
F32R = mybir.dt.float32r
F16 = mybir.dt.float16
BF16 = mybir.dt.bfloat16
I32 = mybir.dt.int32
U32 = mybir.dt.uint32
ALU = mybir.AluOpType
ACT = mybir.ActivationFunctionType
AX_X = mybir.AxisListType.X
PE, ACTE, SPE = mybir.EngineType.PE, mybir.EngineType.Activation, mybir.EngineType.SP

P = 128
SEQS, L, D = 32, 128, 128
TOKENS = SEQS * L
LC = 77
HEADS, HD = 4, 64
INNER = HEADS * HD
CONV = INNER + 2 * P
TAPS = 4
E, TOPK, FF = 16, 4, 512
NF = FF // P
EPS = 1e-5
GT = 4
GROUPS = SEQS // GT
GTOK = GT * L
PADT = 132
OFF = TAPS - 1
STEP = 256
HALVES = STEP // P
STEPS = -(-(TOPK * TOKENS + E * (STEP - 1)) // STEP)
ROWS_RING, Y_RING, HID_RING = 8, 4, 4
STEPS += -STEPS % ROWS_RING
REGION = TOKENS + STEP
MULTIPLES = TOKENS // STEP
ROW_W = 130
W_COL, DST_COL = 128, 129
W_SCALE = 64.0
SKIP_DST = 1 << 20
NORM_FACT = float(1.0 / np.sqrt(np.float32(D)))
N_CONST = 21
N_WEIGHTS = 19
N_SCALED = 8
PADS_PLANNED, N_PLAN = 3, 16


def decoder_layer(nc, x, xT, ctxT, in_wT, conv_w, conv_b, norm_w, out_wT, dt_bias, a_log, d_param,
                  wq, bq, wk, bk, wv, bv, keysT, w1T, b1T, w2T, b2, rwT, rb, out):
    with ExitStack() as ctx:
        def sb(name, shape, dt=F32):
            return ctx.enter_context(nc.sbuf_tensor(name, shape, dt))

        def bank(name):
            return ctx.enter_context(nc.psum_tensor(name, [P, 512], F32))

        sems = {}

        def sem(name):
            if name not in sems:
                sems[name] = ctx.enter_context(nc.semaphore(name))
            return sems[name]

        def wait(eng, name, count):
            if not (isinstance(count, int) and count <= 0):
                eng.wait_ge(sem(name), count)

        def wait_load(eng, name, g, p):
            wait(eng, name, 8 * (g - p) + 16)

        rows_dram = nc.dram_tensor("rows_dram", [E * REGION + STEP, ROW_W], F32).ap()
        parts_dram = nc.dram_tensor("parts_dram", [TOPK * TOKENS, D], F32).ap()
        x2_dram = nc.dram_tensor("x2_dram", [SEQS, L, D], F32).ap()

        ident = sb("ident", [P, P])
        ident16 = sb("ident16", [P, P], F16)
        causal = sb("causal", [P, P])
        after = sb("after", [P, P], F32R)
        before16 = sb("before16", [P, P], BF16)
        ones16 = sb("ones16", [P, P], BF16)
        ones = sb("ones", [P, P])
        pair16 = sb("pair16", [2, P], F16)
        iota_e = sb("iota_e", [P, E])
        region_of = sb("region_of", [P, E])
        dst_of = [sb(f"dst_of{n}", [P, GT * TOPK]) for n in range(2)]
        multiples = sb("multiples", [1, MULTIPLES])
        step_no = sb("step_no", [1, STEPS])
        upto = sb("upto", [1, E, E])
        minus_half = sb("minus_half", [P, GT])
        eps4 = sb("eps4", [P, GT])
        pad_rows = sb("pad_rows", [P, HALVES, ROW_W])

        conv_hi = sb("conv_hi", [P, TAPS, CONV], F32R)
        conv_lo = sb("conv_lo", [P, TAPS, CONV], F32R)
        z_hi = sb("z_hi", [P, INNER], F32R)
        z_lo = sb("z_lo", [P, INNER], F32R)
        convb = sb("convb", [P, 4])
        convb_half = sb("convb_half", [P, 4])
        out_wn = sb("out_wn", [P, 2, D])
        normw = sb("normw", [P, 2])
        dcol = sb("dcol", [P, 2])
        d_diag = sb("d_diag", [P, 2, P])
        dtb = sb("dtb", [P, HEADS])
        alog = sb("alog", [P, HEADS])
        a_exp = sb("a_exp", [P, HEADS])
        wq_s = sb("wq_s", [P, D])
        wk_s = sb("wk_s", [P, D])
        wv_n = sb("wv_n", [P, D])
        bq_s = sb("bq_s", [P, 1])
        bk_s = sb("bk_s", [P, 1])
        bv_n = sb("bv_n", [P, D])
        keys_s = sb("keys_s", [P, E])
        rw_s = sb("rw_s", [P, E])
        rb_s = sb("rb_s", [P, E])
        keys_sq = sb("keys_sq", [P, E])
        route_w = sb("route_w", [P, E])
        route_b = sb("route_b", [P, E])
        w1_hi = sb("w1_hi", [P, E, NF, P], F16)
        w1_lo = sb("w1_lo", [P, E, NF, P], F16)
        w2_16 = sb("w2_16", [P, E, NF, 2, D], F16)
        b1_s = sb("b1_s", [P, E, NF])
        b2_16 = sb("b2_16", [2, E, D], F16)

        ARENA = 11430
        arena = sb("arena", [P, ARENA])
        used = {"at": 0}

        def take(*shape):
            n = int(np.prod(shape))
            v = arena[:, used["at"]:used["at"] + n]
            used["at"] += n
            assert used["at"] <= ARENA, used["at"]
            if len(shape) == 2:
                v = v.rearrange("p (a b) -> p a b", b=shape[1])
            if len(shape) == 3:
                v = v.rearrange("p (a b c) -> p a b c", b=shape[1], c=shape[2])
            return v

        in_w = take(CONV + INNER + HEADS)
        conv_wb = take(TAPS, CONV)
        conv_f = take(TAPS, CONV)
        z_half = take(INNER)
        xT_all = take(SEQS, L)
        dtw = take(8, SEQS * HEADS)
        after_f = take(P)
        before_f = take(P)
        out_w = take(2, D)
        wv_s = take(D)
        bv_s = take(D)
        used["at"] = 0
        x_tok = [take(GT, D) for _ in range(2)]
        ctx_s = [take(GT, LC + 1) for _ in range(2)]
        th = [take(GTOK) for _ in range(2)]
        xbc = take(4, GTOK)
        z_gate = take(GT, INNER)
        xdt = take(GT, INNER)
        cb_masked = take(GT, L)
        decay = [take(HEADS, L) for _ in range(2)]
        gatedT = take(GT, 2, P)
        res1 = take(GT, D)
        x1 = [take(GT, D) for _ in range(2)]
        junk = take(INNER)
        kT_s = take(GT, LC)
        used["at"] = 0
        xg = [take(HALVES, ROW_W) for _ in range(ROWS_RING)]
        xgT = [take(STEP).bitcast(F16).rearrange("p (a b) -> p a b", a=2) for _ in range(2)]
        hid = [take(NF, STEP) for _ in range(2)]
        hid16 = [take(NF, STEP).bitcast(F16).rearrange("p f (a b) -> p f a b", a=2) for _ in range(HID_RING)]
        y_s = [take(HALVES, D) for _ in range(Y_RING)]
        expert_words = used["at"]
        used["at"] = 0
        over = take(E, MULTIPLES)[0:1, :, :]
        before_e = take(E, E)[0:1, :, :]
        done = take(STEPS, E)[0:1, :, :]
        used["at"] = 0
        parts = [take(TOPK, GT * D) for _ in range(2)]
        total = [take(GT, D) for _ in range(2)]
        y_out = [take(GT, D) for _ in range(2)]
        used["at"] = expert_words
        x2_back = [take(GT, D) for _ in range(2)]

        dta = sb("dta", [P, 3, SEQS * HEADS])
        dta_g = [sb(f"dta_g{p}", [P, 3, GT * HEADS]) for p in range(2)]
        xT_g = [sb(f"xT_g{p}", [P, GT, L]) for p in range(2)]
        x_hi = [sb(f"x_hi{p}", [P, GT, PADT], F32R) for p in range(2)]
        x_lo = [sb(f"x_lo{p}", [P, GT, PADT], F32R) for p in range(2)]
        adt_hi = sb("adt_hi", [P, 2 * HEADS, L], F32R)
        adt_lo = sb("adt_lo", [P, 2 * HEADS, L], F32R)
        x1T_s = sb("x1T_s", [P, GTOK])
        qT_s = sb("qT_s", [P, GTOK])
        v_s = sb("v_s", [P, GT, D])
        prob = sb("prob", [P, GT, LC])
        probT = sb("probT", [P, GT, L])
        res2 = sb("res2", [P, GT, D])
        x2 = [sb(f"x2_{p}", [P, GT, D]) for p in range(2)]
        x2T_s = sb("x2T_s", [P, GTOK])
        rows = [sb(f"rows{p}", [P, GT, TOPK, ROW_W]) for p in range(2)]
        b2_stage = rows[0][0:1, :, :, :].rearrange("p t k w -> p (t k w)")[:, 0:E * D]
        b2_lo = rows[1][0:1, :, :, :].rearrange("p t k w -> p (t k w)")[:, 0:E * D // 2].bitcast(F16)
        w_stage = [sb(f"w_stage{p}", [P, FF]) for p in range(2)]

        ss = sb("ss", [P, GT])
        stats = [sb(f"stats{n}", [P, GT, 6]) for n in range(3)]
        mv = [sb(f"mv{n}", [P, GT, 2]) for n in range(3)]
        var_e = [sb(f"var_e{n}", [P, GT]) for n in range(3)]
        rstd = [sb(f"rstd{n}", [P, GT]) for n in range(3)]
        neg_max = sb("neg_max", [P, GT])
        neg_mean = [sb(f"neg_mean{p}", [P, GT]) for p in range(2)]
        prob_sum = sb("prob_sum", [P, GT])
        prob_rsum = sb("prob_rsum", [P, GT])
        logit = sb("logit", [P, GT, E])
        top8 = sb("top8", [P, GT, 8])
        idx8 = sb("idx8", [P, GT, 8], U32)
        idx_f = sb("idx_f", [P, GT, TOPK])
        d4 = sb("d4", [P, GT, TOPK])
        e4 = sb("e4", [P, GT, TOPK])
        s4 = sb("s4", [P, GT])
        r4 = sb("r4", [P, GT])
        onehot = sb("onehot", [P, GT * TOPK, E])
        picked = sb("picked", [P, GT, E], BF16)
        group_n = sb("group_n", [P, E])
        carry16 = [sb(f"carry16_{n}", [P, E], BF16) for n in range(2)]
        slot = sb("slot", [P, GT, E])
        pos_f = sb("pos_f", [P, GT * TOPK])
        pos = [sb(f"pos{p}", [P, GT * TOPK], U32) for p in range(2)]

        cnt = sb("cnt", [1, E])
        n_steps = sb("n_steps", [1, E])
        last_step = sb("last_step", [1, E])
        step_ef = sb("step_ef", [1, STEPS])
        steps_before = sb("steps_before", [1, STEPS])
        row_f = sb("row_f", [1, STEPS])
        step_row = sb("step_row", [1, STEPS], I32)
        step_e = sb("step_e", [1, STEPS], I32)
        pad_f = sb("pad_f", [1, E])
        pad_at = sb("pad_at", [1, E], I32)

        banks = [bank(f"bank{n}") for n in range(8)]
        turn_ps = [banks[p][:, 0:STEP].bitcast(F16).rearrange("p (a b) -> p a b", a=2) for p in range(2)]
        front, segs, mids = banks[0:2], banks[2:4], banks[4:6]
        late = banks[6:8]

        block = ctx.enter_context(nc.Block())

        SCHEDULE = (
            ("load_x", -1), ("load_ctx", 0), ("load_w1", 1), ("dt", 0),
            ("conv0", 0), ("gate_T1", 1), ("silu0", 0), ("xbc0", 0), ("gate_T_out", 1),
            ("conv1", 0), ("norm1", 2), ("mixed", 1), ("silu1", 0), ("xbc1", 0), ("res1", 1),
            ("x2_T", 2), ("x2_T_out", 2), ("w2_high", 2), ("w2_low", 2), ("conv2", 0),
            ("silu2", 0), ("row_high", 2), ("xbc2", 0),
            ("logits", 2), ("conv3", 0), ("split_x", -1), ("top", 2), ("silu3", 0), ("k", 1), ("norm0", 1),
            ("k_out", 1), ("xbc3", 0), ("z0", 0), ("z_tanh0", 0), ("chosen", 2), ("z_gate0", 0),
            ("v", 1), ("z1", 0), ("z_tanh1", 0), ("z_gate1", 0), ("seg0", 0), ("decay0", 0), ("seg1", 0),
            ("decay1", 0), ("ranks", 2), ("top_exp", 2), ("v_out", 1), ("turn_x", 0), ("xdt", 0), ("slots", 2),
            ("weight", 2), ("x1_T", 1), ("x1_T_out", 1), ("cb", 0), ("cb_masked", 0),
            ("q", 1), ("q_out", 1), ("seg2", 0), ("seg3", 0), ("mix0", 0), ("y0", 0), ("mix1", 0), ("y1", 0),
            ("w1_high", 1), ("positions", 2), ("decay2", 0), ("mix2", 0), ("scores", 1), ("decay3", 0),
            ("neg_max", 1), ("softmax", 1), ("y2", 0), ("mix3", 0), ("gate0", 0), ("w1_low", 1), ("load_w2", 1),
            ("y3", 0), ("prob_T", 1), ("prob_T_out", 1), ("gate_T0", 0), ("gate1", 0), ("sumsq", 0),
            ("attended", 1), ("res2", 1))
        POOL_SCHEDULE = (
            ("norm_y", 1), ("norm_b", 2), ("adt0", 0), ("send2", 3), ("norm_a", 1), ("split_x", -1), ("send3", 3),
            ("adt1", 0), ("send0", 2), ("send1", 2))
        POOL_TAIL = (
            ("norm_y", 1), ("norm_b", 2), ("norm_a", 1), ("send2", 3), ("send3", 3), ("send0", 2), ("send1", 2))
        FIRST_LOOPED = 3

        def group_loop(eng, parts_of, schedule=SCHEDULE, tail=SCHEDULE):
            def iteration(g, p, schedule=schedule):
                for part, lag in schedule:
                    if part not in parts_of or isinstance(g, int) and not 0 <= g - lag < GROUPS:
                        continue
                    parts_of[part](g - lag, (p - lag) % 2)

            for g in range(FIRST_LOOPED):
                iteration(g, g % 2)
            with eng.Fori(FIRST_LOOPED // 2, (GROUPS - 1) // 2) as i:
                iteration(2 * i + 1, 1)
                iteration(2 * i + 2, 0)
            iteration(GROUPS - 1, (GROUPS - 1) % 2)
            for g in range(GROUPS, GROUPS + 3):
                iteration(g, g % 2, tail)

        def read_plan(plan, at, n, engine, max_val):
            _, values = nc.values_load_multi_w_load_instructions(
                plan[0:1, bass.ds(at, n)], engines=(engine,), min_val=0, max_val=max_val,
                skip_runtime_bounds_check_because="the plan is clamped to this where it is made")
            return values

        def w_half(layer, e, hl):
            if layer == 0:
                return (w1_hi, w1_lo)[hl][:, bass.ds(e, 1), :, :].rearrange("p e f m -> p (e f) m")
            return w2_16[:, bass.ds(e, 1), :, hl, :].rearrange("p e f m -> p (e f) m")

        def arena_free(eng):
            eng.wait_ge(sem("dt_proj"), 1)
            eng.wait_ge(sem("mixer_low"), 2)
            eng.wait_ge(sem("dt_split"), 3)
            eng.wait_ge(sem("masks"), 2)
            eng.wait_ge(sem("scaled"), N_SCALED)

        def pad_experts(eng, engine, first):
            eng.wait_ge(sem("plan"), PADS_PLANNED)
            at = read_plan(pad_at, first, E // 2, engine, E * REGION - STEP)
            for e in range(E // 2):
                eng.dma_start(rows_dram[bass.ds(at[e], STEP), :].rearrange("(i p) w -> p i w", p=P),
                              pad_rows[:, :, :]).then_inc(sem("padded"), 16)

        @block.sync
        def _(sp):
            def load(dst, src, name="weights"):
                sp.dma_start(dst, src).then_inc(sem(name), 16)

            for q in range(4):
                n = SEQS // 4
                load(xT_all[:, n * q:n * q + n, :],
                     xT[:, n * L * q:n * L * (q + 1)].rearrange("d (s l) -> d s l", l=L), "xT_loaded")
            load(conv_wb.rearrange("p j c -> p (j c)"), conv_w.partition_broadcast(P), "conv_w_loaded")
            xT3 = xT.rearrange("d (s l) -> d s l", l=L)
            load(xT_g[0][:, :, :], xT3[:, 0:GT, :], "xT_loaded0")
            load(dtb[:, :], dt_bias.partition_broadcast(P))
            load(alog[:, :], a_log.partition_broadcast(P))
            load(convb[:, :], conv_b)
            load(out_w, out_wT)
            load(normw[:, :], norm_w)
            for h in range(HEADS):
                load(dcol[HD * (h % 2):HD * (h % 2) + HD, h // 2:h // 2 + 1],
                     d_param[h:h + 1].partition_broadcast(HD))
            load(wv_s, wv)
            load(bv_s, bv.partition_broadcast(P))
            load(keys_s[:, :], keysT)
            load(rw_s[:, :], rwT)
            load(rb_s[:, :], rb.partition_broadcast(P))
            load(wq_s[:, :], wq)
            load(wk_s[:, :], wk)
            load(bq_s[:, :], bq)
            load(bk_s[:, :], bk)
            load(b1_s[:, :, :], b1T)
            load(b2_stage, b2, "b2_loaded")

            def load_x(g, p):
                if not isinstance(g, int) or g > 0:
                    wait(sp, "x_lo", g - 1)
                    load(xT_g[p][:, :, :], xT3[:, bass.ds(GT * g, GT), :], f"xT_loaded{p}")
                if isinstance(g, int) and g <= 1:
                    arena_free(sp)
                wait(sp, "res1", GT * (g - 1))
                sp.dma_start(x_tok[p], x[bass.ds(GT * g, GT), :, :].rearrange("s l d -> l s d")
                             ).then_inc(sem(f"x_loaded{p}"), 16)

            def load_ctx(g, p):
                wait(sp, "v_proj", g - 1)
                wait(sp, "k_proj", g - 1)
                sp.dma_start(ctx_s[p][:, :, 0:LC],
                             ctxT[:, bass.ds(GT * g, GT), :]).then_inc(sem(f"ctx_loaded{p}"), 16)

            def load_w(wT, first):
                def run(c, p):
                    for n in range(2):
                        wait(sp, "w_low", 4 * c + first + n - 1)
                        load(w_stage[n][:, :], wT[:, bass.ds(2 * c + n, 1), :].rearrange("d e f -> d (e f)"),
                             f"w_loaded{n}")
                return run

            load_x(0, 0)
            sp.wait_ge(sem("b2_low"), 1)
            load(b2_16[1:2, :, :].rearrange("p e d -> p (e d)"), b2_lo, "b2_split")
            group_loop(sp, {"load_x": load_x, "load_w1": load_w(w1T, 0), "load_w2": load_w(w2T, 2),
                            "load_ctx": load_ctx})

            pad_experts(sp, SPE, 0)
            sp.wait_ge(sem("padded"), 16 * E)
            for p in range(2):
                sp.wait_ge(sem(f"rows_sent{p}"), 16 * GT * TOPK * GROUPS // 2 + 16)
            sp.wait_ge(sem("plan"), N_PLAN)

            def load_rows(first):
                at = read_plan(step_row, first, ROWS_RING, SPE, E * REGION)
                for b in range(ROWS_RING):
                    if not isinstance(first, int):
                        q, n = b % Y_RING, ROWS_RING // Y_RING * (i - 1) + b // Y_RING + 1
                        sp.wait_ge(sem(f"parts_sent{q}"), 16 * HALVES * n)
                    sp.dma_start(xg[b], rows_dram[bass.ds(at[b], STEP), :].rearrange("(i p) w -> p i w", p=P)
                                 ).then_inc(sem(f"xg_loaded{b}"), 16)

            load_rows(0)
            with sp.Fori(1, STEPS // ROWS_RING) as i:
                load_rows(ROWS_RING * i)

            parts_v = parts_dram.rearrange("(k n p) d -> p k n d", k=TOPK, p=P)

            def load_x2(f, p):
                sp.dma_start(x2_back[p], x2_dram[bass.ds(GT * f, GT), :, :].rearrange("s l d -> l s d")
                             ).then_inc(sem(f"parts_loaded{p}"), 16)

            def load_parts(f, p):
                for k in (2, 3, 0, 1):
                    sp.dma_start(parts[p][:, k, :].rearrange("p (t d) -> p t d", d=D),
                                 parts_v[:, k, bass.ds(GT * f, GT), :]).then_inc(sem(f"parts_loaded{p}"), 16)

            for p in range(2):
                sp.wait_ge(sem(f"x2_stored{p}"), 16 * (GROUPS // 2))
                load_x2(p, p)
            for q in range(Y_RING):
                sp.wait_ge(sem(f"parts_sent{q}"), 16 * HALVES * (STEPS // Y_RING))
            for p in range(2):
                load_parts(p, p)
            with sp.Fori(1, GROUPS // 2) as i:
                for p in range(2):
                    sp.wait_ge(sem("sum"), 3 * (2 * i + p - 1))
                    load_x2(2 * i + p, p)
                    load_parts(2 * i + p, p)
            for p in range(2):
                sp.wait_ge(sem(f"stored{p}"), 16 * (GROUPS // 2))

        @block.gpsimd
        def _(pool):
            pool.memset(ident[:, :], 0.0).then_inc(sem("const0"), 1)
            pool.memset(ident16[:, :], 0.0).then_inc(sem("const0"), 1)
            pool.memset(ones[:, :], 1.0).then_inc(sem("const0"), 1)
            pool.memset(pad_rows[:, :, :], 0.0).then_inc(sem("const0"), 1)
            pool.memset(upto[:, :, :], 1.0).then_inc(sem("const0"), 1)
            c = sem("constants")
            pool.memset(ones16[:, :], 1.0).then_inc(c, 1)
            pool.memset(pair16[:, :], 1.0).then_inc(c, 1)
            pool.memset(minus_half[:, :], -0.5).then_inc(c, 1)
            pool.memset(eps4[:, :], EPS).then_inc(c, 1)
            pool.memset(carry16[1][:, :], 0.0).then_inc(c, 1)
            for p in range(2):
                pool.memset(x_hi[p][:, :, :].bitcast(F32), 0.0).then_inc(c, 1)
                pool.memset(x_lo[p][:, :, :].bitcast(F32), 0.0).then_inc(c, 1)
            pool.iota(iota_e[:, :], [[1, E]], base=0, channel_multiplier=0,
                      allow_small_or_imprecise_dtypes=True).then_inc(c, 1)
            pool.iota(region_of[:, :], [[REGION, E]], base=0, channel_multiplier=0,
                      allow_small_or_imprecise_dtypes=True).then_inc(c, 1)
            pool.iota(dst_of[0][:, :], [[L, GT], [TOKENS, TOPK]], base=0, channel_multiplier=1,
                      allow_small_or_imprecise_dtypes=True).then_inc(c, 1)
            pool.iota(multiples[:, :], [[STEP, MULTIPLES]], base=0, channel_multiplier=0,
                      allow_small_or_imprecise_dtypes=True).then_inc(c, 1)
            pool.iota(step_no[:, :], [[1, STEPS]], base=0, channel_multiplier=0,
                      allow_small_or_imprecise_dtypes=True).then_inc(c, 1)
            pool.wait_ge(sem("const0"), 5)
            for m in (ident, ident16):
                pool.affine_select(out=m[:, :], in_=m[:, :], compare_op=ALU.not_equal, fill=1.0, base=0,
                                   pattern=[[-1, P]], channel_multiplier=1).then_inc(c, 1)
            pool.affine_select(out=causal[:, :], in_=ones[:, :], compare_op=ALU.is_ge, fill=0.0, base=0,
                               pattern=[[1, P]], channel_multiplier=-1).then_inc(c, 1)
            pool.affine_select(out=after_f, in_=ones[:, :], compare_op=ALU.is_gt, fill=0.0, base=0,
                               pattern=[[-1, P]], channel_multiplier=1).then_inc(c, 1)
            pool.affine_select(out=before_f, in_=ones[:, :], compare_op=ALU.is_gt, fill=0.0, base=0,
                               pattern=[[1, P]], channel_multiplier=-1).then_inc(c, 1)
            pool.affine_select(out=upto[:, :, :], in_=upto[:, :, :], compare_op=ALU.is_ge, fill=0.0, base=0,
                               pattern=[[1, E], [-1, E]], channel_multiplier=0).then_inc(c, 1)
            pool.iota(pad_rows[:, :, DST_COL:DST_COL + 1].bitcast(I32), [[0, HALVES]], base=SKIP_DST,
                      channel_multiplier=0).then_inc(c, 1)

            def gate():
                pool.sem_inc(sem("pool_gate"), 1)

            def split_x(g, p):
                wait(pool, "x_hi", g + 1)
                wait(pool, "z_proj", 2 * (g - 1))
                pool.tensor_tensor(x_lo[p][:, :, OFF:OFF + L], xT_g[p][:, :, :],
                                   x_hi[p][:, :, OFF:OFF + L].bitcast(F32), ALU.subtract
                                   ).then_inc(sem("x_lo"), 1)

            def spread_adt(g, p, h):
                wait(pool, "dta_g", g + 1)
                wait(pool, "seg", GT * g + 2 * h)
                gate()
                for n, dst in ((1, adt_hi), (2, adt_lo)):
                    col = dta_g[p][:, n, 2 * HEADS * h:2 * HEADS * (h + 1)]
                    pool.affine_select(out=dst[:, :, :], in_=col.unsqueeze(2).to_broadcast([P, 2 * HEADS, L]),
                                       compare_op=ALU.is_ge, fill=0.0, base=0,
                                       pattern=[[0, 2 * HEADS], [1, L]], channel_multiplier=-1
                                       ).then_inc(sem("adt"), 1)

            def inv_sqrt(n, src, name_in, count, name_out, done_count):
                wait(pool, name_in, count)
                pool.tensor_tensor(var_e[n][:, :], src, eps4[:, :], ALU.add).then_inc(sem(name_out + "_e"), 1)
                wait(pool, name_out + "_e", done_count)
                pool.tensor_tensor(rstd[n][:, :], var_e[n][:, :], minus_half[:, :],
                                   ALU.pow).then_inc(sem(name_out), 1)

            pool.wait_ge(c, N_CONST)
            left_over = rows_dram[E * REGION:E * REGION + STEP, :].rearrange("(i p) w -> p i w", p=P)
            for p in range(2):
                half = slice(p * P // 2, (p + 1) * P // 2)
                pool.dma_start(left_over[half, :, :], pad_rows[half, :, :]).then_inc(sem(f"rows_sent{p}"), 16)

            split_x(0, 0)

            def norm_y(g, p):
                inv_sqrt(2, ss[:, :], "sumsq", GT * (g + 1), "rms", g + 1)

            def norm_a(g, p):
                inv_sqrt(0, mv[0][:, :, 1], "mv0", g + 1, "rstd0", g + 1)

            def norm_b(b, p):
                inv_sqrt(1, mv[1][:, :, 1], "mv1", b + 1, "rstd1", b + 1)

            def send_rows(c_, p, t):
                wait(pool, "pos", c_ + 1)
                wait(pool, "row_copies", c_ + 1)
                wait(pool, "row_w", c_ + 1)
                wait(pool, "row_dst", c_ + 1)
                gate()
                for k in range(TOPK):
                    n = TOPK * t + k
                    pool.indirect_dma_start(rows_dram, bass.IndirectOffsetOnAxis(ap=pos[p][:, n:n + 1], axis=0),
                                            rows[p][:, t, k, :], None).then_inc(sem(f"rows_sent{p}"), 16)

            def rows_of(t):
                return lambda c_, p: send_rows(c_, p, t)

            group_loop(pool, {"split_x": split_x, "adt0": lambda g, p: spread_adt(g, p, 0),
                              "adt1": lambda g, p: spread_adt(g, p, 1), "norm_y": norm_y, "norm_a": norm_a,
                              "norm_b": norm_b} | {f"send{t}": rows_of(t) for t in range(GT)},
                       POOL_SCHEDULE, POOL_TAIL)

            limit = pool.to_reg(TOPK * TOKENS - 1)

            def send_parts(j, b):
                pool.wait_ge(sem("y_scaled"), HALVES * (j + 1))
                gate()
                for i in range(HALVES):
                    dst = xg[b][:, i, DST_COL:DST_COL + 1].bitcast(U32)
                    pool.indirect_dma_start(parts_dram, bass.IndirectOffsetOnAxis(ap=dst, axis=0),
                                            y_s[b % Y_RING][:, i, :], None, bounds_check=limit, oob_is_err=False
                                            ).then_inc(sem(f"parts_sent{b % Y_RING}"), 16)

            with pool.Fori(0, STEPS // ROWS_RING) as i:
                for b in range(ROWS_RING):
                    send_parts(ROWS_RING * i + b, b)

            def pair_sum(f, p):
                pool.wait_ge(sem(f"parts_loaded{p}"), 8 * (TOPK + 1) * (f - p + 2))
                pool.tensor_tensor(parts[p][:, 3, :], parts[p][:, 2, :], parts[p][:, 3, :], ALU.add
                                   ).then_inc(sem("pair_sum"), 1)

            def root(f, p):
                inv_sqrt(p, mv[p][:, :, 1], "mv2", f + 1, "rstd2", f + 1)

            pair_sum(0, 0)
            with pool.Fori(0, GROUPS // 2 - 1) as i:
                for p in range(2):
                    pair_sum(2 * i + p + 1, 1 - p)
                    root(2 * i + p, p)
            pair_sum(GROUPS - 1, 1)
            for f in (GROUPS - 2, GROUPS - 1):
                root(f, f % 2)

        @block.scalar
        def _(act):
            act.dma_start(in_w, in_wT).then_inc(sem("in_w_loaded"), 16)

            def split_x(g, p):
                wait_load(act, f"xT_loaded{p}", g, p)
                wait(act, "z_proj", 2 * (g - 1))
                wait(act, "x_lo", g - 1)
                act.activation(x_hi[p][:, :, OFF:OFF + L], xT_g[p][:, :, :], ACT.Copy).then_inc(sem("x_hi"), 1)

            act.wait_ge(sem("constants"), N_CONST)
            act.wait_ge(sem("mixer_w"), 2)
            act.activation(conv_hi[:, :, :], conv_f, ACT.Copy).then_inc(sem("mixer_high"), 1)
            split_x(0, 0)
            act.wait_ge(sem("mixer_w"), 1)
            act.activation(z_hi[:, :], z_half, ACT.Copy).then_inc(sem("mixer_high"), 1)
            act.wait_ge(sem("dt_prep"), 2)
            act.activation(dtw[:, 2, :], dtw[:, 1, :], ACT.Exp).then_inc(sem("dt_exp"), 1)
            act.activation(a_exp[:, :], alog[:, :], ACT.Exp).then_inc(sem("a_exp"), 1)
            act.wait_ge(sem("dt_prep"), 3)
            act.activation(dtw[:, 4, :], dtw[:, 3, :], ACT.Ln).then_inc(sem("dt_ln"), 1)

            def silu(c):
                def run(g, p):
                    if isinstance(g, int) and g == c == 0:
                        arena_free(act)
                    if c == 0:
                        wait(act, "y", GT * g)
                    wait(act, "conv", 4 * g + c + 1)
                    act.activation(xbc[:, c, :], front[c % 2][:, :], ACT.Identity, bias=convb_half[:, c:c + 1]
                                   ).then_inc(sem("conv_val"), 1)
                    wait(act, "xbc", 4 * g + c - 1)
                    act.activation(th[c % 2], front[c % 2][:, :], ACT.Tanh, bias=convb_half[:, c:c + 1]
                                   ).then_inc(sem("conv_tanh"), 1)
                return run

            def z_tanh(h):
                def run(g, p):
                    wait(act, "gatedT_ps", 2 * g)
                    wait(act, "sumsq", GT * g)
                    wait(act, "z_proj", 2 * g + h + 1)
                    act.activation(z_gate[:, 2 * h:2 * h + 2, :],
                                   front[h][:, :].rearrange("p (t n) -> p t n", t=2), ACT.Tanh
                                   ).then_inc(sem("z_tanh"), 1)
                return run

            def decays(t):
                def run(g, p):
                    wait(act, "seg", GT * g + t + 1)
                    wait(act, "y", GT * g + t - 1)
                    act.activation(decay[t % 2], segs[t % 2][:, :].rearrange("p (h l) -> p h l", h=HEADS),
                                   ACT.Exp).then_inc(sem("decay"), 1)
                return run

            def sum_squares(g, p):
                wait(act, "rms", g)
                for t in range(GT):
                    wait(act, "gated", 2 * g + t // 2 + 1)
                    wait(act, "sumsq", GT * g + t)
                    act.activation(junk, z_gate[:, t, :], ACT.Square, scale=INNER ** -0.5,
                                   accum_out=ss[:, t:t + 1]).then_inc(sem("sumsq"), 1)

            def gate_T(g, p):
                wait(act, "mixed", g)
                for h in range(2):
                    wait(act, "gatedT_ps", 2 * g + h + 1)
                    act.activation(gatedT[:, 2 * h:2 * h + 2, :, :],
                                   mids[1 - h][:, :].rearrange("p (t c l) -> p t c l", t=2, c=2), ACT.Copy
                                   ).then_inc(sem("gatedT"), 1)

            def k_out(b, p):
                wait(act, "k_proj", b + 1)
                wait(act, "scores", b)
                act.activation(kT_s, late[1][:, 0:GT * LC].rearrange("p (t l) -> p t l", t=GT),
                               ACT.Identity, bias=bk_s[:, 0:1]).then_inc(sem("kT"), 1)

            def x1_T(b, p):
                wait(act, "x1T_ps", b + 1)
                wait(act, "q_proj", b)
                act.activation(x1T_s[:, :], late[0][:, :], ACT.Copy).then_inc(sem("x1T"), 1)

            def q_out(b, p):
                wait(act, "q_proj", b + 1)
                wait(act, "scores", b)
                act.activation(qT_s[:, :], late[1][:, :], ACT.Identity, bias=bq_s[:, 0:1]).then_inc(sem("qT"), 1)

            def softmax(b, p):
                wait(act, "neg_max", b + 1)
                wait(act, "probT_ps", b)
                wait(act, "prob_rsum", b)
                for t in range(GT):
                    act.activation(prob[:, t, :], late[0][:, t * LC:(t + 1) * LC], ACT.Exp,
                                   bias=neg_max[:, t:t + 1], accum_out=prob_sum[:, t:t + 1]
                                   ).then_inc(sem("prob"), 1)

            def prob_T(b, p):
                wait(act, "probT_ps", b + 1)
                wait(act, "attended", b)
                act.activation(probT[0:LC, :, :], late[1][0:LC, :].rearrange("p (t l) -> p t l", t=GT),
                               ACT.Copy).then_inc(sem("probT"), 1)

            def x2_T(c, p):
                wait(act, "x2T_ps", c + 1)
                wait(act, "logits", c)
                act.activation(x2T_s[:, :], late[0][:, :], ACT.Copy).then_inc(sem("x2T"), 1)

            def row_high(c, p):
                wait(act, "x2", c + 1)
                act.wait_ge(sem(f"rows_sent{p}"), 8 * GT * TOPK * (c - p) + 16)
                act.activation(rows[p][:, :, 0, 0:D // 2].bitcast(F16), x2[p][:, :, :], ACT.Copy
                               ).then_inc(sem("row_high"), 1)
                act.dma_start(x2_dram[bass.ds(GT * c, GT), :, :].rearrange("s l d -> l s d"), x2[p][:, :, :]
                              ).then_inc(sem(f"x2_stored{p}"), 16)

            def w_high(first):
                def run(c, p):
                    for n in range(2):
                        act.wait_ge(sem(f"w_loaded{n}"), 16 * (2 * c + first // 2 + 1))
                        act.activation(w_half(first, 2 * c + n, 0), w_stage[n][:, :].rearrange(
                            "p (f m) -> p f m", m=P), ACT.Copy, scale=W_SCALE).then_inc(sem("w_high"), 1)
                return run

            def top_exp(c, p):
                wait(act, "top_diff", c + 1)
                wait(act, "row_w", c)
                act.activation(e4[:, :, :], d4[:, :, :], ACT.Exp).then_inc(sem("top_exp"), 1)
                wait(act, "row_low", c + 1)
                act.activation(rows[p][:, :, 1:TOPK, 0:D],
                               rows[p][:, :, 0:1, 0:D].to_broadcast([P, GT, TOPK - 1, D]), ACT.Copy
                               ).then_inc(sem("row_copies"), 1)

            group_loop(act, {"split_x": split_x, "gate_T_out": gate_T, "x2_T_out": x2_T, "row_high": row_high,
                             "k_out": k_out, "top_exp": top_exp, "x1_T_out": x1_T, "q_out": q_out,
                             "softmax": softmax, "prob_T_out": prob_T, "sumsq": sum_squares, "w1_high": w_high(0),
                             "w2_high": w_high(2)}
                       | {f"silu{c}": silu(c) for c in range(4)} | {f"z_tanh{h}": z_tanh(h) for h in range(2)}
                       | {f"decay{t}": decays(t) for t in range(GT)})

            def gelus(j, b, ex):
                p = b % 2
                wait(act, "hid_low", 2 * (j - 1))
                for f in range(NF):
                    act.wait_ge(sem("up"), 2 * j + f // 2 + 1)
                    hb = banks[2 + 2 * p + f // 2]
                    act.activation(hid[p][:, f, :], hb[:, (f % 2) * STEP:(f % 2 + 1) * STEP], ACT.Gelu,
                                   bias=b1_s[:, bass.ds(ex, 1), f:f + 1].rearrange("p e f -> p (e f)"),
                                   scale=1.0 / W_SCALE).then_inc(sem("hidden"), 1)
                    if f % 2:
                        if f == 1:
                            wait(act, "down", j - HID_RING + 1)
                        act.wait_ge(sem("hidden"), NF * j + f + 1)
                        act.activation(hid16[b % HID_RING][:, f - 1:f + 1, 0, :], hid[p][:, f - 1:f + 1, :], ACT.Copy
                                       ).then_inc(sem("hid_high"), 1)

            def gelu_steps(first):
                ex = read_plan(step_e, first, ROWS_RING, ACTE, E - 1)
                for b in range(ROWS_RING):
                    gelus(first + b, b, ex[b])

            pad_experts(act, ACTE, E // 2)
            act.wait_ge(sem("plan"), N_PLAN)
            gelu_steps(0)
            with act.Fori(1, STEPS // ROWS_RING) as i:
                gelu_steps(ROWS_RING * i)

            def norm_out(f, p):
                act.wait_ge(sem("neg_mean"), f + 1)
                if not isinstance(f, int) or f >= 2:
                    act.wait_ge(sem(f"stored{p}"), 8 * (f - p))
                for t in range(GT):
                    ins = act.activation(y_out[p][:, t, :], total[p][:, t, :], ACT.Identity,
                                         scale=rstd[p][:, t:t + 1], bias=neg_mean[p][:, t:t + 1])
                ins.then_inc(sem("normed"), 1)
                act.wait_ge(sem("normed"), f + 1)
                act.dma_start(out[bass.ds(GT * f, GT), :, :].rearrange("s l d -> l s d"), y_out[p]
                              ).then_inc(sem(f"stored{p}"), 16)

            for f in range(2):
                norm_out(f, f)
            with act.Fori(1, GROUPS // 2) as i:
                for p in range(2):
                    norm_out(2 * i + p, p)

        @block.vector
        def _(dve):
            v = nc.vector
            dve.wait_ge(sem("in_w_loaded"), 16)
            dve.wait_ge(sem("conv_w_loaded"), 16)
            v.tensor_scalar(z_half, in_w[:, 0:INNER], 0.5, None, ALU.mult).then_inc(sem("mixer_w"), 1)
            v.scalar_tensor_tensor(conv_f, conv_wb, 0.5, in_w[:, INNER:INNER + CONV].unsqueeze(1).to_broadcast(
                [P, TAPS, CONV]), ALU.mult, ALU.mult).then_inc(sem("mixer_w"), 1)
            dve.wait_ge(sem("constants"), N_CONST)
            v.tensor_copy(after[:, :], after_f).then_inc(sem("masks"), 1)
            v.tensor_copy(before16[:, :], before_f).then_inc(sem("masks"), 1)
            dve.wait_ge(sem("mixer_high"), 1)
            v.tensor_tensor(conv_lo[:, :, :], conv_f, conv_hi[:, :, :].bitcast(F32), ALU.subtract
                            ).then_inc(sem("mixer_low"), 1)
            dve.wait_ge(sem("mixer_high"), 2)
            v.tensor_tensor(z_lo[:, :], z_half, z_hi[:, :].bitcast(F32), ALU.subtract).then_inc(sem("mixer_low"), 1)
            dve.wait_ge(sem("weights"), 16 * N_WEIGHTS)
            s = sem("scaled")
            v.tensor_scalar(convb_half[:, :], convb[:, :], 0.5, None, ALU.mult).then_inc(s, 1)
            for c in range(2):
                v.tensor_scalar(out_wn[:, c, :], out_w[:, c, :], normw[:, c:c + 1], None, ALU.mult).then_inc(s, 1)
                v.tensor_scalar(d_diag[:, c, :], ident[:, :], dcol[:, c:c + 1], None, ALU.mult).then_inc(s, 1)
            v.tensor_scalar(wv_n[:, :], wv_s, NORM_FACT, None, ALU.mult).then_inc(s, 1)
            v.tensor_scalar(bv_n[:, :], bv_s, NORM_FACT, None, ALU.mult).then_inc(s, 1)
            v.scalar_tensor_tensor(route_w[:, :], keys_s[:, :], 2.0, rw_s[:, :], ALU.mult, ALU.add).then_inc(s, 1)
            v.tensor_tensor(keys_sq[:, :], keys_s[:, :], keys_s[:, :], ALU.mult).then_inc(sem("keys_sq"), 1)
            dve.wait_ge(sem("dt_proj"), 1)
            dtv = late[0][:, 0:SEQS * HEADS].rearrange("p (s h) -> p s h", h=HEADS)
            dt3 = dtw.rearrange("p n (s h) -> p n s h", h=HEADS)
            v.tensor_tensor(dt3[:, 0, :, :], dtv, dtb[:, :].unsqueeze(1).to_broadcast([P, SEQS, HEADS]), ALU.add
                            ).then_inc(sem("dt_prep"), 1)
            dve.wait_ge(sem("dt_prep"), 1)
            v.scalar_tensor_tensor(dtw[:, 1, :], dtw[:, 0, :], -1.0, dtw[:, 0, :], ALU.mult, ALU.min
                                   ).then_inc(sem("dt_prep"), 1)
            dve.wait_ge(sem("dt_exp"), 1)
            v.tensor_scalar(dtw[:, 3, :], dtw[:, 2, :], 1.0, None, ALU.add).then_inc(sem("dt_prep"), 1)
            dve.wait_ge(sem("dt_prep"), 3)
            v.tensor_scalar(dtw[:, 5, :], dtw[:, 3, :], -1.0, None, ALU.add).then_inc(sem("dt_log"), 1)
            dve.wait_ge(sem("dt_log"), 1)
            v.scalar_tensor_tensor(dtw[:, 6, :], dtw[:, 5, :], 0.0, dtw[:, 2, :], ALU.is_equal, ALU.mult
                                   ).then_inc(sem("dt_log"), 1)
            v.tensor_scalar(dtw[:, 7, :], dtw[:, 5, :], 1e-30, None, ALU.max).then_inc(sem("dt_log"), 1)
            dve.wait_ge(sem("dt_log"), 3)
            v.reciprocal(dtw[:, 5, :], dtw[:, 7, :]).then_inc(sem("dt_log"), 1)
            dve.wait_ge(sem("dt_log"), 4)
            v.tensor_tensor(dtw[:, 7, :], dtw[:, 5, :], dtw[:, 2, :], ALU.mult).then_inc(sem("dt_log"), 1)
            dve.wait_ge(sem("dt_log"), 5)
            dve.wait_ge(sem("dt_ln"), 1)
            v.tensor_tensor(dtw[:, 5, :], dtw[:, 7, :], dtw[:, 4, :], ALU.mult).then_inc(sem("dt_log"), 1)
            dve.wait_ge(sem("dt_log"), 6)
            v.tensor_tensor(dtw[:, 7, :], dtw[:, 5, :], dtw[:, 6, :], ALU.add).then_inc(sem("dt_log"), 1)
            dve.wait_ge(sem("dt_log"), 7)
            v.scalar_tensor_tensor(dta[:, 0, :], dtw[:, 0, :], 0.0, dtw[:, 7, :], ALU.max, ALU.add
                                   ).then_inc(sem("dt_split"), 1)
            dve.wait_ge(sem("dt_split"), 1)
            dve.wait_ge(sem("a_exp"), 1)
            v.scalar_tensor_tensor(dt3[:, 1, :, :], dta[:, 0, :].rearrange("p (s h) -> p s h", h=HEADS), -1.0,
                                   a_exp[:, :].unsqueeze(1).to_broadcast([P, SEQS, HEADS]), ALU.mult, ALU.mult
                                   ).then_inc(sem("adt_full"), 1)
            dve.wait_ge(sem("adt_full"), 1)
            v.tensor_copy(dta[:, 1, :].bitcast(F32R), dtw[:, 1, :]).then_inc(sem("dt_split"), 1)
            dve.wait_ge(sem("dt_split"), 2)
            v.tensor_tensor(dta[:, 2, :].bitcast(F32R), dtw[:, 1, :], dta[:, 1, :], ALU.subtract
                            ).then_inc(sem("dt_split"), 1)
            dve.wait_ge(sem("b2_loaded"), 16)
            b2_hi = b2_16[0:1, :, :].rearrange("p e d -> p (e d)")
            v.tensor_scalar(b2_hi, b2_stage, W_SCALE, None, ALU.mult).then_inc(sem("b2_high"), 1)
            dve.wait_ge(sem("b2_high"), 1)
            v.scalar_tensor_tensor(b2_lo, b2_stage, W_SCALE, b2_hi, ALU.mult, ALU.subtract).then_inc(sem("b2_low"), 1)

            def group_dt(g, p):
                wait(dve, "adt", 4 * (g - 1))
                v.tensor_copy(dta_g[p][:, :, :], dta[:, :, bass.ds(GT * HEADS * g, GT * HEADS)]
                              ).then_inc(sem("dta_g"), 1)

            def silu(c):
                def run(g, p):
                    wait(dve, "conv_tanh", 4 * g + c + 1)
                    v.scalar_tensor_tensor(xbc[:, c, :], th[c % 2], 1.0, xbc[:, c, :], ALU.add, ALU.mult
                                           ).then_inc(sem("xbc"), 1)
                return run

            def z_gates(h):
                def run(g, p):
                    wait(dve, "z_tanh", 2 * g + h + 1)
                    zz = z_gate[:, 2 * h:2 * h + 2, :].rearrange("p t n -> p (t n)")
                    v.scalar_tensor_tensor(zz, zz, 1.0, front[h][:, :], ALU.add, ALU.mult
                                           ).then_inc(sem("z_gate"), 1)
                return run

            def times_dt(g, p):
                if isinstance(g, int) and g == 0:
                    dve.wait_ge(sem("keys_norm"), 1)
                    v.tensor_tensor(route_b[:, :], rb_s[:, :], late[1][:, 0:E], ALU.subtract
                                    ).then_inc(sem("route_b"), 1)
                wait(dve, "dta_g", g + 1)
                wait(dve, "y", GT * g)
                for h in range(2):
                    wait(dve, "x_turned", 2 * g + h + 1)
                    dtc = dta_g[p][:, 0, 2 * HEADS * h:2 * HEADS * (h + 1)]
                    v.tensor_tensor(xdt[:, 2 * h:2 * h + 2, :].rearrange("p t (h n) -> p (t h) n", n=HD),
                                    front[h][:, :].rearrange("p (a n) -> p a n", n=HD),
                                    dtc.unsqueeze(2).to_broadcast([P, 2 * HEADS, HD]), ALU.mult
                                    ).then_inc(sem("xdt"), 1)

            def mask_cb(g, p):
                wait(dve, "cb", g + 1)
                v.tensor_tensor(cb_masked, mids[0][:, :].rearrange("p (t l) -> p t l", t=GT),
                                causal[:, :].unsqueeze(1).to_broadcast([P, GT, L]), ALU.mult
                                ).then_inc(sem("cb_masked"), 1)

            def mix(t):
                def run(g, p):
                    wait(dve, "cb_masked", g + 1)
                    wait(dve, "decay", GT * g + t + 1)
                    v.tensor_tensor(decay[t % 2], decay[t % 2],
                                    cb_masked[:, t:t + 1, :].to_broadcast([P, HEADS, L]), ALU.mult
                                    ).then_inc(sem("mix"), 1)
                return run

            def gates(h):
                def run(g, p):
                    wait(dve, "y", GT * g + 2 * h + 2)
                    wait(dve, "z_gate", 2 * g + h + 1)
                    zz = z_gate[:, 2 * h:2 * h + 2, :].rearrange("p t n -> p (t n)")
                    v.tensor_tensor(zz, mids[1 - h][:, :], zz, ALU.mult).then_inc(sem("gated"), 1)
                return run

            def moments(n, g, res, res_name):
                for t in range(GT):
                    wait(dve, res_name, GT * g + t + 1)
                    v.bn_stats(stats[n][:, t, :], res[:, t, :]).then_inc(sem(f"stats{n}"), 1)
                wait(dve, f"stats{n}", GT * (g + 1))
                wait(dve, f"rstd{n}_e", g)
                dve.sem_inc(sem("dve_gate"), 1)
                for t in range(GT):
                    ins = v.bn_aggr(mv[n][:, t, :], stats[n][:, t, :])
                ins.then_inc(sem(f"mv{n}"), 1)

            def normalise(n, g, res, out_of, out_name):
                wait(dve, f"mv{n}", g + 1)
                wait(dve, f"rstd{n}", g + 1)
                for t in range(GT):
                    ins = v.tensor_scalar(out_of[:, t, :], res[:, t, :], mv[n][:, t, 0:1], rstd[n][:, t:t + 1],
                                          ALU.subtract, ALU.mult)
                ins.then_inc(sem(out_name), 1)

            def residual1(g, p):
                wait(dve, "mixed", g + 1)
                wait(dve, "rms", g + 1)
                wait_load(dve, f"x_loaded{p}", g, p)
                for t in range(GT):
                    v.scalar_tensor_tensor(res1[:, t, :], mids[1][:, t * D:(t + 1) * D], rstd[2][:, t:t + 1],
                                           x_tok[p][:, t, :], ALU.mult, ALU.add).then_inc(sem("res1"), 1)
                moments(0, g, res1, "res1")

            def norm0(g, p):
                wait(dve, "x1T_ps", g - 1)
                wait(dve, "res2", GT * (g - 1))
                normalise(0, g, res1, x1[p], "x1")

            def v_out(b, p):
                wait(dve, "v_proj", b + 1)
                wait(dve, "attended", b)
                v.tensor_tensor(v_s[0:LC, :, :], late[0][0:LC, :].rearrange("p (t d) -> p t d", t=GT),
                                bv_n[0:LC, :].unsqueeze(1).to_broadcast([LC, GT, D]), ALU.add
                                ).then_inc(sem("v"), 1)

            def row_max(b, p):
                wait(dve, "scores", b + 1)
                wait(dve, "prob", GT * b)
                v.tensor_reduce(neg_max[:, :], late[0][:, 0:GT * LC].rearrange("p (t l) -> p t l", t=GT),
                                AX_X, ALU.max, negate=True).then_inc(sem("neg_max"), 1)

            def residual2(b, p):
                wait(dve, "prob", GT * (b + 1))
                wait(dve, "res2", GT * b)
                v.reciprocal(prob_rsum[:, :], prob_sum[:, :]).then_inc(sem("prob_rsum"), 1)
                wait(dve, "attended", b + 1)
                wait(dve, "prob_rsum", b + 1)
                wait(dve, "x1", b + 1)
                for t in range(GT):
                    v.scalar_tensor_tensor(res2[:, t, :], late[0][:, t * D:(t + 1) * D], prob_rsum[:, t:t + 1],
                                           x1[p][:, t, :], ALU.mult, ALU.add).then_inc(sem("res2"), 1)
                moments(1, b, res2, "res2")

            def norm1(b, p):
                if not isinstance(b, int) or b >= 2:
                    dve.wait_ge(sem(f"x2_stored{p}"), 8 * (b - p))
                wait(dve, "x2T_ps", b - 1)
                wait(dve, "row_low", b - 1)
                wait(dve, "row_high", b - 1)
                normalise(1, b, res2, x2[p], "x2")

            def w_low(first):
                def run(c, p):
                    for n in range(2):
                        wait(dve, "w_high", 4 * c + first + n + 1)
                        v.scalar_tensor_tensor(w_half(first, 2 * c + n, 1), w_stage[n][:, :].rearrange(
                            "p (f m) -> p f m", m=P), W_SCALE, w_half(first, 2 * c + n, 0), ALU.mult, ALU.subtract
                                               ).then_inc(sem("w_low"), 1)
                return run

            def top_experts(c, p):
                wait(dve, "logits", c + 1)
                v.tensor_tensor(logit[:, :, :], late[1][:, 0:GT * E].rearrange("p (t e) -> p t e", t=GT),
                                route_b[:, :].unsqueeze(1).to_broadcast([P, GT, E]), ALU.add
                                ).then_inc(sem("logit"), 1)
                wait(dve, "row_high", c + 1)
                v.tensor_tensor(rows[p][:, :, 0, D // 2:D].bitcast(F16), x2[p][:, :, :],
                                rows[p][:, :, 0, 0:D // 2].bitcast(F16), ALU.subtract
                                ).then_inc(sem("row_low"), 1)
                wait(dve, "logit", c + 1)
                dve.sem_inc(sem("dve_gate"), 1)
                for t in range(GT):
                    ins = v.max(top8[:, t, :], logit[:, t, :])
                ins.then_inc(sem("top8"), 1)
                wait(dve, "top8", c + 1)
                dve.sem_inc(sem("dve_gate"), 1)
                for t in range(GT):
                    ins = v.max_index(idx8[:, t, :], top8[:, t, :], logit[:, t, :])
                ins.then_inc(sem("idx8"), 1)
                v.tensor_tensor(d4[:, :, :], top8[:, :, 0:TOPK], top8[:, :, 0:1].to_broadcast([P, GT, TOPK]),
                                ALU.subtract).then_inc(sem("top_diff"), 1)

            def chosen(c, p):
                wait(dve, "idx8", c + 1)
                v.tensor_copy(idx_f[:, :, :], idx8[:, :, 0:TOPK]).then_inc(sem("choice"), 1)
                wait(dve, "dst_next", c)
                v.tensor_scalar(rows[p][:, :, :, DST_COL].bitcast(U32),
                                dst_of[p][:, :].rearrange("p (t k) -> p t k", k=TOPK), 0.0, None, ALU.add
                                ).then_inc(sem("row_dst"), 1)
                v.tensor_scalar(dst_of[1 - p][:, :], dst_of[p][:, :], float(GTOK), None, ALU.add
                                ).then_inc(sem("dst_next"), 1)
                wait(dve, "choice", 2 * c + 1)
                v.tensor_tensor(onehot[:, :, :],
                                idx_f[:, :, :].rearrange("p t k -> p (t k)").unsqueeze(2).to_broadcast(
                                    [P, GT * TOPK, E]),
                                iota_e[:, :].unsqueeze(1).to_broadcast([P, GT * TOPK, E]), ALU.is_equal
                                ).then_inc(sem("choice"), 1)
                wait(dve, "choice", 2 * c + 2)
                wait(dve, "ranks", c)
                with nc.allow_low_precision(reason="zeros and ones"):
                    v.tensor_reduce(picked[:, :, :], onehot[:, :, :].rearrange("p (t k) e -> p t e k", t=GT),
                                    AX_X, ALU.add).then_inc(sem("picked"), 1)

            def weights(c, p):
                wait(dve, "top_exp", c + 1)
                v.tensor_reduce(s4[:, :], e4[:, :, :], AX_X, ALU.add).then_inc(sem("top_norm"), 1)
                wait(dve, "picked", c + 1)
                v.tensor_reduce(group_n[:, :], picked[:, :, :].rearrange("p t e -> p e t"), AX_X, ALU.add
                                ).then_inc(sem("group_n"), 1)
                wait(dve, "top_norm", 2 * c + 1)
                v.reciprocal(r4[:, :], s4[:, :]).then_inc(sem("top_norm"), 1)
                wait(dve, "group_n", c + 1)
                v.tensor_tensor(carry16[p][:, :], carry16[1 - p][:, :], group_n[:, :], ALU.add
                                ).then_inc(sem("carry"), 1)
                wait(dve, "top_norm", 2 * c + 2)
                v.scalar_tensor_tensor(rows[p][:, :, :, W_COL], e4[:, :, :], 1.0 / W_SCALE,
                                       r4[:, :].unsqueeze(2).to_broadcast([P, GT, TOPK]), ALU.mult, ALU.mult
                                       ).then_inc(sem("row_w"), 1)

            def slots(c, p):
                wait(dve, "ranks", c + 1)
                v.tensor_tensor(slot[:, :, :], late[1][:, 0:GT * E].rearrange("p (t e) -> p t e", t=GT),
                                region_of[:, :].unsqueeze(1).to_broadcast([P, GT, E]), ALU.add
                                ).then_inc(sem("slot"), 1)

            def positions(c, p):
                wait(dve, "slot", c + 1)
                v.tensor_tensor(onehot[:, :, :].rearrange("p (t k) e -> p t k e", t=GT),
                                onehot[:, :, :].rearrange("p (t k) e -> p t k e", t=GT),
                                slot[:, :, :].unsqueeze(2).to_broadcast([P, GT, TOPK, E]), ALU.mult
                                ).then_inc(sem("place"), 1)
                wait(dve, "place", 2 * c + 1)
                v.tensor_reduce(pos_f[:, :], onehot[:, :, :], AX_X, ALU.add).then_inc(sem("place"), 1)
                wait(dve, "place", 2 * c + 2)
                v.tensor_copy(pos[p][:, :], pos_f[:, :]).then_inc(sem("pos"), 1)

            group_loop(dve, {"dt": group_dt, "xdt": times_dt, "cb_masked": mask_cb, "res1": residual1,
                             "norm0": norm0, "v_out": v_out, "neg_max": row_max, "res2": residual2,
                             "norm1": norm1, "w1_low": w_low(0), "w2_low": w_low(2), "top": top_experts,
                             "chosen": chosen,
                             "weight": weights, "slots": slots, "positions": positions}
                       | {f"xbc{c}": silu(c) for c in range(4)} | {f"z_gate{h}": z_gates(h) for h in range(2)}
                       | {f"mix{t}": mix(t) for t in range(GT)} | {f"gate{h}": gates(h) for h in range(2)})

            plan, n_plan = sem("plan"), [0]

            def planned(ins):
                ins.then_inc(plan, 1)
                n_plan[0] += 1
                dve.wait_ge(plan, n_plan[0])

            dve.wait_ge(sem("counts"), 1)
            planned(v.tensor_copy(cnt[:, :], banks[0][0:1, 0:E]))
            planned(v.tensor_tensor(pad_f[:, :], cnt[:, :], region_of[0:1, :], ALU.add))
            planned(v.tensor_copy(pad_at[:, :], pad_f[:, :]))
            assert n_plan[0] == PADS_PLANNED
            planned(v.tensor_tensor(over[:, :, :], cnt[:, :].unsqueeze(2).to_broadcast([1, E, MULTIPLES]),
                                    multiples[:, :].unsqueeze(1).to_broadcast([1, E, MULTIPLES]), ALU.is_gt))
            planned(v.tensor_reduce(n_steps[:, :], over[:, :, :], AX_X, ALU.add))
            planned(v.tensor_tensor(before_e[:, :, :], n_steps[:, :].unsqueeze(1).to_broadcast([1, E, E]),
                                    upto[:, :, :], ALU.mult))
            planned(v.tensor_reduce(last_step[:, :], before_e[:, :, :], AX_X, ALU.add))
            planned(v.tensor_tensor(done[:, :, :], last_step[:, :].unsqueeze(1).to_broadcast([1, STEPS, E]),
                                    step_no[:, :].unsqueeze(2).to_broadcast([1, STEPS, E]), ALU.is_le))
            planned(v.tensor_reduce(step_ef[:, :], done[:, :, :], AX_X, ALU.add))
            planned(v.tensor_tensor(done[:, :, :], done[:, :, :],
                                    n_steps[:, :].unsqueeze(1).to_broadcast([1, STEPS, E]), ALU.mult))
            planned(v.tensor_reduce(steps_before[:, :], done[:, :, :], AX_X, ALU.add))
            planned(v.tensor_tensor(row_f[:, :], step_no[:, :], steps_before[:, :], ALU.subtract))
            planned(v.tensor_scalar(row_f[:, :], row_f[:, :], float(STEP), None, ALU.mult))
            planned(v.scalar_tensor_tensor(row_f[:, :], step_ef[:, :], float(REGION), row_f[:, :],
                                           ALU.mult, ALU.add))
            planned(v.tensor_scalar(step_row[:, :], row_f[:, :], float(E * REGION), None, ALU.min))
            planned(v.tensor_scalar(step_e[:, :], step_ef[:, :], float(E - 1), None, ALU.min))
            assert n_plan[0] == N_PLAN

            def turned(j, p):
                dve.wait_ge(sem("rows_turned"), j + 1)
                wait(dve, "up", 2 * (j - 1))
                v.tensor_copy(xgT[p], turn_ps[p]).then_inc(sem("xgT"), 1)

            def hid_lows(j, b):
                for n in range(2):
                    fs = slice(2 * n, 2 * n + 2)
                    dve.wait_ge(sem("hid_high"), 2 * j + n + 1)
                    v.tensor_tensor(hid16[b % HID_RING][:, fs, 1, :], hid[b % 2][:, fs, :],
                                    hid16[b % HID_RING][:, fs, 0, :], ALU.subtract).then_inc(sem("hid_low"), 1)

            def scaled(j, b):
                y, both = y_s[b % Y_RING], banks[6 + b % 2][:, :].rearrange("p (i a d) -> p i a d", i=HALVES, a=2)
                q = b % Y_RING
                if not isinstance(j, int) or j >= Y_RING:
                    dve.wait_ge(sem(f"parts_sent{q}"), 16 * HALVES // Y_RING * (j - q))
                dve.wait_ge(sem("down"), j + 1)
                for i in range(HALVES):
                    v.tensor_scalar(y[:, i, :], both[:, i, 0, :], xg[b][:, i, W_COL:W_COL + 1], None, ALU.mult
                                    ).then_inc(sem("y_high"), 1)
                for i in range(HALVES):
                    dve.wait_ge(sem("y_high"), HALVES * j + i + 1)
                    v.scalar_tensor_tensor(y[:, i, :], both[:, i, 1, :], xg[b][:, i, W_COL:W_COL + 1], y[:, i, :],
                                           ALU.mult, ALU.add).then_inc(sem("y_scaled"), 1)

            def step(j, b):
                turned(j, b % 2)
                if not isinstance(j, int) or j >= 2:
                    hid_lows(j - 2, (b - 2) % ROWS_RING)
                if not isinstance(j, int) or j >= 3:
                    scaled(j - 3, (b - 3) % ROWS_RING)

            for j in range(ROWS_RING):
                step(j, j)
            with dve.Fori(1, STEPS // ROWS_RING) as i:
                for b in range(ROWS_RING):
                    step(ROWS_RING * i + b, b)
            for j in (STEPS - 2, STEPS - 1):
                hid_lows(j, j % ROWS_RING)
            for j in (STEPS - 3, STEPS - 2, STEPS - 1):
                scaled(j, j % ROWS_RING)

            def sum_parts(f, p):
                dve.wait_ge(sem(f"parts_loaded{p}"), 8 * (TOPK + 1) * (f - p + 2))
                tot = total[p].rearrange("p t d -> p (t d)")
                if not isinstance(f, int) or f >= 2:
                    dve.wait_ge(sem("normed"), f - 1)
                v.tensor_tensor(tot, x2_back[p].rearrange("p t d -> p (t d)"), parts[p][:, 0, :], ALU.add
                                ).then_inc(sem("sum"), 1)
                dve.wait_ge(sem("sum"), 3 * f + 1)
                v.tensor_tensor(tot, tot, parts[p][:, 1, :], ALU.add).then_inc(sem("sum"), 1)
                dve.wait_ge(sem("pair_sum"), f + 1)
                dve.wait_ge(sem("sum"), 3 * f + 2)
                v.tensor_tensor(tot, tot, parts[p][:, 3, :], ALU.add).then_inc(sem("sum"), 1)

            def moments_of(f, p):
                dve.wait_ge(sem("sum"), 3 * f + 3)
                for t in range(GT):
                    v.bn_stats(stats[p][:, t, :], total[p][:, t, :]).then_inc(sem("stats2"), 1)
                dve.wait_ge(sem("stats2"), GT * (f + 1))
                dve.sem_inc(sem("dve_gate"), 1)
                for t in range(GT):
                    ins = v.bn_aggr(mv[p][:, t, :], stats[p][:, t, :])
                ins.then_inc(sem("mv2"), 1)

            def neg_means(f, p):
                dve.wait_ge(sem("mv2"), f + 1)
                dve.wait_ge(sem("rstd2"), f + 1)
                if not isinstance(f, int) or f >= 2:
                    dve.wait_ge(sem("normed"), f - 1)
                v.scalar_tensor_tensor(neg_mean[p][:, :], mv[p][:, :, 0], -1.0, rstd[p][:, :], ALU.mult, ALU.mult
                                       ).then_inc(sem("neg_mean"), 1)

            def summed(f, p):
                sum_parts(f, p)
                if not isinstance(f, int) or f >= 1:
                    neg_means(f - 1, 1 - p)
                moments_of(f, p)

            for f in range(4):
                summed(f, f % 2)
            with dve.Fori(2, GROUPS // 2) as i:
                for p in range(2):
                    summed(2 * i + p, p)
            neg_means(GROUPS - 1, (GROUPS - 1) % 2)

        @block.tensor
        def _(pe):
            mm = nc.tensor.matmul

            def three(ps, lhi, llo, rhi, rlo, start=True, stop=True):
                mm(ps, lhi, rlo, start=start, stop=False)
                mm(ps, llo, rhi, start=False, stop=False)
                return mm(ps, lhi, rhi, start=False, stop=stop)

            pe.wait_ge(sem("xT_loaded"), 64)
            pe.wait_ge(sem("in_w_loaded"), 16)
            for n in range(SEQS):
                ins = mm(late[0][:, HEADS * n:HEADS * (n + 1)], xT_all[:, n, :], in_w[:, INNER + CONV:],
                         start=True, stop=True)
            ins.then_inc(sem("dt_proj"), 1)
            pe.wait_ge(sem("mixer_low"), 2)

            def conv(c):
                def run(g, p):
                    if c == 0:
                        wait(pe, "x_hi", g + 1)
                        wait(pe, "x_lo", g + 1)
                    if c < 2:
                        wait(pe, "xdt", 2 * (g - 1) + c + 1)
                    else:
                        wait(pe, "conv_tanh", 4 * g + c - 1)
                    ps = front[c % 2][:, :]
                    w = slice(c * P, (c + 1) * P)
                    for j in range(TAPS):
                        ins = three(ps, conv_hi[:, j, w], conv_lo[:, j, w], x_hi[p][:, :, j:j + L],
                                    x_lo[p][:, :, j:j + L], start=(j == 0), stop=(j == TAPS - 1))
                    ins.then_inc(sem("conv"), 1)
                return run

            def z_proj(h):
                def run(g, p):
                    wait(pe, "conv_tanh", 4 * g + 3 + h)
                    for t in (2 * h, 2 * h + 1):
                        ins = three(front[h][:, (t % 2) * INNER:(t % 2 + 1) * INNER],
                                    x_hi[p][:, t, OFF:OFF + L], x_lo[p][:, t, OFF:OFF + L],
                                    z_hi[:, :], z_lo[:, :])
                    ins.then_inc(sem("z_proj"), 1)
                return run

            def turn_x(g, p):
                if isinstance(g, int) and g == 0:
                    pe.wait_ge(sem("keys_sq"), 1)
                    mm(late[1][:, 0:E], ones[:, :], keys_sq[:, :], start=True,
                       stop=True).then_inc(sem("keys_norm"), 1)
                    arena_free(pe)
                wait(pe, "xbc", 4 * g + 2)
                for h in range(2):
                    wait(pe, "z_gate", 2 * g + h + 1)
                    for t in (2 * h, 2 * h + 1):
                        for c in range(2):
                            at = (t % 2) * INNER + c * P
                            ins = nc.tensor.transpose(front[h][:, at:at + P], xbc[:, c, t * L:(t + 1) * L],
                                                      ident[:, :])
                    ins.then_inc(sem("x_turned"), 1)

            def segments(t):
                def run(g, p):
                    wait(pe, "adt", 4 * g + 2 * (t // 2) + 2)
                    wait(pe, "decay", GT * g + t - 1)
                    hs = slice(HEADS * (t % 2), HEADS * (t % 2 + 1))
                    mm(segs[t % 2][:, :], after[:, :], adt_hi[:, hs, :], start=True, stop=False)
                    mm(segs[t % 2][:, :], after[:, :], adt_lo[:, hs, :], start=False, stop=True
                       ).then_inc(sem("seg"), 1)
                return run

            def pair_products(g, p):
                wait(pe, "xbc", 4 * g + 4)
                wait(pe, "gatedT", 2 * g)
                for t in range(GT):
                    ts = slice(t * L, (t + 1) * L)
                    ins = mm(mids[0][:, ts], xbc[:, 2, ts], xbc[:, 3, ts], start=True, stop=True)
                ins.then_inc(sem("cb"), 1)

            def outputs(t):
                def run(g, p):
                    wait(pe, "xdt", 2 * g + t // 2 + 1)
                    if t == 0:
                        wait(pe, "res1", GT * g)
                    if t == 2:
                        wait(pe, "cb_masked", g + 1)
                    wait(pe, "mix", GT * g + t + 1)
                    ps = mids[1 - t // 2]
                    for c in range(2):
                        at = (t % 2) * INNER + c * P
                        mm(ps[:, at:at + P], xbc[:, c, t * L:(t + 1) * L], d_diag[:, c, :], start=True, stop=False)
                        for h in (2 * c, 2 * c + 1):
                            at = (t % 2) * INNER + h * HD
                            ins = mm(ps[:, at:at + HD], decay[t % 2][:, h, :], xdt[:, t, h * HD:(h + 1) * HD],
                                     start=False, stop=(h == 2 * c + 1))
                    ins.then_inc(sem("y"), 1)
                return run

            def gate_T(h):
                def run(g, p):
                    wait(pe, "gated", 2 * g + h + 1)
                    for t in (2 * h, 2 * h + 1):
                        for c in range(2):
                            at = (t % 2) * INNER + c * P
                            ins = nc.tensor.transpose(mids[1 - h][:, at:at + P], z_gate[:, t, c * P:(c + 1) * P],
                                                      ident[:, :])
                    ins.then_inc(sem("gatedT_ps"), 1)
                return run

            def mixed(g, p):
                wait(pe, "gatedT", 2 * g + 2)
                for t in range(GT):
                    for c in range(2):
                        ins = mm(mids[1][:, t * D:(t + 1) * D], gatedT[:, t, c, :], out_wn[:, c, :],
                                 start=(c == 0), stop=(c == 1))
                ins.then_inc(sem("mixed"), 1)

            def k_proj(b, p):
                wait_load(pe, f"ctx_loaded{p}", b, p)
                pe.wait_ge(sem("route_b"), 1)
                wait(pe, "logit", b)
                mm(late[1][:, 0:GT * LC], wk_s[:, :], ctx_s[p][:, :, 0:LC], start=True, stop=True
                   ).then_inc(sem("k_proj"), 1)

            def v_proj(b, p):
                wait(pe, "x2T", b)
                for t in range(GT):
                    ins = mm(late[0][0:LC, t * D:(t + 1) * D], ctx_s[p][:, t, 0:LC], wv_n[:, :],
                             start=True, stop=True)
                ins.then_inc(sem("v_proj"), 1)

            def x1_T(b, p):
                wait(pe, "x1", b + 1)
                wait(pe, "v", b + 1)
                for t in range(GT):
                    ins = nc.tensor.transpose(late[0][:, t * L:(t + 1) * L], x1[p][:, t, :], ident[:, :])
                ins.then_inc(sem("x1T_ps"), 1)

            def q_proj(b, p):
                wait(pe, "slot", b)
                wait(pe, "kT", b + 1)
                wait(pe, "x1T", b + 1)
                mm(late[1][:, :], wq_s[:, :], x1T_s[:, :], start=True, stop=True).then_inc(sem("q_proj"), 1)

            def scores(b, p):
                wait(pe, "qT", b + 1)
                for t in range(GT):
                    ins = mm(late[0][:, t * LC:(t + 1) * LC], qT_s[:, t * L:(t + 1) * L], kT_s[:, t, :],
                             start=True, stop=True)
                ins.then_inc(sem("scores"), 1)

            def prob_T(b, p):
                wait(pe, "prob", GT * (b + 1))
                for t in range(GT):
                    ins = nc.tensor.transpose(late[1][0:LC, t * L:(t + 1) * L], prob[:, t, :], ident[:, :])
                ins.then_inc(sem("probT_ps"), 1)

            def attended(b, p):
                wait(pe, "probT", b + 1)
                for t in range(GT):
                    ins = mm(late[0][:, t * D:(t + 1) * D], probT[0:LC, t, :], v_s[0:LC, t, :],
                             start=True, stop=True)
                ins.then_inc(sem("attended"), 1)

            def x2_T(c, p):
                wait(pe, "x2", c + 1)
                for t in range(GT):
                    ins = nc.tensor.transpose(late[0][:, t * L:(t + 1) * L], x2[p][:, t, :], ident[:, :])
                ins.then_inc(sem("x2T_ps"), 1)

            def logits(c, p):
                wait(pe, "x2T", c + 1)
                for t in range(GT):
                    ins = mm(late[1][:, t * E:(t + 1) * E], x2T_s[:, t * L:(t + 1) * L], route_w[:, :],
                             start=True, stop=True)
                ins.then_inc(sem("logits"), 1)

            def ranks(c, p):
                wait(pe, "picked", c + 1)
                wait(pe, "carry", c)
                if not isinstance(c, int) or c + 1 < GROUPS:
                    wait(pe, "kT", c + 2)
                ps = late[1]
                flat = picked[:, :, :].rearrange("p t e -> p (t e)")
                mm(ps[:, 0:GT * E], before16[:, :], flat, start=True, stop=False)
                for t in range(GT - 1):
                    n = GT - 1 - t
                    mm(ps[:, (t + 1) * E:GT * E].rearrange("p (t e) -> p t e", e=E), ones16[:, :],
                       picked[:, t:t + 1, :].to_broadcast([P, n, E]), start=False, stop=False)
                mm(ps[:, 0:GT * E].rearrange("p (t e) -> p t e", e=E), ones16[:, :],
                   carry16[1 - p][:, :].unsqueeze(1).to_broadcast([P, GT, E]), start=False, stop=True
                   ).then_inc(sem("ranks"), 1)

            group_loop(pe, {"turn_x": turn_x, "cb": pair_products, "gate_T0": gate_T(0), "gate_T1": gate_T(1),
                            "mixed": mixed,
                            "k": k_proj, "v": v_proj, "x1_T": x1_T, "q": q_proj, "scores": scores,
                            "prob_T": prob_T, "attended": attended, "x2_T": x2_T, "logits": logits,
                            "ranks": ranks}
                       | {f"conv{c}": conv(c) for c in range(4)} | {f"z{h}": z_proj(h) for h in range(2)}
                       | {f"seg{t}": segments(t) for t in range(GT)} | {f"y{t}": outputs(t) for t in range(GT)})

            pe.wait_ge(sem("carry"), GROUPS)
            pe.wait_ge(sem("xdt"), 2 * GROUPS)
            mm(banks[0][:, 0:E], ones16[:, :], carry16[(GROUPS - 1) % 2][:, :], start=True, stop=True
               ).then_inc(sem("counts"), 1)

            pe.wait_ge(sem("plan"), N_PLAN)
            pe.wait_ge(sem("w_low"), 2 * E)
            pe.wait_ge(sem("b2_split"), 16)
            pe.wait_ge(sem("x2"), GROUPS)

            def turn(j, p, b):
                pe.wait_ge(sem(f"xg_loaded{b}"), 16 // ROWS_RING * (j - b) + 16)
                wait(pe, "xgT", j - 1)
                for hl in range(2):
                    for i in range(HALVES):
                        ins = nc.tensor.transpose(turn_ps[p][:, hl, i * P:(i + 1) * P],
                                                  xg[b][:, i, hl * D // 2:(hl + 1) * D // 2].bitcast(F16),
                                                  ident16[:, :])
                ins.then_inc(sem("rows_turned"), 1)

            def up(j, p, ex):
                wait(pe, "xgT", j + 1)
                for f in range(NF):
                    wait(pe, "hidden", NF * (j - 2) + 2 * (f // 2) + 2)
                    ps = banks[2 + 2 * p + f // 2][:, (f % 2) * STEP:(f % 2 + 1) * STEP]
                    wh = w1_hi[:, bass.ds(ex, 1), f, :].rearrange("p e m -> p (e m)")
                    wl = w1_lo[:, bass.ds(ex, 1), f, :].rearrange("p e m -> p (e m)")
                    ins = three(ps, wh, wl, xgT[p][:, 0, :], xgT[p][:, 1, :])
                    if f % 2:
                        ins.then_inc(sem("up"), 1)

            def down(j, b, ex):
                wait(pe, "y_scaled", HALVES * (j - 1))
                h = hid16[b % HID_RING]
                for i in range(HALVES):
                    ps = banks[6 + b % 2][:, 2 * i * D:2 * (i + 1) * D]

                    def high(f):
                        return mm(ps, h[:, f, 0, i * P:(i + 1) * P],
                                  w2_16[:, bass.ds(ex, 1), f, :, :].rearrange("p e a m -> p (e a m)"),
                                  start=(f == 0), stop=(f == NF - 1))

                    def low(f):
                        mm(ps[:, 0:D], h[:, f, 1, i * P:(i + 1) * P],
                           w2_16[:, bass.ds(ex, 1), f, 0, :].rearrange("p e m -> p (e m)"), start=False, stop=False)

                    pe.wait_ge(sem("hid_low"), 2 * j + 1)
                    high(0)
                    low(0)
                    mm(ps[:, 0:D], pair16[:, :], b2_16[:, bass.ds(ex, 1), :].rearrange("p e m -> p (e m)"),
                       start=False, stop=False)
                    for f in range(1, NF):
                        pe.wait_ge(sem("hid_low"), 2 * j + f // 2 + 1)
                        low(f)
                        ins = high(f)
                ins.then_inc(sem("down"), 1)

            BACK = 3

            def steps(first):
                peeled = isinstance(first, int)
                back = 0 if peeled else BACK
                ex = read_plan(step_e, first - back, ROWS_RING + back, PE, E - 1)
                for b in range(ROWS_RING):
                    turn(first + b, b % 2, b)
                    if not peeled or b >= 1:
                        up(first + b - 1, (b - 1) % 2, ex[back + b - 1])
                    if not peeled or b >= BACK:
                        down(first + b - BACK, (b - BACK) % ROWS_RING, ex[back + b - BACK])

            steps(0)
            with pe.Fori(1, STEPS // ROWS_RING) as i:
                steps(ROWS_RING * i)
            ex = read_plan(step_e, STEPS - BACK, BACK, PE, E - 1)
            up(STEPS - 1, (STEPS - 1) % 2, ex[-1])
            for j in range(STEPS - BACK, STEPS):
                down(j, j % ROWS_RING, ex[j - STEPS])


_INS = ["x", "xT", "ctxT", "in_wT", "conv_w", "conv_b", "norm_w", "out_wT", "dt_bias", "a_log", "d_param",
        "wq", "bq", "wk", "bk", "wv", "bv", "keysT", "w1T", "b1T", "w2T", "b2", "rwT", "rb"]


def kernel(x, ctx_1024, L0_attn_in_proj_w, L0_attn_conv_w, L0_attn_conv_b, L0_attn_norm_w, L0_attn_out_proj_w,
           L0_attn_dt_bias, L0_attn_A_log, L0_attn_D_param, L0_xattn_Wq, L0_xattn_bq, L0_xattn_Wk, L0_xattn_bk,
           L0_xattn_Wv, L0_xattn_bv, L0_ffn_keys, L0_ffn_w1, L0_ffn_b1, L0_ffn_w2, L0_ffn_b2, L0_ffn_rw,
           L0_ffn_rb):
    import concourse.bacc as _bacc
    from concourse.bass_utils import run_bass_kernel_spmd as _run

    a = [np.asarray(v) for v in (
        x, ctx_1024, L0_attn_in_proj_w, L0_attn_conv_w, L0_attn_conv_b, L0_attn_norm_w, L0_attn_out_proj_w,
        L0_attn_dt_bias, L0_attn_A_log, L0_attn_D_param, L0_xattn_Wq, L0_xattn_bq, L0_xattn_Wk, L0_xattn_bk,
        L0_xattn_Wv, L0_xattn_bv, L0_ffn_keys, L0_ffn_w1, L0_ffn_b1, L0_ffn_w2, L0_ffn_b2, L0_ffn_rw, L0_ffn_rb)]
    (xx, cc, inw, cw, cb, nw, ow, dtb, al, dp, wq, bq, wk, bk, wv, bv, keys, w1, b1, w2, b2, rw, rb) = a
    laid = dict(
        x=xx, xT=xx.reshape(TOKENS, D).T, ctxT=cc.transpose(2, 0, 1), in_wT=inw.T,
        conv_w=cw.reshape(CONV, TAPS).T.reshape(-1), conv_b=cb.reshape(4, P).T, norm_w=nw.reshape(2, P).T,
        out_wT=ow.T.reshape(2, P, D).transpose(1, 0, 2), dt_bias=dtb, a_log=al, d_param=dp,
        wq=wq, bq=bq.reshape(P, 1), wk=wk, bk=bk.reshape(P, 1), wv=wv, bv=bv, keysT=keys.T,
        w1T=w1.transpose(2, 0, 1), b1T=b1.reshape(E, NF, P).transpose(2, 0, 1),
        w2T=w2.reshape(E, D, NF, P).transpose(3, 0, 2, 1).reshape(P, E, NF * D), b2=b2.reshape(1, E * D),
        rwT=rw.T, rb=rb)
    nc = _bacc.Bacc("TRN2", target_bir_lowering=False, num_devices=1)
    arrays, args = {}, []
    for name in _INS:
        v = np.ascontiguousarray(laid[name])
        arrays[f"in_{name}_dram"] = v
        args.append(nc.dram_tensor(f"in_{name}_dram", v.shape, mybir.dt.from_np(v.dtype), kind="ExternalInput").ap())
    out = nc.dram_tensor("out_dram", (SEQS, L, D), F32, kind="ExternalOutput").ap()
    decoder_layer(nc, *args, out)
    r = _run(nc, [arrays], core_ids=[0])
    return r.results[0]["out_dram"]
```
